# Optimizing a Trainium2 kernel written in Bass

```python
import numpy as np
import jax
import jax.numpy as jnp

def _softmax(x, axis=-1):
    return jax.nn.softmax(x, axis=axis)

def _gelu(x):
    return jax.nn.gelu(x, approximate=True)

def _silu(x):
    return jax.nn.silu(x)

def _sigmoid(x):
    return jax.nn.sigmoid(x)

def _layernorm(x, axis=-1, eps=1e-05):
    m = jnp.mean(x, axis=axis, keepdims=True)
    v = jnp.var(x, axis=axis, keepdims=True)
    return (x - m) / jnp.sqrt(v + eps)

def _scatter_add(tgt, idx, src, axis=0):
    return tgt.at[idx].add(src)

def _segment_sum(src, seg, n):
    return jax.ops.segment_sum(src, seg, n)
kernel_name = 'mk_seq_preln_d2_jaxref_r4_1a75cc'

def setup_inputs(seed: int=0):
    np.random.seed(seed)
    _w = jnp.asarray

    def _L0_attn_setup():
        import jax, jax.numpy as jnp
        import numpy as np
        DIM = 1024
        N_HEADS = 32
        N_KV_HEADS = 8
        HEAD_DIM = DIM // N_HEADS
        N_REP = N_HEADS // N_KV_HEADS
        THETA = 10000.0
        B, S = (4, 256)

        def _rope_cos_sin(seq_len):
            freqs = 1.0 / THETA ** (jnp.arange(0, HEAD_DIM, 2, dtype=jnp.float32) / HEAD_DIM)
            t = jnp.arange(seq_len, dtype=jnp.float32)
            ang = jnp.outer(t, freqs)
            return (jnp.cos(ang), jnp.sin(ang))

        def _apply_rope(x, cos, sin):
            xr = x[..., 0::2]
            xi = x[..., 1::2]
            c = cos[None, :, None, :]
            s = sin[None, :, None, :]
            out_r = xr * c - xi * s
            out_i = xr * s + xi * c
            return jnp.stack([out_r, out_i], axis=-1).reshape(x.shape)
        key = jax.random.key(seed)
        ks = jax.random.split(key, 5)
        sc = 1.0 / np.sqrt(DIM).astype(np.float32)
        x = jax.random.normal(ks[0], (B, S, DIM), jnp.float32)
        wq = jax.random.normal(ks[1], (DIM, N_HEADS * HEAD_DIM), jnp.float32) * sc
        wk = jax.random.normal(ks[2], (DIM, N_KV_HEADS * HEAD_DIM), jnp.float32) * sc
        wv = jax.random.normal(ks[3], (DIM, N_KV_HEADS * HEAD_DIM), jnp.float32) * sc
        wo = jax.random.normal(ks[4], (N_HEADS * HEAD_DIM, DIM), jnp.float32) * sc
        return {'x': x, 'wq': wq, 'wk': wk, 'wv': wv, 'wo': wo}
    _L0_attn_in = _L0_attn_setup()

    def _L0_ffn_setup():
        import jax, jax.numpy as jnp
        import numpy as np
        N_STREAMS = 4
        DIM = 256
        SINKHORN_ITERS = 50
        SINKHORN_TAU = 0.1
        RMS_EPS = 1.1920929e-07

        def sinkhorn_log(logits, num_iters=SINKHORN_ITERS, tau=SINKHORN_TAU):
            Z = logits / tau
            u0 = jnp.zeros(Z.shape[:-1], Z.dtype)
            v0 = jnp.zeros_like(u0)

            def step(carry, _):
                u, v = carry
                u = -jax.nn.logsumexp(Z + v[..., None, :], axis=-1)
                v = -jax.nn.logsumexp(Z + u[..., :, None], axis=-2)
                return ((u, v), None)
            (u, v), _ = jax.lax.scan(step, (u0, v0), None, length=num_iters)
            return jnp.exp(Z + u[..., :, None] + v[..., None, :])
        key = jax.random.key(seed)
        ks = jax.random.split(key, 6)
        B, T = (4, 512)
        n, C = (N_STREAMS, DIM)
        wd = n * C
        x = jax.random.normal(ks[0], (B, T, wd), dtype=jnp.float32)
        W_res = 0.01 * jax.random.normal(ks[1], (n * n, wd), dtype=jnp.float32)
        W_pre = 0.01 * jax.random.normal(ks[2], (n, wd), dtype=jnp.float32)
        W_post = 0.01 * jax.random.normal(ks[3], (n, wd), dtype=jnp.float32)
        H_res_base = jnp.full((n, n), -0.5, dtype=jnp.float32)
        H_res_base = H_res_base.at[jnp.arange(n), jnp.arange(n)].set(0.0)
        H_pre_base = jnp.zeros((n,), dtype=jnp.float32).at[0].set(1.0)
        H_post_base = jnp.zeros((n,), dtype=jnp.float32)
        gate = jnp.array([5.0], dtype=jnp.float32)
        W_branch = 1.0 / np.sqrt(C) * jax.random.normal(ks[4], (C, C), dtype=jnp.float32)
        return {'x': x, 'W_res': W_res, 'W_pre': W_pre, 'W_post': W_post, 'H_res_base': H_res_base, 'H_pre_base': H_pre_base, 'H_post_base': H_post_base, 'gate': gate, 'W_branch': W_branch}
    _L0_ffn_in = _L0_ffn_setup()

    def _L1_attn_setup():
        import jax, jax.numpy as jnp
        import numpy as np
        HIDDEN = 1024
        NHQ = 32
        NHKV = 8
        HEAD_DIM = HIDDEN // NHQ
        THETA = 10000.0

        def _rope(x, theta_base):
            b, h, s, d = x.shape
            inv_freq = 1.0 / theta_base ** (jnp.arange(0, d, 2, dtype=jnp.float32)[:d // 2] / d)
            freqs = jnp.arange(s, dtype=jnp.float32)[:, None] * inv_freq[None, :]
            cos = jnp.cos(freqs).astype(x.dtype)
            sin = jnp.sin(freqs).astype(x.dtype)
            x1, x2 = (x[..., :d // 2], x[..., d // 2:])
            return jnp.concatenate([x1 * cos - x2 * sin, x2 * cos + x1 * sin], axis=-1)
        key = jax.random.key(seed)
        ks = jax.random.split(key, 5)
        std = 1.0 / np.sqrt(HIDDEN)
        x = jax.random.normal(ks[0], (2, 512, HIDDEN), dtype=jnp.float32)
        Wq = jax.random.normal(ks[1], (HIDDEN, HIDDEN), dtype=jnp.float32) * std
        Wk = jax.random.normal(ks[2], (HIDDEN, NHKV * HEAD_DIM), dtype=jnp.float32) * std
        Wv = jax.random.normal(ks[3], (HIDDEN, NHKV * HEAD_DIM), dtype=jnp.float32) * std
        Wo = jax.random.normal(ks[4], (HIDDEN, HIDDEN), dtype=jnp.float32) * std
        return {'x': x, 'Wq': Wq, 'Wk': Wk, 'Wv': Wv, 'Wo': Wo}
    _L1_attn_in = _L1_attn_setup()

    def _L1_ffn_setup():
        import jax, jax.numpy as jnp
        import numpy as np
        B, S, D, O, E, R = (4, 512, 1024, 1024, 8, 16)
        SCALING = 32.0 / 16.0
        MAX_THRESHOLD = 0.125
        key = jax.random.key(seed)
        ks = jax.random.split(key, 8)
        return {'x': jax.random.normal(ks[0], (B, S, D), jnp.float32), 'W_base': jax.random.normal(ks[1], (O, D), jnp.float32) * (1.0 / np.sqrt(D)), 'b_base': jax.random.normal(ks[2], (O,), jnp.float32) * 0.02, 'W_gate': jax.random.normal(ks[3], (E, D), jnp.float32) * (1.0 / np.sqrt(D)), 'W_thr': jax.random.normal(ks[4], (D,), jnp.float32) * (1.0 / np.sqrt(D)), 'b_thr': jax.random.normal(ks[5], (1,), jnp.float32) * 0.02, 'A_w': jax.random.normal(ks[6], (E, R, D), jnp.float32) * (1.0 / np.sqrt(D)), 'B_w': jax.random.normal(ks[7], (E, O, R), jnp.float32) * (1.0 / np.sqrt(R))}
    _L1_ffn_in = _L1_ffn_setup()
    _d = {'L0_attn_x': _L0_attn_in['x'], 'L0_attn_wq': _L0_attn_in['wq'], 'L0_attn_wk': _L0_attn_in['wk'], 'L0_attn_wv': _L0_attn_in['wv'], 'L0_attn_wo': _L0_attn_in['wo'], 'L0_ffn_W_res': _L0_ffn_in['W_res'], 'L0_ffn_W_pre': _L0_ffn_in['W_pre'], 'L0_ffn_W_post': _L0_ffn_in['W_post'], 'L0_ffn_H_res_base': _L0_ffn_in['H_res_base'], 'L0_ffn_H_pre_base': _L0_ffn_in['H_pre_base'], 'L0_ffn_H_post_base': _L0_ffn_in['H_post_base'], 'L0_ffn_gate': _L0_ffn_in['gate'], 'L0_ffn_W_branch': _L0_ffn_in['W_branch'], 'L1_attn_Wq': _L1_attn_in['Wq'], 'L1_attn_Wk': _L1_attn_in['Wk'], 'L1_attn_Wv': _L1_attn_in['Wv'], 'L1_attn_Wo': _L1_attn_in['Wo'], 'L1_ffn_W_base': _L1_ffn_in['W_base'], 'L1_ffn_b_base': _L1_ffn_in['b_base'], 'L1_ffn_W_gate': _L1_ffn_in['W_gate'], 'L1_ffn_W_thr': _L1_ffn_in['W_thr'], 'L1_ffn_b_thr': _L1_ffn_in['b_thr'], 'L1_ffn_A_w': _L1_ffn_in['A_w'], 'L1_ffn_B_w': _L1_ffn_in['B_w']}
    _x0 = _d['L0_attn_x']
    _d['L0_attn_x'] = jax.random.normal(jax.random.fold_in(jax.random.key(seed), 1), (2, 1024, 1024), dtype=_x0.dtype)
    del _x0
    return _d

def reference(L0_attn_x, L0_attn_wq, L0_attn_wk, L0_attn_wv, L0_attn_wo, L0_ffn_W_res, L0_ffn_W_pre, L0_ffn_W_post, L0_ffn_H_res_base, L0_ffn_H_pre_base, L0_ffn_H_post_base, L0_ffn_gate, L0_ffn_W_branch, L1_attn_Wq, L1_attn_Wk, L1_attn_Wv, L1_attn_Wo, L1_ffn_W_base, L1_ffn_b_base, L1_ffn_W_gate, L1_ffn_W_thr, L1_ffn_b_thr, L1_ffn_A_w, L1_ffn_B_w):

    def _L0_attn_ref(x, wq, wk, wv, wo):
        import jax, jax.numpy as jnp
        import numpy as np
        DIM = 1024
        N_HEADS = 32
        N_KV_HEADS = 8
        HEAD_DIM = DIM // N_HEADS
        N_REP = N_HEADS // N_KV_HEADS
        THETA = 10000.0
        B, S = (4, 256)

        def _rope_cos_sin(seq_len):
            freqs = 1.0 / THETA ** (jnp.arange(0, HEAD_DIM, 2, dtype=jnp.float32) / HEAD_DIM)
            t = jnp.arange(seq_len, dtype=jnp.float32)
            ang = jnp.outer(t, freqs)
            return (jnp.cos(ang), jnp.sin(ang))

        def _apply_rope(x, cos, sin):
            xr = x[..., 0::2]
            xi = x[..., 1::2]
            c = cos[None, :, None, :]
            s = sin[None, :, None, :]
            out_r = xr * c - xi * s
            out_i = xr * s + xi * c
            return jnp.stack([out_r, out_i], axis=-1).reshape(x.shape)
        bsz, seq_len, _ = x.shape
        q = (x @ wq).reshape(bsz, seq_len, N_HEADS, HEAD_DIM)
        k = (x @ wk).reshape(bsz, seq_len, N_KV_HEADS, HEAD_DIM)
        v = (x @ wv).reshape(bsz, seq_len, N_KV_HEADS, HEAD_DIM)
        cos, sin = _rope_cos_sin(seq_len)
        q = _apply_rope(q, cos, sin)
        k = _apply_rope(k, cos, sin)
        k = jnp.repeat(k, N_REP, axis=2)
        v = jnp.repeat(v, N_REP, axis=2)
        scores = jnp.einsum('bqhd,bkhd->bhqk', q, k) / np.float32(np.sqrt(HEAD_DIM))
        mask = jnp.triu(jnp.full((seq_len, seq_len), -jnp.inf, dtype=scores.dtype), k=1)
        scores = scores + mask
        attn = jax.nn.softmax(scores.astype(jnp.float32), axis=-1).astype(q.dtype)
        out = jnp.einsum('bhqk,bkhd->bqhd', attn, v).reshape(bsz, seq_len, N_HEADS * HEAD_DIM)
        return out @ wo

    def _L0_ffn_ref(x, W_res, W_pre, W_post, H_res_base, H_pre_base, H_post_base, gate, W_branch):
        import jax, jax.numpy as jnp
        import numpy as np
        N_STREAMS = 4
        DIM = 256
        SINKHORN_ITERS = 50
        SINKHORN_TAU = 0.1
        RMS_EPS = 1.1920929e-07

        def sinkhorn_log(logits, num_iters=SINKHORN_ITERS, tau=SINKHORN_TAU):
            Z = logits / tau
            u0 = jnp.zeros(Z.shape[:-1], Z.dtype)
            v0 = jnp.zeros_like(u0)

            def step(carry, _):
                u, v = carry
                u = -jax.nn.logsumexp(Z + v[..., None, :], axis=-1)
                v = -jax.nn.logsumexp(Z + u[..., :, None], axis=-2)
                return ((u, v), None)
            (u, v), _ = jax.lax.scan(step, (u0, v0), None, length=num_iters)
            return jnp.exp(Z + u[..., :, None] + v[..., None, :])
        B, T, nC = x.shape
        n = N_STREAMS
        C = nC // n
        x_norm = x * jax.lax.rsqrt(jnp.mean(x * x, axis=-1, keepdims=True) + RMS_EPS)
        H_res_logits = (x_norm @ W_res.T).reshape(B, T, n, n) + H_res_base
        H_pre_logits = x_norm @ W_pre.T + H_pre_base
        H_post_logits = x_norm @ W_post.T + H_post_base
        H_res = sinkhorn_log(H_res_logits)
        H_pre = jax.nn.softmax(H_pre_logits, axis=-1)
        H_post = jax.nn.softmax(H_post_logits, axis=-1)
        g = jax.nn.sigmoid(gate)[0]
        I = jnp.eye(n, dtype=H_res.dtype)
        H_res = (1.0 - g) * I + g * H_res
        x_streams = x.reshape(B, T, n, C)
        x_pre = jnp.einsum('btnc,btn->btc', x_streams, H_pre)
        y = x_pre @ W_branch
        x_mixed = jnp.einsum('btij,btjc->btic', H_res, x_streams)
        y_distributed = jnp.einsum('btc,btn->btnc', y, H_post)
        return (x_mixed + y_distributed).reshape(B, T, nC)

    def _L1_attn_ref(x, Wq, Wk, Wv, Wo):
        import jax, jax.numpy as jnp
        import numpy as np
        HIDDEN = 1024
        NHQ = 32
        NHKV = 8
        HEAD_DIM = HIDDEN // NHQ
        THETA = 10000.0

        def _rope(x, theta_base):
            b, h, s, d = x.shape
            inv_freq = 1.0 / theta_base ** (jnp.arange(0, d, 2, dtype=jnp.float32)[:d // 2] / d)
            freqs = jnp.arange(s, dtype=jnp.float32)[:, None] * inv_freq[None, :]
            cos = jnp.cos(freqs).astype(x.dtype)
            sin = jnp.sin(freqs).astype(x.dtype)
            x1, x2 = (x[..., :d // 2], x[..., d // 2:])
            return jnp.concatenate([x1 * cos - x2 * sin, x2 * cos + x1 * sin], axis=-1)
        b, s, _ = x.shape
        q_per_kv = NHQ // NHKV
        q = (x @ Wq).reshape(b, s, NHQ, HEAD_DIM).transpose(0, 2, 1, 3)
        k = (x @ Wk).reshape(b, s, NHKV, HEAD_DIM).transpose(0, 2, 1, 3)
        v = (x @ Wv).reshape(b, s, NHKV, HEAD_DIM).transpose(0, 2, 1, 3)
        q = _rope(q, THETA)
        k = _rope(k, THETA)
        qg = q.reshape(b, NHKV, q_per_kv, s, HEAD_DIM)
        scores = jnp.einsum('bkgqd,bkmd->bkgqm', qg, k) / np.sqrt(HEAD_DIM)
        causal = jnp.tril(jnp.ones((s, s), dtype=bool))
        scores = jnp.where(causal, scores, -jnp.inf)
        attn = jax.nn.softmax(scores, axis=-1)
        out = jnp.einsum('bkgqm,bkmd->bkgqd', attn, v)
        out = out.reshape(b, NHQ, s, HEAD_DIM).transpose(0, 2, 1, 3).reshape(b, s, HIDDEN)
        return out @ Wo

    def _L1_ffn_ref(x, W_base, b_base, W_gate, W_thr, b_thr, A_w, B_w):
        import jax, jax.numpy as jnp
        import numpy as np
        B, S, D, O, E, R = (4, 512, 1024, 1024, 8, 16)
        SCALING = 32.0 / 16.0
        MAX_THRESHOLD = 0.125
        base = jnp.einsum('bsd,od->bso', x, W_base) + b_base
        xf = x.reshape(-1, D)
        gate = jax.nn.softmax(xf @ W_gate.T, axis=-1)
        thr = jax.nn.sigmoid(xf @ W_thr + b_thr[0]) * MAX_THRESHOLD
        adapted = gate - thr[:, None]
        selected = (adapted >= 0).astype(x.dtype)
        w = adapted * selected
        wsum = jnp.sum(w, axis=-1, keepdims=True)
        wsum = jnp.where(wsum == 0, jnp.ones_like(wsum), wsum)
        w = w / wsum
        h = jnp.einsum('nd,erd->ner', xf, A_w)
        moe = jnp.einsum('ner,ne,eor->no', h, w, B_w) * SCALING
        return base + moe.reshape(base.shape)
    x = L0_attn_x
    x = x + _L0_attn_ref(_layernorm(x, axis=-1), L0_attn_wq, L0_attn_wk, L0_attn_wv, L0_attn_wo)
    x = x + _L0_ffn_ref(_layernorm(x, axis=-1), L0_ffn_W_res, L0_ffn_W_pre, L0_ffn_W_post, L0_ffn_H_res_base, L0_ffn_H_pre_base, L0_ffn_H_post_base, L0_ffn_gate, L0_ffn_W_branch)
    x = x + _L1_attn_ref(_layernorm(x, axis=-1), L1_attn_Wq, L1_attn_Wk, L1_attn_Wv, L1_attn_Wo)
    x = x + _L1_ffn_ref(_layernorm(x, axis=-1), L1_ffn_W_base, L1_ffn_b_base, L1_ffn_W_gate, L1_ffn_W_thr, L1_ffn_b_thr, L1_ffn_A_w, L1_ffn_B_w)
    return x

_drawn_inputs = setup_inputs


def setup_inputs(seed=0):
    import zlib

    import numpy as np

    out = dict(_drawn_inputs(seed))
    spreads = {'L0_ffn_H_post_base': (0.0, 0.8)}
    factors = {'L0_ffn_W_pre': 2.796, 'L1_ffn_b_base': 7.017}
    for name, (base, spread) in spreads.items():
        noise = np.random.default_rng([zlib.crc32(name.encode()), seed]).standard_normal(out[name].shape)
        drawn = base * np.exp(spread * noise) if base else spread * noise
        out[name] = jnp.asarray(drawn.astype(out[name].dtype))
    for name, factor in factors.items():
        out[name] = (out[name] * factor).astype(out[name].dtype)
    return out
```

```python
from contextlib import ExitStack, contextmanager

import numpy as np

import concourse.bass as bass
from concourse import mybir

F32 = mybir.dt.float32
F32R = mybir.dt.float32r
BF16 = mybir.dt.bfloat16
ALU = mybir.AluOpType
ACT = mybir.ActivationFunctionType
AX = mybir.AxisListType

P = 128
B, S, D = 2, 1024, 1024
T = B * S
NT = T // P
ST_ = S // P
KC = D // P
HD = 32
NG = 8
GH = 4
BANK = 512
NQC = S // BANK
LN_EPS = 1e-5
RMS_EPS = 1.1920929e-07
THETA = 10000.0
MASKED = -1e30
N_WCHUNK = 12
ds = bass.ds


UNITS = [(qc, ki) for qc in range(NQC) for ki in range(4 * qc + 4)]
NU = len(UNITS)
DIAGONAL = [e for e, (qc, ki) in enumerate(UNITS) if ki >= 4 * qc]
CHUNK_END = [e for e, (qc, ki) in enumerate(UNITS) if ki == 4 * qc + 3]


def unit_offset(e):
    qc, ki = UNITS[e]
    return max(0, ki * P - qc * BANK)


def score_uses():
    out = []
    for qt in range(ST_):
        for kc in range(qt // 4 + 1):
            n = min(BANK, (qt + 1) * P - kc * BANK)
            m = BANK // n if BANK % n == 0 else 1
            for h in range(0, GH, m):
                out.append((qt, kc, n, tuple(range(h, h + m)), kc == qt // 4))
    return out


USES = score_uses()


def iteration(full_s=True, proj=True):
    fill = {e: [] for e in range(NU)}
    if proj:
        fill[0] += [("P", 0)]
        fill[1] += [("WL", 0)]
        fill[5] += [("P", 1)]
        fill[3] += [("HI", 0)]
        fill[4] += [("LO", 0)]
        fill[7] += [("WS", 0), ("HI", 1)]
        fill[8] += [("LO", 1)]
    if full_s:
        n = 0
        for e, m in zip([1, 2, 3, 4, 6, 7, 8, 9], [5, 5, 5, 5, 5, 5, 4, 4]):
            fill[e] += [("S", k) for k in range(n, n + m)]
            n += m
        assert n == len(USES)
        fill[9] += [("MT", 0)]
    order = [("ST", 0)]
    for e in range(NU):
        order += fill[e]
        if e == CHUNK_END[0] + 2:
            order += [("NORM", 0)]
        if e + 1 < NU:
            order += [("ST", e + 1)]
        order += [("PV", e)]
    return order + [("RS", 0), ("NORM", 1)]


def shared_uses(order):
    return sum(k in ("P", "S", "MT") for k, _ in order)


def attention(nc, sem, layer, x_in, wqkv, cos_in, sin_in, swap, oT_d):
    kT_d = nc.dram_tensor(f"kT_{layer}", (2, B, NG * HD, S), F32, kind="Internal").ap()
    m_d = nc.dram_tensor(f"rowmax_{layer}", (2, GH * ST_, P), F32, kind="Internal").ap()
    scale = 1.0 / float(np.sqrt(np.float32(HD)))

    s = {n: sem(f"a{layer}_{n}") for n in (
        "const", "table", "xl0", "xl1", "stats", "pow", "z_ready", "zT_ready", "zT_hi", "zT_evac",
        "wl0", "wl1", "w_hi", "w_ready", "sh_ready", "sh_free", "roped", "q_hi", "q_lo", "v_ready",
        "k_out", "rs0", "rs1", "mx_ready", "mT_ready", "m_out", "mr0", "mr1", "st_ready",
        "exp_done", "mask_done", "pv_done", "acc_copied", "norm_done", "vg_ready", "os0", "os1",
        "pool_turn", "sp_turn")}
    x_loaded, w_loaded = (s["xl0"], s["xl1"]), (s["wl0"], s["wl1"])
    restacked, max_row, o_stored = (s["rs0"], s["rs1"]), (s["mr0"], s["mr1"]), (s["os0"], s["os1"])
    ZT0, W0, SH0, R0, E0, PV0, AC0, N0, ST0, DMA0 = 4, 2, 2, 4, 2, 2, 2, 1, 2, 16

    PRO = [("P", p, c) for p in range(6) for c in range(2)]
    U_PRO = 12 + 4 + len(USES) + 1
    body, body6, body7 = iteration(), iteration(proj=False), iteration(False, False)
    U_IT, U_IT6 = shared_uses(body), shared_uses(body6)
    U_BATCH = U_PRO + 6 * U_IT + U_IT6
    RB = 20

    with ExitStack() as ctx:
        def sb(name, shape, dt=F32):
            return ctx.enter_context(nc.sbuf_tensor(f"a{layer}_{name}", shape, dt))

        ident = sb("ident", [P, P])
        identb = sb("identb", [P, P], BF16)
        negmask = sb("negmask", [P, P], BF16)
        ones = sb("ones", [P, HD])
        nhalf = sb("nhalf", [P, 1])
        cos = sb("cos", [P, S])
        sin = sb("sin", [P, S])
        xin = [sb(f"xin{i}", [P, D]) for i in range(2)]
        stat = [sb(f"stat{i}", [P, 2, 6]) for i in range(2)]
        mv = [sb(f"mv{i}", [P, 4]) for i in range(2)]
        xT = [sb(f"xT_{n}", [P, KC, S], F32R) for n in ("hi", "lo")]
        wraw = [sb(f"wraw{i}", [P, KC, P]) for i in range(2)]
        w = [[sb(f"w_{n}{i}", [P, KC, P], F32R) for n in ("hi", "lo")] for i in range(2)]
        rot = [sb(f"rot{i}", [P, BANK]) for i in range(2)]
        swp = [sb(f"swp{i}", [P, BANK]) for i in range(2)]
        stg = [sb(f"stg_{n}", [P, S], F32R) for n in ("hi", "lo")]
        qst = [sb(f"qst{i}", [P, GH, S], F32R) for i in range(2)]
        kst = [sb(f"kst{i}", [P, S], F32R) for i in range(2)]
        vT = sb("vT", [P, S])
        vall = sb("vall", [P, ST_, NG * HD])
        vg = [sb(f"vg{i}", [P, ST_, HD]) for i in range(2)]
        prob = [sb(f"prob{i}", [P, GH, BANK]) for i in range(2)]
        mx = sb("mx", [P, 2, GH * ST_])
        mT = sb("mT", [GH * ST_, P])
        pvs = sb("pvs", [P, BANK])
        dens = sb("dens", [P, BANK])
        oT = [sb(f"oT{i}", [P, BANK]) for i in range(2)]
        pst = ctx.enter_context(nc.psum_tensor(f"a{layer}_pst", [P, 2, 2, BANK], F32))
        psh = ctx.enter_context(nc.psum_tensor(f"a{layer}_psh", [P, 2, BANK], F32))
        ppv = ctx.enter_context(nc.psum_tensor(f"a{layer}_ppv", [P, BANK], F32))
        pden = ctx.enter_context(nc.psum_tensor(f"a{layer}_pden", [P, BANK], F32))
        mx_hq = [mx[:, i, :].rearrange("p (h q) -> p h q", q=ST_) for i in range(2)]
        block = ctx.enter_context(nc.Block())

        def over_groups(eng, b, group):
            u0 = b * U_BATCH + U_PRO
            with eng.Fori(0, NG // 2 - 1) as j:
                for par in range(2):
                    group(body, b, j * 2 + par, j, par, u0 + (j * 2 + par) * U_IT, U_PRO + par * U_IT)
            group(body6, b, NG - 2, NG // 2 - 1, 0, u0 + 6 * U_IT, U_PRO)
            group(body7, b, NG - 1, NG // 2 - 1, 1, u0 + 6 * U_IT + U_IT6, U_PRO + U_IT6)

        @block.sync
        def _(sp):
            def load_w(n, chunk, par):
                sp.wait_ge(s["w_ready"], n + 1)
                sp.dma_start(wraw[par][:, :, :], wqkv[chunk]).then_inc(w_loaded[par], 16)

            def store_k(b, p):
                sp.wait_ge(s["q_lo"], b * RB + 2 * p + 2)
                for part in range(2):
                    sp.dma_start(kT_d[part, ds(b, 1), p * P:(p + 1) * P, :].rearrange("o p n -> p (o n)"),
                                 stg[part][:, :].bitcast(F32)).then_inc(s["k_out"], 16)

            def restack(b, g, par):
                for h in range(GH):
                    for row, part in enumerate((0, 1, 0)):
                        sp.dma_start(qst[par][row * HD:(row + 1) * HD, h, :].bitcast(F32),
                                     stg[part][h * HD:(h + 1) * HD, :].bitcast(F32)).then_inc(restacked[par], 16)
                for row, part in enumerate((0, 0, 1)):
                    src = kT_d[part, ds(b, 1), ds(g * HD, HD), :].rearrange("o p n -> p (o n)")
                    sp.dma_start(kst[par][row * HD:(row + 1) * HD, :].bitcast(F32), src).then_inc(restacked[par], 16)

            def row_max(b, g, par):
                n = b * NG + g
                sp.wait_ge(s["mT_ready"], n + 1)
                sp.dma_start(m_d[par], mT[:, :]).then_inc(s["m_out"], 16)
                sp.wait_ge(s["m_out"], DMA0 + n * 16 + 16)
                sp.dma_start(qst[par][96:97, :, :].rearrange("o h n -> o (h n)").bitcast(F32),
                             m_d[par].rearrange("a (o n) -> o (a n)", o=1)).then_inc(max_row[par], 16)

            def store_o(b, g, qc):
                sp.wait_ge(s["norm_done"], N0 + (b * NG + g) * 2 + qc + 1)
                sp.dma_start(oT_d[ds(g, 1), :, ds(b * ST_ + qc * 4, 4), :].rearrange("o p t n -> p (o t) n"),
                             oT[qc][:, :].rearrange("p (t n) -> p t n", n=P)).then_inc(o_stored[qc], 16)

            def group(order, b, g, gh, par, u, ub):
                n = b * NG + g
                for what, k in order:
                    if what == "WL":
                        load_w(b * N_WCHUNK + g + 8, g + 8, par)
                    if what == "MT":
                        row_max(b, g + 1, 1 - par)
                    if what == "NORM":
                        store_o(b, g, k)
                    if what == "RS" and order is body:
                        sp.wait_ge(s["st_ready"], ST0 + n * 2 * NU + 2 * NU)
                        sp.wait_ge(s["q_lo"], b * RB + 4 + (g + 2) * 2 + 2)
                        restack(b, g + 2, par)

            for credited in (s["m_out"], *o_stored):
                sp.sem_inc(credited, DMA0)
            sp.dma_start(cos[:, :], cos_in).then_inc(s["table"], 16)
            sp.dma_start(sin[:, :], sin_in).then_inc(s["table"], 16)
            load_w(0, 0, 0)
            load_w(1, 1, 1)
            with sp.Fori(0, B) as b:
                for t in range(ST_):
                    sp.wait_ge(s["zT_ready"], (b * ST_ + t) * 2 + 2)
                    sp.dma_start(xin[t % 2][:, :], x_in[ds((b * ST_ + t) * P, P), :]).then_inc(x_loaded[t % 2], 16)
                for p in range(2, 8):
                    load_w(b * N_WCHUNK + p, p, p % 2)
                    if p in (2, 3):
                        store_k(b, p - 2)
                    if p in (6, 7):
                        g = p - 6
                        sp.wait_ge(s["k_out"], b * 64 + 64)
                        sp.sem_inc(s["sp_turn"], 1)
                        sp.wait_ge(s["st_ready"], ST0 + b * NG * 2 * NU)
                        sp.sem_inc(s["sp_turn"], 1)
                        sp.wait_ge(s["q_lo"], b * RB + 4 + 2 * g + 2)
                        sp.sem_inc(s["sp_turn"], 1)
                        restack(b, g, g)
                row_max(b, 0, 0)
                over_groups(sp, b, group)
            for qc in range(NQC):
                sp.wait_ge(o_stored[qc], DMA0 + 16 * B * NG)

        @block.gpsimd
        def _(pool):
            def copy_v(b, g, par):
                pool.sem_inc(s["pool_turn"], 1)
                pool.tensor_copy(vg[par][:, :, :], vall[:, :, ds(g * HD, HD)]).then_inc(s["vg_ready"], 1)

            def group(order, b, g, gh, par, u, ub):
                n = b * NG + g
                for what, e in order:
                    if what == "ST" and e in DIAGONAL:
                        off = unit_offset(e)
                        pool.wait_ge(s["exp_done"], E0 + (n * NU + e) * 2 + 2)
                        pool.sem_inc(s["pool_turn"], 1)
                        blk = prob[e % 2][:, :, off:off + P]
                        pool.affine_select(out=blk, in_=blk, compare_op=ALU.is_ge, fill=0.0, base=0,
                                           pattern=[[0, GH], [1, P]], channel_multiplier=-1)\
                            .then_inc(s["mask_done"], 1)
                if order is body:
                    pool.wait_ge(s["pv_done"], PV0 + n * NU + NU)
                    copy_v(b, g + 2, par)

            pool.memset(ident[:, :], 0.0)
            pool.memset(negmask[:, :], 0.0)
            pool.memset(ones[:, :], 1.0)
            pool.memset(nhalf[:, :], -0.5)
            pool.drain()
            for i in range(2):
                pool.memset(kst[i][96:97, :].bitcast(F32), -1.0)
            pool.drain()
            pool.affine_select(out=ident[:, :], in_=ident[:, :], compare_op=ALU.not_equal, fill=1.0, base=0,
                               pattern=[[-1, P]], channel_multiplier=1)
            pool.affine_select(out=negmask[:, :], in_=negmask[:, :], compare_op=ALU.is_ge, fill=MASKED, base=0,
                               pattern=[[-1, P]], channel_multiplier=1)
            pool.drain()
            pool.tensor_copy(identb[:, :], ident[:, :])
            pool.drain().then_inc(s["const"], 1)
            with pool.Fori(0, B) as b:
                for t in range(ST_):
                    pool.wait_ge(s["stats"], b * ST_ + t + 1)
                    pool.tensor_tensor(mv[t % 2][:, 3:4], mv[t % 2][:, 2:3], nhalf[:, :], ALU.pow)\
                        .then_inc(s["pow"], 1)
                pool.wait_ge(s["v_ready"], b * 4 + 4)
                copy_v(b, 0, 0)
                copy_v(b, 1, 1)
                over_groups(pool, b, group)

        @block.scalar
        def _(act):
            def w_hi(n, half_n, par):
                act.wait_ge(w_loaded[par], half_n * 16 + 16)
                act.wait_ge(s["roped"], 2 * n + 2)
                act.activation(w[par][0][:, :, :], wraw[par][:, :, :], ACT.Copy).then_inc(s["w_hi"], 1)

            def part_hi(n, c):
                act.wait_ge(s["roped"], R0 + 2 * n + c + 1)
                act.activation(stg[0][:, c * BANK:(c + 1) * BANK], rot[c][:, :], ACT.Copy).then_inc(s["q_hi"], 1)

            def group(order, b, g, gh, par, u, ub):
                n = b * NG + g
                for what, k in order:
                    if what == "ST":
                        off = unit_offset(k)
                        act.wait_ge(s["pv_done"], n * NU + k + 1)
                        for half in range(2):
                            act.wait_ge(s["st_ready"], ST0 + (n * NU + k) * 2 + half + 1)
                            act.activation(prob[k % 2][:, 2 * half:2 * half + 2, off:], pst[:, half, :, off:],
                                           ACT.Exp, scale=scale).then_inc(s["exp_done"], 1)
                    if what == "PV" and k in CHUNK_END:
                        q = n * 2 + CHUNK_END.index(k)
                        act.wait_ge(s["pv_done"], PV0 + n * NU + k + 1)
                        act.wait_ge(s["norm_done"], q + 1)
                        act.copy(pvs[:, :], ppv[:, :]).then_inc(s["acc_copied"], 1)
                        act.copy(dens[:, :], pden[:, :]).then_inc(s["acc_copied"], 1)
                    if what == "WS":
                        w_hi(b * N_WCHUNK + g + 8, b * 6 + gh + 4, par)
                    if what == "HI":
                        if k == 0:
                            act.wait_ge(restacked[1 - par], (b * 4 + gh + par + 1) * 240)
                        part_hi(b * N_WCHUNK + g + 6, k)

            act.drain().then_inc(s["exp_done"], E0)
            act.drain().then_inc(s["acc_copied"], AC0)
            w_hi(0, 0, 0)
            w_hi(1, 0, 1)
            with act.Fori(0, B) as b:
                for t in range(ST_):
                    for half in range(2):
                        n = 2 * t + half
                        act.wait_ge(s["zT_ready"], ZT0 + b * 2 * ST_ + n + 1)
                        act.activation(xT[0][:, 4 * half:4 * half + 4, t * P:(t + 1) * P],
                                       pst[:, n // 2 % 2, n % 2, :].rearrange("p (k n) -> p k n", n=P),
                                       ACT.Copy).then_inc(s["zT_hi"], 1)
                for p in range(6):
                    if p == 1:
                        act.wait_ge(s["k_out"], b * 64 + 32)
                    if p == 4:
                        act.wait_ge(s["k_out"], b * 64 + 64)
                    if p == 5:
                        act.wait_ge(restacked[0], (b * 4 + 1) * 240)
                    if p not in (2, 3):
                        for c in range(2):
                            part_hi(b * N_WCHUNK + p, c)
                    w_hi(b * N_WCHUNK + p + 2, b * 6 + p // 2 + 1, p % 2)
                over_groups(act, b, group)

        @block.vector
        def _(dve):
            def w_lo(n, par):
                dve.wait_ge(s["w_hi"], n + 1)
                dve.tensor_tensor(w[par][1][:, :, :], wraw[par][:, :, :], w[par][0][:, :, :].bitcast(F32),
                                  ALU.subtract).then_inc(s["w_ready"], 1)

            def rotate(u, bank, c):
                dve.drain()
                dve.wait_ge(s["sh_ready"], u + 1)
                dve.tensor_tensor(rot[c][:, :], psh[:, bank, :], cos[:, c * BANK:(c + 1) * BANK], ALU.mult)
                dve.stream_shuffle(swp[c][:, :], psh[:, bank, :], swap).then_inc(s["sh_free"], 1)
                dve.drain()
                dve.tensor_tensor(swp[c][:, :], swp[c][:, :], sin[:, c * BANK:(c + 1) * BANK], ALU.mult)
                dve.drain()
                dve.tensor_tensor(rot[c][:, :], rot[c][:, :], swp[c][:, :], ALU.add).then_inc(s["roped"], 1)

            def part_lo(r, c):
                cols = slice(c * BANK, (c + 1) * BANK)
                dve.wait_ge(s["q_hi"], r + 1)
                dve.tensor_tensor(stg[1][:, cols], rot[c][:, :], stg[0][:, cols].bitcast(F32), ALU.subtract)\
                    .then_inc(s["q_lo"], 1)

            def maximum(u, bank, k):
                qt, kc, n, heads, _ = USES[k]
                m = len(heads)
                dve.wait_ge(s["sh_ready"], u + 1)
                dve.tensor_reduce(mx_hq[kc][:, heads[0]:heads[0] + m, qt],
                                  psh[:, bank, 0:m * n].rearrange("p (m n) -> p m n", n=n), AX.X, ALU.max)\
                    .then_inc(s["sh_free"], 1)

            def max_rows(u, bank):
                dve.tensor_tensor(mx_hq[0][:, :, 4:], mx_hq[0][:, :, 4:], mx_hq[1][:, :, 4:], ALU.max)\
                    .then_inc(s["mx_ready"], 1)
                dve.wait_ge(s["sh_ready"], u + 1)
                dve.tensor_copy(mT[:, :], psh[0:GH * ST_, bank, 0:P]).then_inc(s["sh_free"], 1)
                dve.drain().then_inc(s["mT_ready"], 1)

            def group(order, b, g, gh, par, u, ub):
                n = b * NG + g
                i = 0
                for what, k in order:
                    if what == "P":
                        rotate(u + i, (ub + i) % 2, k)
                    if what == "S":
                        maximum(u + i, (ub + i) % 2, k)
                    if what == "MT":
                        dve.drain()
                        dve.wait_ge(s["m_out"], DMA0 + (n + 1) * 16)
                        max_rows(u + i, (ub + i) % 2)
                    i += what in ("P", "S", "MT")
                    if what == "LO":
                        part_lo(b * RB + 4 + (g + 2) * 2 + k, k)
                    if what == "WS":
                        w_lo(b * N_WCHUNK + g + 8, par)
                    if what == "NORM":
                        q = n * 2 + k
                        dve.drain()
                        dve.wait_ge(s["acc_copied"], AC0 + 2 * q + 2)
                        dve.reciprocal(dens[:, :], dens[:, :])
                        dve.drain()
                        dve.wait_ge(o_stored[k], DMA0 + n * 16)
                        dve.tensor_tensor(oT[k][:, :], pvs[:, :], dens[:, :], ALU.mult).then_inc(s["norm_done"], 1)

            dve.drain().then_inc(s["zT_evac"], ZT0)
            dve.drain().then_inc(s["w_ready"], W0)
            dve.drain().then_inc(s["sh_free"], SH0)
            dve.drain().then_inc(s["roped"], R0)
            dve.drain().then_inc(s["norm_done"], N0)
            w_lo(0, 0)
            w_lo(1, 1)
            dve.wait_ge(s["table"], 32)
            with dve.Fori(0, B) as b:
                for t in range(ST_ + 2):
                    if t < ST_:
                        dve.wait_ge(x_loaded[t % 2], (b * (ST_ // 2) + t // 2) * 16 + 16)
                        for i in range(2):
                            dve.bn_stats(stat[t % 2][:, i, :], xin[t % 2][:, i * BANK:(i + 1) * BANK])
                        dve.drain()
                        dve.bn_aggr(mv[t % 2][:, 0:2], stat[t % 2][:, :, :])
                        dve.drain()
                        dve.tensor_scalar(mv[t % 2][:, 2:3], mv[t % 2][:, 1:2], LN_EPS, None, ALU.add)\
                            .then_inc(s["stats"], 1)
                    if 1 <= t <= ST_:
                        i = (t - 1) % 2
                        dve.wait_ge(s["pow"], b * ST_ + t)
                        dve.tensor_scalar(xin[i][:, :], xin[i][:, :], mv[i][:, 0:1], mv[i][:, 3:4],
                                          ALU.subtract, ALU.mult).then_inc(s["z_ready"], 1)
                    if t >= 2:
                        for half in range(2):
                            n = 2 * (t - 2) + half
                            dve.wait_ge(s["zT_hi"], b * 2 * ST_ + n + 1)
                            at = (slice(None), slice(4 * half, 4 * half + 4), slice((t - 2) * P, (t - 1) * P))
                            dve.tensor_tensor(xT[1][at], pst[:, n // 2 % 2, n % 2, :].rearrange("p (k n) -> p k n", n=P),
                                              xT[0][at].bitcast(F32), ALU.subtract).then_inc(s["zT_evac"], 1)
                i = 0
                for p in range(6):
                    for c in range(2):
                        u, bank = b * U_BATCH + i, i % 2
                        if p in (2, 3):
                            dve.wait_ge(s["sh_ready"], u + 1)
                            dve.tensor_copy(vT[:, c * BANK:(c + 1) * BANK], psh[:, bank, :]).then_inc(s["sh_free"], 1)
                            dve.drain().then_inc(s["roped"], 1)
                        else:
                            rotate(u, bank, c)
                        i += 1
                    if p in (2, 3):
                        for c in range(2):
                            u, bank = b * U_BATCH + i, i % 2
                            dve.wait_ge(s["sh_ready"], u + 1)
                            dve.tensor_copy(vall[:, 4 * c:4 * c + 4, (p - 2) * P:(p - 1) * P],
                                            psh[:, bank, :].rearrange("p (k n) -> p k n", n=P))\
                                .then_inc(s["sh_free"], 1)
                            dve.drain().then_inc(s["v_ready"], 1)
                            i += 1
                    else:
                        for c in range(2):
                            part_lo(b * RB + (2 * p + c if p < 2 else 4 + 2 * (p - 4) + c), c)
                    w_lo(b * N_WCHUNK + p + 2, p % 2)
                for k in range(len(USES)):
                    maximum(b * U_BATCH + i, i % 2, k)
                    i += 1
                dve.drain()
                dve.wait_ge(s["m_out"], DMA0 + b * NG * 16)
                max_rows(b * U_BATCH + i, i % 2)
                assert i + 1 == U_PRO
                over_groups(dve, b, group)

        @block.tensor
        def _(pe):
            def project(n, u, bank, par, c):
                pe.wait_ge(s["w_ready"], W0 + n + 1)
                pe.wait_ge(s["sh_free"], u + 1)
                passes = [(k, a, x) for k in range(KC) for a, x in ((0, 0), (0, 1), (1, 0))]
                for i, (k, a, x) in enumerate(passes):
                    mm = pe.matmul(psh[:, bank, :], w[par][a][:, k, :], xT[x][:, k, c * BANK:(c + 1) * BANK],
                                   start=(i == 0), stop=(i == len(passes) - 1))
                mm.then_inc(s["sh_ready"], 1)

            def row_scores(u, bank, par, k):
                qt, kc, n, heads, last = USES[k]
                pe.wait_ge(s["sh_free"], u + 1)
                for i, h in enumerate(heads):
                    mm = pe.matmul(psh[:, bank, i * n:(i + 1) * n], qst[par][0:96, h, qt * P:(qt + 1) * P],
                                   kst[par][0:96, kc * BANK:kc * BANK + n], start=True, stop=not last,
                                   skip_group_check=True)
                    if last:
                        mm = pe.matmul(psh[:, bank, (i + 1) * n - P:(i + 1) * n], identb[:, :], negmask[:, :],
                                       start=False, stop=True, skip_group_check=True)
                mm.then_inc(s["sh_ready"], 1)

            def transpose_max(n, u, bank):
                pe.wait_ge(s["mx_ready"], n + 1)
                pe.wait_ge(s["sh_free"], u + 1)
                pe.transpose(psh[0:GH * ST_, bank, 0:P], mx[:, 0, :], ident[:, :]).then_inc(s["sh_ready"], 1)

            def group(order, b, g, gh, par, u, ub):
                n = b * NG + g
                i = 0
                for what, k in order:
                    if what == "P":
                        project(b * N_WCHUNK + g + 6, u + i, (ub + i) % 2, par, k)
                    if what == "S":
                        if k == 0:
                            pe.wait_ge(restacked[1 - par], (b * 4 + gh + par + 1) * 240)
                        row_scores(u + i, (ub + i) % 2, 1 - par, k)
                    if what == "MT":
                        transpose_max(n + 1, u + i, (ub + i) % 2)
                    i += what in ("P", "S", "MT")
                    if what == "ST":
                        qc, ki = UNITS[k]
                        off = min(unit_offset(k), BANK // 2)
                        if k == 0:
                            pe.wait_ge(max_row[par], (b * 4 + gh + 1) * 16)
                        for half in range(2):
                            pe.wait_ge(s["exp_done"], (n * NU + k) * 2 + half + 1)
                            for hh in range(2):
                                mm = pe.matmul(pst[:, half, hh, off:], kst[par][0:97, ki * P:(ki + 1) * P],
                                               qst[par][0:97, 2 * half + hh, qc * BANK + off:(qc + 1) * BANK],
                                               start=True, stop=True)
                            mm.then_inc(s["st_ready"], 1)
                    if what == "PV":
                        qc, ki = UNITS[k]
                        off = unit_offset(k)
                        if k == 0:
                            pe.wait_ge(s["vg_ready"], n + 1)
                        if k in DIAGONAL:
                            pe.wait_ge(s["mask_done"], n * len(DIAGONAL) + DIAGONAL.index(k) + 1)
                        else:
                            pe.wait_ge(s["exp_done"], E0 + (n * NU + k) * 2 + 2)
                        if ki == 0:
                            pe.wait_ge(s["acc_copied"], (n * 2 + qc) * 2 + 2)
                        for acc, lhs in ((ppv, vg[par][:, ki, :]), (pden, ones[:, :])):
                            for h in range(GH):
                                mm = pe.matmul(acc[h * HD:(h + 1) * HD, off:], lhs, prob[k % 2][:, h, off:],
                                               start=(ki == 0), stop=(ki == 4 * qc + 3), skip_group_check=True)
                        mm.then_inc(s["pv_done"], 1)

            pe.wait_ge(s["const"], 1)
            pe.sem_inc(s["zT_ready"], ZT0)
            pe.sem_inc(s["pv_done"], PV0)
            pe.sem_inc(s["st_ready"], ST0)
            with pe.Fori(0, B) as b:
                pe.wait_ge(s["exp_done"], E0 + b * NG * NU * 2)
                for t in range(ST_):
                    pe.wait_ge(s["z_ready"], b * ST_ + t + 1)
                    for half in range(2):
                        n = 2 * t + half
                        pe.wait_ge(s["zT_evac"], b * 2 * ST_ + n + 1)
                        for k in range(4):
                            tr = pe.transpose(pst[:, n // 2 % 2, n % 2, k * P:(k + 1) * P],
                                              xin[t % 2][:, (4 * half + k) * P:(4 * half + k + 1) * P], ident[:, :])
                        tr.then_inc(s["zT_ready"], 1)
                pe.wait_ge(s["zT_evac"], ZT0 + (b + 1) * 2 * ST_)
                i = 0
                for p in range(6):
                    for c in range(2):
                        project(b * N_WCHUNK + p, b * U_BATCH + i, i % 2, p % 2, c)
                        i += 1
                    if p in (2, 3):
                        pe.wait_ge(s["roped"], R0 + (b * N_WCHUNK + p) * 2 + 2)
                        for c in range(2):
                            pe.wait_ge(s["sh_free"], b * U_BATCH + i + 1)
                            for k in range(4):
                                tr = pe.transpose(psh[:, i % 2, k * P:(k + 1) * P],
                                                  vT[:, (4 * c + k) * P:(4 * c + k + 1) * P], ident[:, :])
                            tr.then_inc(s["sh_ready"], 1)
                            i += 1
                pe.wait_ge(restacked[0], (b * 4 + 1) * 240)
                for k in range(len(USES)):
                    row_scores(b * U_BATCH + i, i % 2, 0, k)
                    i += 1
                transpose_max(b * NG, b * U_BATCH + i, i % 2)
                over_groups(pe, b, group)


def output_projection(nc, sem, layer, oT_d, wo, x_in, x_out):
    s = {n: sem(f"o{layer}_{n}") for n in (
        "wl0", "wl1", "w_hi", "w_lo", "ol0", "ol1", "o_hi", "o_lo", "x0", "x1", "mm", "sum", "st0", "st1")}
    w_loaded, o_loaded, x_loaded, stored = ((s["wl0"], s["wl1"]), (s["ol0"], s["ol1"]), (s["x0"], s["x1"]),
                                            (s["st0"], s["st1"]))
    M0, L0, S0, DMA0 = 8, 2, 4, 16
    TURNS = NT // 4
    with ExitStack() as ctx:
        def sb(name, shape, dt=F32):
            return ctx.enter_context(nc.sbuf_tensor(f"o{layer}_{name}", shape, dt))

        wraw = [sb(f"wraw{i}", [P, D]) for i in range(2)]
        w = [sb(f"w_{n}", [P, KC, D], F32R) for n in ("hi", "lo")]
        oraw = [sb(f"oraw{i}", [P, NG, 2 * P]) for i in range(2)]
        o = [[sb(f"o_{n}{i}", [P, NG, 2 * P], F32R) for n in ("hi", "lo")] for i in range(2)]
        xres = [sb(f"xres{i}", [P, D]) for i in range(2)]
        pout = ctx.enter_context(nc.psum_tensor(f"o{layer}_pout", [P, 2, 2, BANK], F32))
        block = ctx.enter_context(nc.Block())

        @block.sync
        def _(sp):
            def load_w(k):
                if k >= 2:
                    sp.wait_ge(s["w_lo"], k - 1)
                sp.dma_start(wraw[k % 2][:, :], wo[k * P:(k + 1) * P, :]).then_inc(w_loaded[k % 2], 16)

            def load_o(i, par):
                sp.wait_ge(s["o_lo"], i + 1)
                sp.dma_start(oraw[par][:, :, :].rearrange("p g (t n) -> p g t n", n=P),
                             oT_d[:, :, ds(i * 2, 2), :].rearrange("g p t n -> p g t n")).then_inc(o_loaded[par], 16)

            for i in range(2):
                sp.sem_inc(stored[i], DMA0)
            load_w(0)
            load_o(0, 0)
            for k in range(1, KC):
                load_w(k)
            load_o(1, 1)

            def turn(j, more):
                for q in range(4):
                    sp.wait_ge(stored[q % 2], DMA0 + (j * 2 + q // 2) * 16)
                    sp.dma_start(xres[q % 2][:, :], x_in[ds((j * 4 + q) * P, P), :]).then_inc(x_loaded[q % 2], 16)
                    if q % 2 == 1:
                        sp.wait_ge(s["sum"], S0 + (j * 4 + q) * 2)
                        sp.dma_start(x_out[ds((j * 4 + q - 1) * P, P), :], xres[0][:, :]).then_inc(stored[0], 16)
                        if more:
                            load_o(j * 2 + 2 + q // 2, q // 2)
                        sp.wait_ge(s["sum"], S0 + (j * 4 + q) * 2 + 2)
                        sp.dma_start(x_out[ds((j * 4 + q) * P, P), :], xres[1][:, :]).then_inc(stored[1], 16)

            with sp.Fori(0, TURNS - 1) as j:
                turn(j, True)
            turn(TURNS - 1, False)
            for i in range(2):
                sp.wait_ge(stored[i], DMA0 + 16 * NT // 2)

        @block.scalar
        def _(act):
            def o_hi(i, i_half, par):
                act.wait_ge(o_loaded[par], i_half * 16 + 16)
                act.wait_ge(s["mm"], M0 - 4 + i * 4)
                act.activation(o[par][0][:, :, :], oraw[par][:, :, :], ACT.Copy).then_inc(s["o_hi"], 1)

            for k in range(KC):
                act.wait_ge(w_loaded[k % 2], (k // 2 + 1) * 16)
                act.activation(w[0][:, k, :], wraw[k % 2][:, :], ACT.Copy).then_inc(s["w_hi"], 1)
                if k == 0:
                    o_hi(0, 0, 0)
            with act.Fori(0, TURNS - 1) as j:
                o_hi(j * 2 + 1, j, 1)
                o_hi(j * 2 + 2, j + 1, 0)
            o_hi(NT // 2 - 1, TURNS - 1, 1)

        @block.vector
        def _(dve):
            def o_lo(i, par):
                dve.wait_ge(s["o_hi"], i + 1)
                dve.tensor_tensor(o[par][1][:, :, :], oraw[par][:, :, :], o[par][0][:, :, :].bitcast(F32),
                                  ALU.subtract).then_inc(s["o_lo"], 1)

            dve.drain().then_inc(s["o_lo"], L0)
            dve.drain().then_inc(s["sum"], S0)
            for k in range(KC):
                dve.wait_ge(s["w_hi"], k + 1)
                dve.tensor_tensor(w[1][:, k, :], wraw[k % 2][:, :], w[0][:, k, :].bitcast(F32), ALU.subtract)\
                    .then_inc(s["w_lo"], 1)
                if k == 0:
                    o_lo(0, 0)

            def turn(j, more):
                for q in range(4):
                    if q == 0:
                        o_lo(j * 2 + 1, 1)
                    if q == 2 and more:
                        o_lo(j * 2 + 2, 0)
                    dve.wait_ge(x_loaded[q % 2], (j * 2 + q // 2) * 16 + 16)
                    for half in range(2):
                        cols = slice(half * BANK, (half + 1) * BANK)
                        dve.wait_ge(s["mm"], M0 + (j * 4 + q) * 2 + half + 1)
                        dve.tensor_tensor(xres[q % 2][:, cols], xres[q % 2][:, cols], pout[:, q % 2, half, :],
                                          ALU.add).then_inc(s["sum"], 1)

            with dve.Fori(0, TURNS - 1) as j:
                turn(j, True)
            turn(TURNS - 1, False)

        @block.tensor
        def _(pe):
            pe.sem_inc(s["mm"], M0)
            with pe.Fori(0, TURNS) as j:
                for q in range(4):
                    par = q // 2
                    if q == 0:
                        pe.wait_ge(s["w_lo"], KC)
                    if q % 2 == 0:
                        pe.wait_ge(s["o_lo"], L0 + j * 2 + par + 1)
                    for half in range(2):
                        pe.wait_ge(s["sum"], (j * 4 + q) * 2 + half + 1)
                        passes = [(k, a, x) for k in range(KC) for a, x in ((0, 0), (0, 1), (1, 0))]
                        for i, (k, a, x) in enumerate(passes):
                            mm = pe.matmul(pout[:, q % 2, half, :], o[par][a][:, k, (q % 2) * P:(q % 2 + 1) * P],
                                           w[x][:, k, half * BANK:(half + 1) * BANK],
                                           start=(i == 0), stop=(i == len(passes) - 1))
                        mm.then_inc(s["mm"], 1)


NS = 4
C = D // NS
NL = NS * NS + 2 * NS
SINKHORN_ITERS = 50
TAU = 0.1


def hyper_connection(nc, sem, x_in, w24, base24, gate, w_branch, x_out):
    s = {n: sem(f"h_{n}") for n in (
        "const", "small", "x0", "x1", "stat_in", "rstd", "rms_in", "rms", "z", "zT_ready", "zT", "logit",
        "read", "gate", "e_in", "e_out", "z2", "pre", "preT_ready", "preT", "y", "mixed", "stored")}
    x_loaded = (s["x0"], s["x1"])
    ZR0, ZT0, LG0, RD0, MX0, PR0, PT0, Y0, DMA0 = 4, 4, 2, 2, 2, 2, 1, 1, 16
    with ExitStack() as ctx:
        def sb(name, shape, dt=F32):
            return ctx.enter_context(nc.sbuf_tensor(f"h_{name}", shape, dt))

        ident = sb("ident", [P, P])
        x = sb("x", [P, NT, D])
        z = [sb(f"z{i}", [P, D]) for i in range(2)]
        stat = sb("stat", [P, 2, 6])
        aggr = sb("aggr", [P, 2])
        mv = sb("mv", [P, NT, 2])
        nhalf = sb("nhalf", [P, NT])
        nmr = sb("nmr", [P, NT])
        rstd, var_e, rms, rms_e = (sb(n, [P, NT]) for n in ("rstd", "var_e", "rms", "rms_e"))
        zT = [sb(f"zT{i}", [P, KC, P]) for i in range(2)]
        w24_sb = sb("w24", [P, KC, NL])
        base = sb("base", [P, NL])
        wb = sb("wb", [P, C // P, C])
        lg = sb("lg", [P, NT, NL])
        m = sb("m", [P, NT, NS * NS])
        e = sb("e", [P, NT, NS * NS])
        pp = sb("pp", [P, NT, 2, NS])
        r64 = sb("r64", [P, NT, NS])
        sums = sb("sums", [P, NT, 2])
        g = sb("g", [P, 4])
        pre = [sb(f"pre{i}", [P, C]) for i in range(2)]
        preT = sb("preT", [P, C // P, P])
        pz = ctx.enter_context(nc.psum_tensor("h_pz", [P, 2, 2, BANK], F32))
        plg = ctx.enter_context(nc.psum_tensor("h_plg", [P, 2, BANK], F32))
        ppre = ctx.enter_context(nc.psum_tensor("h_ppre", [P, BANK], F32))
        py = plg
        block = ctx.enter_context(nc.Block())

        def lines(buf, axis):
            return buf[:, :, :].rearrange("p t (i j) -> p t i j" if axis == "row" else "p t (i j) -> p t j i", j=NS)

        def spread(v, n=NS):
            return v.unsqueeze(3).broadcast_to([P, NT, v.shape[2], n])

        def tile(buf, t):
            return buf[:, ds(t, 1), :].rearrange("p o n -> p (o n)")

        @block.sync
        def _(sp):
            for dst, src in ((w24_sb[:, :, :], w24), (base[:, :], base24), (g[:, 0:1], gate),
                             (wb[:, :, :], w_branch.rearrange("(c p) n -> p c n", p=P))):
                sp.dma_start(dst, src).then_inc(s["small"], 16)
            for i in range(2):
                sp.sem_inc(x_loaded[i], DMA0)
            with sp.Fori(0, NT // 2) as j:
                for i in range(2):
                    sp.wait_ge(x_loaded[i], DMA0 + j * 16)
                    sp.dma_start(x[:, ds(j * 2 + i, 1), :].rearrange("p o n -> p (o n)"),
                                 x_in[ds((j * 2 + i) * P, P), :]).then_inc(x_loaded[i], 16)
            with sp.Fori(0, NT) as t:
                sp.wait_ge(s["mixed"], MX0 + t + 1)
                sp.dma_start(x_out[ds(t * P, P), :],
                             x[:, ds(t, 1), :].rearrange("p o n -> p (o n)")).then_inc(s["stored"], 16)
            sp.wait_ge(s["stored"], 16 * NT)

        @block.gpsimd
        def _(pool):
            pool.memset(ident[:, :], 0.0)
            pool.memset(nhalf[:, :], -0.5)
            pool.drain()
            pool.affine_select(out=ident[:, :], in_=ident[:, :], compare_op=ALU.not_equal, fill=1.0, base=0,
                               pattern=[[-1, P]], channel_multiplier=1).then_inc(s["const"], 1)
            pool.wait_ge(s["stat_in"], 1)
            pool.tensor_tensor(rstd[:, :], var_e[:, :], nhalf[:, :], ALU.pow).then_inc(s["rstd"], 1)
            pool.wait_ge(s["rms_in"], 1)
            pool.tensor_tensor(rms[:, :], rms_e[:, :], nhalf[:, :], ALU.pow).then_inc(s["rms"], 1)

        @block.scalar
        def _(act):
            act.wait_ge(s["small"], 64)
            act.activation(g[:, 1:2], g[:, 0:1], ACT.Exp, scale=-1.0).then_inc(s["gate"], 1)
            act.drain().then_inc(s["zT"], ZT0)
            act.drain().then_inc(s["preT"], PT0)
            with act.Fori(0, NT // 2) as j:
                for par in range(2):
                    t = j * 2 + par
                    for half in range(2):
                        act.wait_ge(s["logit"], t + 1)
                        act.wait_ge(s["zT_ready"], ZR0 + t * 2 + half + 1)
                        act.activation(zT[par][:, 4 * half:4 * half + 4, :],
                                       pz[:, par, half, :].rearrange("p (k n) -> p k n", n=P), ACT.Copy)\
                            .then_inc(s["zT"], 1)
            act.wait_ge(s["e_in"], 1)
            act.activation(pp[:, :, :, :], pp[:, :, :, :], ACT.Exp).then_inc(s["e_out"], 1)
            act.activation(e[:, :, :], m[:, :, :], ACT.Exp).then_inc(s["e_out"], 1)
            act.wait_ge(s["e_in"], 2)
            act.activation(r64[:, :, :], r64[:, :, :], ACT.Ln).then_inc(s["e_out"], 1)
            act.wait_ge(s["e_in"], 3)
            act.activation(m[:, :, :], m[:, :, :], ACT.Exp).then_inc(s["e_out"], 1)

            def normalise(t, par):
                act.wait_ge(s["mixed"], t + 1)
                act.activation(z[par][:, :], tile(x, t), ACT.Identity, bias=nmr[:, ds(t, 1)],
                               scale=rstd[:, ds(t, 1)]).then_inc(s["z2"], 1)

            def copy_pre(t):
                act.wait_ge(s["y"], t + 1)
                act.wait_ge(s["preT_ready"], PR0 + t + 1)
                act.activation(preT[:, :, :], ppre[:, 0:C].rearrange("p (k n) -> p k n", n=P), ACT.Copy)\
                    .then_inc(s["preT"], 1)

            normalise(0, 0)
            normalise(1, 1)
            with act.Fori(0, NT // 2 - 1) as j:
                for par in range(2):
                    copy_pre(j * 2 + par)
                    normalise(j * 2 + par + 2, par)
            for par in range(2):
                copy_pre(NT - 2 + par)

        @block.vector
        def _(dve):
            dve.drain().then_inc(s["read"], RD0)
            dve.drain().then_inc(s["mixed"], MX0)
            with dve.Fori(0, NT // 2) as j:
                for i in range(2):
                    t = j * 2 + i
                    dve.wait_ge(x_loaded[i], DMA0 + j * 16 + 16)
                    for half in range(2):
                        dve.bn_stats(stat[:, half, :], x[:, ds(t, 1), half * BANK:(half + 1) * BANK]
                                     .rearrange("p o n -> p (o n)"))
                    dve.drain()
                    dve.bn_aggr(aggr[:, :], stat[:, :, :])
                    dve.drain()
                    dve.tensor_copy(tile(mv, t), aggr[:, :])
            dve.drain()
            dve.tensor_scalar(var_e[:, :], mv[:, :, 1], LN_EPS, None, ALU.add).then_inc(s["stat_in"], 1)
            dve.wait_ge(s["rstd"], 1)
            dve.tensor_tensor(rms_e[:, :], rstd[:, :], rstd[:, :], ALU.mult)
            dve.drain()
            dve.tensor_tensor(rms_e[:, :], rms_e[:, :], mv[:, :, 1], ALU.mult)
            dve.drain()
            dve.tensor_scalar(rms_e[:, :], rms_e[:, :], RMS_EPS, None, ALU.add).then_inc(s["rms_in"], 1)
            dve.tensor_tensor(nmr[:, :], rstd[:, :], mv[:, :, 0], ALU.mult)
            dve.drain()
            dve.tensor_scalar(nmr[:, :], nmr[:, :], -1.0, None, ALU.mult)

            def normalise_tile(t, par):
                dve.wait_ge(s["zT_ready"], 2 * t + 2)
                dve.tensor_scalar(z[par][:, :], tile(x, t), mv[:, ds(t, 1), 0], rstd[:, ds(t, 1)],
                                  ALU.subtract, ALU.mult).then_inc(s["z"], 1)

            def logits(t, par):
                dve.wait_ge(s["logit"], LG0 + t + 1)
                dve.scalar_tensor_tensor(tile(lg, t), plg[:, par, 0:NL], rms[:, ds(t, 1)], base[:, :],
                                         ALU.mult, ALU.add).then_inc(s["read"], 1)

            normalise_tile(0, 0)
            normalise_tile(1, 1)
            dve.wait_ge(s["rms"], 1)
            dve.wait_ge(s["small"], 64)
            with dve.Fori(0, NT // 2 - 1) as j:
                for par in range(2):
                    normalise_tile(j * 2 + par + 2, par)
                    logits(j * 2 + par, par)
            for par in range(2):
                logits(NT - 2 + par, par)
            dve.drain()
            ppl = lg[:, :, NS * NS:].rearrange("p t (a n) -> p t a n", a=2)
            half64 = r64[:, :, 0:2]
            dve.tensor_reduce(half64, ppl, AX.X, ALU.max)
            dve.drain()
            dve.tensor_tensor(pp[:, :, :, :], ppl, spread(half64), ALU.subtract)
            dve.tensor_scalar(m[:, :, :], lg[:, :, 0:NS * NS], 1.0 / TAU, None, ALU.mult)
            dve.drain()
            dve.tensor_reduce(r64[:, :, :], lines(m, "row"), AX.X, ALU.max)
            dve.drain()
            dve.tensor_tensor(lines(m, "row"), lines(m, "row"), spread(r64[:, :, :]), ALU.subtract)\
                .then_inc(s["e_in"], 1)
            dve.wait_ge(s["e_out"], 2)
            dve.tensor_reduce(r64[:, :, :], lines(e, "row"), AX.X, ALU.add)\
                .then_inc(s["e_in"], 1)
            dve.wait_ge(s["gate"], 1)
            dve.tensor_scalar(g[:, 2:3], g[:, 1:2], 1.0, None, ALU.add)
            dve.drain()
            dve.reciprocal(g[:, 2:3], g[:, 2:3])
            dve.drain()
            dve.tensor_scalar(g[:, 3:4], g[:, 2:3], -1.0, 1.0, ALU.mult, ALU.add)
            dve.wait_ge(s["e_out"], 3)
            dve.tensor_tensor(lines(m, "row"), lines(m, "row"), spread(r64[:, :, :]), ALU.subtract)
            dve.drain()
            dve.tensor_reduce(r64[:, :, :], lines(m, "col"), AX.X, ALU.max)
            dve.drain()
            dve.tensor_tensor(lines(m, "col"), lines(m, "col"), spread(r64[:, :, :]), ALU.subtract)\
                .then_inc(s["e_in"], 1)
            dve.tensor_reduce(sums[:, :, :], pp[:, :, :, :], AX.X, ALU.add)
            dve.drain()
            dve.reciprocal(sums[:, :, :], sums[:, :, :])
            dve.drain()
            dve.tensor_tensor(pp[:, :, :, :], pp[:, :, :, :], spread(sums[:, :, :]), ALU.mult)
            dve.wait_ge(s["e_out"], 4)

            def normalise(axis):
                dve.drain()
                dve.tensor_reduce(r64[:, :, :], lines(m, axis), AX.X, ALU.add)
                dve.drain()
                dve.reciprocal(r64[:, :, :], r64[:, :, :])
                dve.drain()
                dve.tensor_tensor(lines(m, axis), lines(m, axis), spread(r64[:, :, :]), ALU.mult)

            normalise("col")
            with dve.Fori(0, SINKHORN_ITERS - 1):
                normalise("row")
                normalise("col")
            dve.drain()
            dve.tensor_scalar(m[:, :, :], m[:, :, :], g[:, 2:3], None, ALU.mult)
            dve.drain()
            diag = m[:, :, 0:NS * NS:NS + 1]
            dve.tensor_scalar(diag, diag, g[:, 3:4], None, ALU.add)
            dve.drain()

            def stream(t, n):
                return x[:, ds(t, 1), n * C:(n + 1) * C].rearrange("p o n -> p (o n)")

            def premix(t, par):
                dve.wait_ge(s["z2"], t + 1)
                dve.wait_ge(s["preT_ready"], t + 1)
                for n in range(NS):
                    zn = z[par][:, n * C:(n + 1) * C]
                    if n == 0:
                        dve.tensor_scalar(pre[par][:, :], zn, pp[:, ds(t, 1), 0, n], None, ALU.mult)
                    else:
                        dve.drain()
                        ins = dve.scalar_tensor_tensor(pre[par][:, :], zn, pp[:, ds(t, 1), 0, n],
                                                       pre[par][:, :], ALU.mult, ALU.add)
                ins.then_inc(s["pre"], 1)

            def mix(t, par):
                for j in range(NS):
                    for i in range(NS):
                        dve.scalar_tensor_tensor(stream(t, i), z[par][:, j * C:(j + 1) * C],
                                                 m[:, ds(t, 1), i * NS + j], stream(t, i), ALU.mult, ALU.add)
                    dve.drain()
                dve.wait_ge(s["y"], Y0 + t + 1)
                for i in range(NS):
                    dve.scalar_tensor_tensor(stream(t, i), py[:, par, 0:C], pp[:, ds(t, 1), 1, i],
                                             stream(t, i), ALU.mult, ALU.add)
                dve.drain().then_inc(s["mixed"], 1)

            premix(0, 0)
            with dve.Fori(0, NT // 2 - 1) as j:
                for par in range(2):
                    premix(j * 2 + par + 1, 1 - par)
                    mix(j * 2 + par, par)
            premix(NT - 1, 1)
            mix(NT - 2, 0)
            mix(NT - 1, 1)

        @block.tensor
        def _(pe):
            def transposes(t, par):
                pe.wait_ge(s["z"], t + 1)
                for half in range(2):
                    pe.wait_ge(s["zT"], 2 * t + half + 1)
                    for k in range(4):
                        tr = pe.transpose(pz[:, par, half, k * P:(k + 1) * P],
                                          z[par][:, (4 * half + k) * P:(4 * half + k + 1) * P], ident[:, :])
                    tr.then_inc(s["zT_ready"], 1)

            def logits(t, par):
                pe.wait_ge(s["read"], t + 1)
                pe.wait_ge(s["zT"], ZT0 + 2 * t + 2)
                for k in range(KC):
                    mm = pe.matmul(plg[:, par, 0:NL], zT[par][:, k, :], w24_sb[:, k, :],
                                   start=(k == 0), stop=(k == KC - 1))
                mm.then_inc(s["logit"], 1)

            def branch(t, par):
                pe.wait_ge(s["pre"], t + 1)
                pe.wait_ge(s["preT"], t + 1)
                for k in range(C // P):
                    tr = pe.transpose(ppre[:, k * P:(k + 1) * P], pre[par][:, k * P:(k + 1) * P], ident[:, :])
                tr.then_inc(s["preT_ready"], 1)
                pe.wait_ge(s["mixed"], t + 1)
                pe.wait_ge(s["preT"], PT0 + t + 1)
                for k in range(C // P):
                    mm = pe.matmul(py[:, par, 0:C], preT[:, k, :], wb[:, k, :],
                                   start=(k == 0), stop=(k == C // P - 1))
                mm.then_inc(s["y"], 1)

            pe.wait_ge(s["const"], 1)
            pe.wait_ge(s["small"], 64)
            pe.sem_inc(s["zT_ready"], ZR0)
            pe.sem_inc(s["logit"], LG0)
            pe.sem_inc(s["preT_ready"], PR0)
            pe.sem_inc(s["y"], Y0)
            transposes(0, 0)
            with pe.Fori(0, NT // 2 - 1) as j:
                for par in range(2):
                    transposes(j * 2 + par + 1, 1 - par)
                    logits(j * 2 + par, par)
            transposes(NT - 1, 1)
            logits(NT - 2, 0)
            logits(NT - 1, 1)
            with pe.Fori(0, NT // 2) as j:
                for par in range(2):
                    branch(j * 2 + par, par)


NE, NR = 8, 16
ER = NE * NR
NX = 256
SCALING = 32.0 / 16.0
MAX_THRESHOLD = 0.125


def expert_ffn(nc, sem, x_in, w_base, w_small, w_b, bias, b_thr, x_out):
    s = {n: sem(f"e_{n}") for n in (
        "const", "small", "w0", "w1", "w_hi", "w_lo", "x0", "x1", "x2", "x3", "stats", "pow", "z", "zT_ready",
        "zT_hi", "zT_lo", "ex", "g_in", "g_exp", "hw", "hwT_ready", "hw_hi", "hw_lo", "out", "xb", "done",
        "st0", "st1", "st2", "st3")}
    x_loaded, stored = [s[f"x{i}"] for i in range(4)], [s[f"st{i}"] for i in range(4)]
    w_loaded = (s["w0"], s["w1"])
    ZT0, HL0, DN0, ZR0, DMA0 = 2, 2, 4, 4, 16
    TURNS = NT // 4
    with ExitStack() as ctx:
        def sb(name, shape, dt=F32):
            return ctx.enter_context(nc.sbuf_tensor(f"e_{name}", shape, dt))

        ident = sb("ident", [P, P])
        nhalf = sb("nhalf", [P, 1])
        bias_sb = sb("bias", [P, D])
        thr_b = sb("thr_b", [P, 1])
        wraw = [sb(f"wraw{i}", [P, D]) for i in range(2)]
        wbase = [sb(f"wbase_{n}", [P, KC, D], F32R) for n in ("hi", "lo")]
        wsmall = [sb(f"wsmall_{n}", [P, KC, NX], F32R) for n in ("hi", "lo")]
        wexp = [sb(f"wexp_{n}", [P, D], F32R) for n in ("hi", "lo")]
        x = [sb(f"x{i}", [P, D]) for i in range(4)]
        z = sb("z", [P, D])
        stat = sb("stat", [P, 2, 6])
        mv = [sb(f"mv{i}", [P, 4]) for i in range(2)]
        zT = [[sb(f"zT_{n}{i}", [P, KC, P], F32R) for n in ("hi", "lo")] for i in range(2)]
        lg = sb("lg", [P, NE + 1])
        nmx = sb("nmx", [P, 1])
        ge = sb("ge", [P, NE + 1])
        sc = sb("sc", [P, 8])
        hw = sb("hw", [P, ER])
        hwT = [sb(f"hwT_{n}", [P, P], F32R) for n in ("hi", "lo")]
        pz = ctx.enter_context(nc.psum_tensor("e_pz", [P, 2, BANK], F32))
        pex = ctx.enter_context(nc.psum_tensor("e_pex", [P, 2, BANK], F32))
        pout = ctx.enter_context(nc.psum_tensor("e_pout", [P, 2, 2, BANK], F32))
        block = ctx.enter_context(nc.Block())

        W = [(w_small[k * P:(k + 4) * P, :].rearrange("(k p) n -> p k n", p=P), 4,
              [w[:, k:k + 4, :] for w in wsmall]) for k in (0, 4)]
        W += [(w_base[k * P:(k + 1) * P, :].rearrange("p (o n) -> p o n", o=1), 1,
               [w[:, k:k + 1, :] for w in wbase]) for k in range(KC)]
        W += [(w_b.rearrange("p (o n) -> p o n", o=1), 1,
               [w[:, :].rearrange("p (o n) -> p o n", o=1) for w in wexp])]

        def turns(eng, turn):
            with eng.Fori(0, TURNS - 1) as j:
                turn(j, False)
            turn(TURNS - 1, True)

        @block.sync
        def _(sp):
            def load_x(t, q, j):
                sp.wait_ge(stored[q], DMA0 + j * 16)
                sp.dma_start(x[q][:, :], x_in[ds(t * P, P), :]).then_inc(x_loaded[q], 16)

            def load_w(i):
                if i >= 2:
                    sp.wait_ge(s["w_lo"], i - 1)
                src, n, _ = W[i]
                sp.dma_start(wraw[i % 2][:, :].rearrange("p (k n) -> p k n", k=n), src).then_inc(w_loaded[i % 2], 16)

            for q in range(4):
                sp.sem_inc(stored[q], DMA0)
            for q in range(2):
                load_x(q, q, 0)
            sp.dma_start(bias_sb[:, :], bias).then_inc(s["small"], 16)
            sp.dma_start(thr_b[:, :], b_thr).then_inc(s["small"], 16)
            for i in range(len(W)):
                load_w(i)
            for q in range(2, 4):
                load_x(q, q, 0)

            def turn(j, last):
                for q in range(4):
                    sp.wait_ge(s["done"], DN0 + (j * 4 + q) * 2 + 2)
                    sp.dma_start(x_out[ds((j * 4 + q) * P, P), :], x[q][:, :]).then_inc(stored[q], 16)
                    if not last:
                        load_x((j + 1) * 4 + q, q, j + 1)

            turns(sp, turn)
            for q in range(4):
                sp.wait_ge(stored[q], DMA0 + 16 * TURNS)

        @block.gpsimd
        def _(pool):
            pool.memset(ident[:, :], 0.0)
            pool.memset(nhalf[:, :], -0.5)
            pool.drain()
            pool.affine_select(out=ident[:, :], in_=ident[:, :], compare_op=ALU.not_equal, fill=1.0, base=0,
                               pattern=[[-1, P]], channel_multiplier=1).then_inc(s["const"], 1)
            pool.wait_ge(s["small"], 32)

            def rstd(t, par):
                pool.wait_ge(s["stats"], t + 1)
                pool.tensor_tensor(mv[par][:, 3:4], mv[par][:, 2:3], nhalf[:, :], ALU.pow).then_inc(s["pow"], 1)

            def add_bias(t, q):
                pool.wait_ge(s["z"], t + 1)
                pool.tensor_tensor(x[q][:, :], x[q][:, :], bias_sb[:, :], ALU.add).then_inc(s["xb"], 1)

            rstd(0, 0)
            add_bias(0, 0)
            rstd(1, 1)

            def turn(j, last):
                for q in range(4):
                    if last and q == 3:
                        continue
                    add_bias(j * 4 + q + 1, (q + 1) % 4)
                    if not (last and q == 2):
                        rstd(j * 4 + q + 2, q % 2)

            turns(pool, turn)

        @block.scalar
        def _(act):
            for i, (_, n, dst) in enumerate(W):
                act.wait_ge(w_loaded[i % 2], (i // 2 + 1) * 16)
                act.activation(dst[0], wraw[i % 2][:, :].rearrange("p (k n) -> p k n", k=n), ACT.Copy)\
                    .then_inc(s["w_hi"], 1)

            def part_hi(t, par):
                for half in range(2):
                    act.wait_ge(s["zT_ready"], ZR0 + 2 * t + half + 1)
                    act.activation(zT[par][0][:, 4 * half:4 * half + 4, :],
                                   pz[:, half, :].rearrange("p (k n) -> p k n", n=P), ACT.Copy).then_inc(s["zT_hi"], 1)

            def experts(t, par):
                act.wait_ge(s["g_in"], t + 1)
                act.activation(ge[:, :], lg[:, :], ACT.Exp).then_inc(s["g_exp"], 1)
                act.wait_ge(s["hwT_ready"], t + 1)
                act.activation(hwT[0][:, :], pex[:, par, NX:NX + P], ACT.Copy).then_inc(s["hw_hi"], 1)

            part_hi(0, 0)

            def turn(j, last):
                for q in range(4):
                    if not (last and q == 3):
                        part_hi(j * 4 + q + 1, (q + 1) % 2)
                    experts(j * 4 + q, q % 2)

            turns(act, turn)

        @block.vector
        def _(dve):
            dve.drain().then_inc(s["zT_lo"], ZT0)
            dve.drain().then_inc(s["hw_lo"], HL0)
            dve.drain().then_inc(s["done"], DN0)

            def statistics(t, par, q, jq):
                dve.wait_ge(x_loaded[q], jq * 16 + 16)
                for half in range(2):
                    dve.bn_stats(stat[:, half, :], x[q][:, half * BANK:(half + 1) * BANK])
                dve.drain()
                dve.bn_aggr(mv[par][:, 0:2], stat[:, :, :])
                dve.drain()
                dve.tensor_scalar(mv[par][:, 2:3], mv[par][:, 1:2], LN_EPS, None, ALU.add).then_inc(s["stats"], 1)

            def normalise(t, par, q):
                dve.wait_ge(s["pow"], t + 1)
                dve.wait_ge(s["zT_ready"], 2 * t + 2 + 2)
                dve.tensor_scalar(z[:, :], x[q][:, :], mv[par][:, 0:1], mv[par][:, 3:4],
                                  ALU.subtract, ALU.mult).then_inc(s["z"], 1)

            def part_lo(t, par):
                for half in range(2):
                    dve.wait_ge(s["zT_hi"], 2 * t + half + 1)
                    cols = slice(4 * half, 4 * half + 4)
                    dve.tensor_tensor(zT[par][1][:, cols, :], pz[:, half, :].rearrange("p (k n) -> p k n", n=P),
                                      zT[par][0][:, cols, :].bitcast(F32), ALU.subtract).then_inc(s["zT_lo"], 1)

            def experts(t, par):
                logits = pex[:, par, ER:ER + NE + 1]
                dve.wait_ge(s["ex"], t + 1)
                dve.tensor_reduce(nmx[:, :], logits[:, 0:NE], AX.X, ALU.max)
                dve.tensor_scalar(lg[:, NE:], logits[:, NE:], thr_b[:, :], -1.0, ALU.add, ALU.mult)
                dve.drain()
                dve.tensor_scalar(lg[:, 0:NE], logits[:, 0:NE], nmx[:, :], None, ALU.subtract).then_inc(s["g_in"], 1)
                dve.wait_ge(s["g_exp"], t + 1)
                dve.tensor_reduce(sc[:, 0:1], ge[:, 0:NE], AX.X, ALU.add)
                dve.tensor_scalar(sc[:, 1:2], ge[:, NE:], 1.0, None, ALU.add)
                dve.drain()
                dve.reciprocal(sc[:, 2:4], sc[:, 0:2])
                dve.drain()
                dve.tensor_scalar(sc[:, 3:4], sc[:, 3:4], MAX_THRESHOLD, None, ALU.mult)
                dve.drain()
                dve.tensor_scalar(ge[:, 0:NE], ge[:, 0:NE], sc[:, 2:3], sc[:, 3:4], ALU.mult, ALU.subtract)
                dve.drain()
                dve.tensor_scalar(ge[:, 0:NE], ge[:, 0:NE], 0.0, None, ALU.max)
                dve.drain()
                dve.tensor_reduce(sc[:, 4:5], ge[:, 0:NE], AX.X, ALU.add)
                dve.drain()
                dve.tensor_scalar(sc[:, 5:6], sc[:, 4:5], 0.0, None, ALU.is_equal)
                dve.drain()
                dve.tensor_tensor(sc[:, 4:5], sc[:, 4:5], sc[:, 5:6], ALU.add)
                dve.drain()
                dve.reciprocal(sc[:, 6:7], sc[:, 4:5])
                dve.drain()
                dve.tensor_scalar(ge[:, 0:NE], ge[:, 0:NE], sc[:, 6:7], SCALING, ALU.mult, ALU.mult)
                dve.drain()
                dve.tensor_tensor(hw[:, :].rearrange("p (e r) -> p e r", r=NR),
                                  pex[:, par, 0:ER].rearrange("p (e r) -> p e r", r=NR),
                                  ge[:, 0:NE].unsqueeze(2).broadcast_to([P, NE, NR]), ALU.mult).then_inc(s["hw"], 1)

            def expert_lo(t, par):
                dve.wait_ge(s["hw_hi"], t + 1)
                dve.tensor_tensor(hwT[1][:, :], pex[:, par, NX:NX + P], hwT[0][:, :].bitcast(F32), ALU.subtract)\
                    .then_inc(s["hw_lo"], 1)

            def finish(t, par, q):
                dve.wait_ge(s["xb"], t + 1)
                for half in range(2):
                    cols = slice(half * BANK, (half + 1) * BANK)
                    dve.wait_ge(s["out"], 2 * t + half + 1)
                    dve.tensor_tensor(x[q][:, cols], x[q][:, cols], pout[:, par, half, :], ALU.add)\
                        .then_inc(s["done"], 1)

            statistics(0, 0, 0, 0)
            normalise(0, 0, 0)
            statistics(1, 1, 1, 0)
            for i, (_, n, dst) in enumerate(W):
                dve.wait_ge(s["w_hi"], i + 1)
                dve.tensor_tensor(dst[1], wraw[i % 2][:, :].rearrange("p (k n) -> p k n", k=n), dst[0].bitcast(F32),
                                  ALU.subtract).then_inc(s["w_lo"], 1)
            part_lo(0, 0)
            dve.wait_ge(s["small"], 32)

            def turn(j, last):
                for q in range(4):
                    t, par = j * 4 + q, q % 2
                    if not (last and q == 3):
                        normalise(t + 1, 1 - par, (q + 1) % 4)
                    if not (last and q >= 2):
                        dve.drain()
                        statistics(t + 2, par, (q + 2) % 4, j + (q + 2) // 4)
                    experts(t, par)
                    if not (last and q == 3):
                        part_lo(t + 1, 1 - par)
                    expert_lo(t, par)
                    finish(t, par, q)

            turns(dve, turn)

        @block.tensor
        def _(pe):
            THREE = ((0, 0), (0, 1), (1, 0))

            def transposes(t):
                pe.wait_ge(s["z"], t + 1)
                for half in range(2):
                    pe.wait_ge(s["zT_lo"], 2 * t + half + 1)
                    for k in range(4):
                        tr = pe.transpose(pz[:, half, k * P:(k + 1) * P],
                                          z[:, (4 * half + k) * P:(4 * half + k + 1) * P], ident[:, :])
                    tr.then_inc(s["zT_ready"], 1)

            def products(t, par):
                pe.wait_ge(s["zT_lo"], ZT0 + 2 * t + 2)
                pe.wait_ge(s["hw_lo"], t + 1)
                n = 0
                for k in range(KC):
                    for a, b in THREE:
                        mm = pe.matmul(pex[:, par, 0:NX], zT[par][a][:, k, :], wsmall[b][:, k, :],
                                       start=(n == 0), stop=(n == 3 * KC - 1))
                        n += 1
                mm.then_inc(s["ex"], 1)
                for half in range(2):
                    pe.wait_ge(s["done"], 2 * t + half + 1)
                    n = 0
                    for k in range(KC):
                        for a, b in THREE:
                            pe.matmul(pout[:, par, half, :], zT[par][a][:, k, :],
                                      wbase[b][:, k, half * BANK:(half + 1) * BANK], start=(n == 0), stop=False)
                            n += 1
                pe.wait_ge(s["hw"], t + 1)
                pe.transpose(pex[:, par, NX:NX + P], hw[:, :], ident[:, :]).then_inc(s["hwT_ready"], 1)
                pe.wait_ge(s["hw_lo"], HL0 + t + 1)
                for half in range(2):
                    for n, (a, b) in enumerate(THREE):
                        mm = pe.matmul(pout[:, par, half, :], hwT[a][:, :], wexp[b][:, half * BANK:(half + 1) * BANK],
                                       start=False, stop=(n == 2))
                    mm.then_inc(s["out"], 1)

            pe.wait_ge(s["const"], 1)
            pe.sem_inc(s["zT_ready"], ZR0)
            transposes(0)
            pe.wait_ge(s["w_lo"], len(W))

            def turn(j, last):
                for q in range(4):
                    if not (last and q == 3):
                        transposes(j * 4 + q + 1)
                    products(j * 4 + q, q % 2)

            turns(pe, turn)


@contextmanager
def stage(nc):
    taken = []

    def sem(name):
        taken.append(nc.alloc_semaphore(name))
        return taken[-1]

    yield sem
    nc.clear_and_free_semaphores(taken)
    nc.all_engine_barrier()


def build(nc, x, wqkv, rope, wo, ffn0, ffn1, out):
    def scratch(name, shape):
        return nc.dram_tensor(name, shape, F32, kind="Internal").ap()

    x1, x2, x3 = (scratch(f"x{i}", (T, D)) for i in (1, 2, 3))
    oT_d = [scratch(f"oT_{i}", (NG, P, NT, P)) for i in range(2)]
    swaps = [[i ^ 1 for i in range(HD)], [(i + HD // 2) % HD for i in range(HD)]]
    with stage(nc) as sem:
        attention(nc, sem, 0, x, wqkv[0], *rope[0], swaps[0], oT_d[0])
    with stage(nc) as sem:
        output_projection(nc, sem, 0, oT_d[0], wo[0], x, x1)
    with stage(nc) as sem:
        hyper_connection(nc, sem, x1, *ffn0, x2)
    with stage(nc) as sem:
        attention(nc, sem, 1, x2, wqkv[1], *rope[1], swaps[1], oT_d[1])
    with stage(nc) as sem:
        output_projection(nc, sem, 1, oT_d[1], wo[1], x2, x3)
    with stage(nc) as sem:
        expert_ffn(nc, sem, x3, *ffn1, out)


def rope_tables(pair_of, sign_of):
    freq = (1.0 / np.float32(THETA) ** (np.arange(0, HD, 2, dtype=np.float32) / np.float32(HD))).astype(np.float32)
    ang = np.outer(freq[pair_of], np.arange(S, dtype=np.float32)).astype(np.float32)
    cos, sin = np.cos(ang).astype(np.float32), (np.sin(ang) * sign_of[:, None]).astype(np.float32)
    return np.tile(cos, (GH, 1)), np.tile(sin, (GH, 1))


def qkv_layout(wk, wv, wq):
    w = np.concatenate([wk, wv, wq], axis=1).reshape(KC, P, N_WCHUNK, P).transpose(2, 1, 0, 3)
    return np.concatenate([w, w[:2]], axis=0)


def laid_out(a):
    i = np.arange(HD)
    rope = [rope_tables(i // 2, np.where(i % 2 == 0, -1, 1).astype(np.float32)),
            rope_tables(i % (HD // 2), np.where(i < HD // 2, -1, 1).astype(np.float32))]
    w24 = np.concatenate([a["L0_ffn_W_res"], a["L0_ffn_W_pre"], a["L0_ffn_W_post"]], axis=0)
    base24 = np.concatenate([a["L0_ffn_H_res_base"].reshape(-1), a["L0_ffn_H_pre_base"], a["L0_ffn_H_post_base"]])
    small = np.concatenate([a["L1_ffn_A_w"].reshape(ER, D), a["L1_ffn_W_gate"], a["L1_ffn_W_thr"][None, :],
                            np.zeros((NX - ER - NE - 1, D), np.float32)], axis=0)
    out = {
        "x": a["L0_attn_x"].reshape(T, D),
        "wqkv0": qkv_layout(a["L0_attn_wk"], a["L0_attn_wv"], a["L0_attn_wq"]),
        "wqkv1": qkv_layout(a["L1_attn_Wk"], a["L1_attn_Wv"], a["L1_attn_Wq"]),
        "cos0": rope[0][0], "sin0": rope[0][1], "cos1": rope[1][0], "sin1": rope[1][1],
        "wo0": a["L0_attn_wo"], "wo1": a["L1_attn_Wo"],
        "w24": w24.T.reshape(KC, P, NL).transpose(1, 0, 2),
        "base24": np.broadcast_to(base24, (P, NL)),
        "gate": np.broadcast_to(a["L0_ffn_gate"], (P, 1)),
        "w_branch": a["L0_ffn_W_branch"],
        "w_base": a["L1_ffn_W_base"].T,
        "w_small": small.T,
        "w_b": a["L1_ffn_B_w"].transpose(0, 2, 1).reshape(ER, D),
        "bias": np.broadcast_to(a["L1_ffn_b_base"], (P, D)),
        "b_thr": np.broadcast_to(a["L1_ffn_b_thr"], (P, 1)),
    }
    return {n: np.ascontiguousarray(v) for n, v in out.items()}


def program(nc, t, out):
    build(nc, t["x"], (t["wqkv0"], t["wqkv1"]), ((t["cos0"], t["sin0"]), (t["cos1"], t["sin1"])),
          (t["wo0"], t["wo1"]), (t["w24"], t["base24"], t["gate"], t["w_branch"]),
          (t["w_base"], t["w_small"], t["w_b"], t["bias"], t["b_thr"]), out)


def kernel(**inputs):
    import concourse.bacc as bacc
    from concourse.bass_utils import run_bass_kernel_spmd

    nc = bacc.Bacc("TRN2", target_bir_lowering=False, num_devices=1)
    arrays = laid_out({n: np.asarray(v) for n, v in inputs.items()})
    aps = {n: nc.dram_tensor(f"in_{n}", v.shape, F32, kind="ExternalInput").ap() for n, v in arrays.items()}
    out = nc.dram_tensor("out", (T, D), F32, kind="ExternalOutput").ap()
    program(nc, aps, out)
    r = run_bass_kernel_spmd(nc, [{f"in_{n}": v for n, v in arrays.items()}], core_ids=[0])
    return r.results[0]["out"].reshape(B, S, D)
```

```python
from contextlib import ExitStack, contextmanager

import numpy as np

import concourse.bass as bass
from concourse import mybir

F32 = mybir.dt.float32
F32R = mybir.dt.float32r
BF16 = mybir.dt.bfloat16
ALU = mybir.AluOpType
ACT = mybir.ActivationFunctionType
AX = mybir.AxisListType

P = 128
B, S, D = 2, 1024, 1024
T = B * S
NT = T // P
ST_ = S // P
KC = D // P
HD = 32
NG = 8
GH = 4
BANK = 512
NQC = S // BANK
NX_BUF = 6
LN_EPS = 1e-5
RMS_EPS = 1.1920929e-07
THETA = 10000.0
MASKED = -1e30
N_WCHUNK = 12
ds = bass.ds


UNITS = [(qc, ki) for qc in range(NQC) for ki in range(4 * qc + 4)]
NU = len(UNITS)
DIAGONAL = [e for e, (qc, ki) in enumerate(UNITS) if ki >= 4 * qc]
CHUNK_END = [e for e, (qc, ki) in enumerate(UNITS) if ki == 4 * qc + 3]


def unit_offset(e):
    qc, ki = UNITS[e]
    return max(0, ki * P - qc * BANK)


def score_uses():
    out = []
    for qt in range(ST_):
        for kc in range(qt // 4 + 1):
            n = min(BANK, (qt + 1) * P - kc * BANK)
            m = BANK // n if BANK % n == 0 else 1
            for h in range(0, GH, m):
                out.append((qt, kc, n, tuple(range(h, h + m)), kc == qt // 4))
    return out


USES = score_uses()
SECOND_HALF = [qt for qt, *_ in USES].index(ST_ // 2)


PIECES = 4


def columns(step):
    what, e, _ = step
    n = BANK - unit_offset(e)
    return 2 * max(n, BANK // 2) if what == "ST" else 4 * n


def iteration(full_s=True, proj=True):
    steps = [[("ST", e + 1, 0), ("ST", e + 1, 1), ("PV", e, 0), ("PV", e, 1)] for e in range(NU)]
    steps[-1] = steps[-1][2:]
    after = {step: [] for unit in steps for step in unit}
    first = []
    if proj:
        first = [("P", 0, 0)]
        for i, step in enumerate(steps[0][:3]):
            after[step] += [("P", 0, i + 1)]
        after[steps[0][0]] += [("WS", 0)]
        after[steps[1][1]] += [("HI", 0)]
        after[steps[2][0]] += [("LO", 0)]
        after[steps[2][0]] += [("WL", 0)]
        after[steps[5][0]] += [("RS", 0)]
        after[steps[10][1]] += [("P", 1, 0)]
        after[steps[10][2]] += [("P", 1, 1)]
        after[steps[10][3]] += [("P", 1, 2), ("P", 1, 3)]
    if full_s:
        window = [step for unit in steps[1:10] for step in unit]
        total, done, k = sum(map(columns, window)), 0, 0
        for step in window:
            done += columns(step)
            while k < len(USES) and k * total < done * len(USES) - total // 2:
                after[step] += [("S", k)]
                k += 1
        assert k == len(USES)
        after[steps[10][1]] += [("MT", 0)]
    after[steps[10][1]] += [("NORM", 0)]
    order = [("ST", 0, 0), ("ST", 0, 1)] + first
    for unit in steps:
        for step in unit:
            order += [step] + after[step]
    if proj:
        order += [("HI", 1), ("LO", 1), ("RK", 0), ("RS", 1)]
    return order + [("NORM", 1)]


def prologue():
    order = []
    for p in range(6):
        for c in range(2):
            for i in range(PIECES):
                order += [("P", p, c, i)]
        if p in VALUES:
            order += [("VT", p, 0), ("VT", p, 1)]
    k = 0
    out = []
    for step in order:
        out.append(step)
        if step[0] == "P" and (step[1] == VALUES[1] or step[1:3] == (5, 0)):
            n = 4 if step[3] % 2 == 0 or step[1:4] in ((4, 0, 1), (4, 0, 3)) else 3
            for _ in range(min(n, len(USES) - k)):
                out.append(("S", k))
                k += 1
            if k == len(USES):
                out.append(("MT", 0))
                k += 1
    assert k == len(USES) + 1
    return out


VALUES = (3, 4)
LO_ORDER = (0, 1, 2, 5)


def bank_plan(order, spare=()):
    last, plan, n, held = {}, {}, 0, None
    for step in order:
        what = step[0]
        if what == "P" and step[-1] == 0:
            held = spare[len([k for k in plan if k[0] == "P"]) % len(spare)] if spare else \
                min((0, 1), key=lambda x: last.get(x, -1))
            plan[step[:-1]] = [None, held, last.get(held, -1)]
        if what == "P" and step[-1] == PIECES - 1:
            plan[step[:-1]][0] = n
            last[held], held = n, None
            n += 1
        if what in ("S", "MT", "VT"):
            bank = min((x for x in (0, 1) if x != held), key=lambda x: last.get(x, -1))
            plan[step] = [n, bank, last.get(bank, -1)]
            last[bank] = n
            n += 1
    return plan, n


def attention(nc, sem, layer, x_in, wqkv, cos_in, sin_in, swap, oT_d):
    kT_d = nc.dram_tensor(f"kT_{layer}", (2, B, NG * HD, S), F32, kind="Internal").ap()
    m_d = nc.dram_tensor(f"rowmax_{layer}", (2, GH * ST_, P), F32, kind="Internal").ap()
    scale = 1.0 / float(np.sqrt(np.float32(HD)))

    s = {n: sem(f"a{layer}_{n}") for n in (
        "const", "table", "xl0", "xl1", "xl2", "xl3", "xl4", "xl5", "stats", "pow", "z_ready", "zT_ready", "zT_hi", "zT_evac",
        "wl0", "wl1", "w_hi", "w_ready", "sh_ready", "sh_free", "roped", "q_hi", "q_lo", "v_ready",
        "k_out", "qs00", "qs01", "qs10", "qs11", "ks0", "ks1", "mx_ready", "mT_ready", "m_out", "mr0", "mr1", "st_ready",
        "exp_done", "mask_done", "pv_done", "acc_copied", "norm_done", "vg_ready", "os0", "os1",
        "pool_turn", "sp_turn", "pe_turn")}
    x_loaded, w_loaded = [s[f"xl{i}"] for i in range(NX_BUF)], (s["wl0"], s["wl1"])
    max_row, o_stored = (s["mr0"], s["mr1"]), (s["os0"], s["os1"])
    stacked, k_stacked = [[s[f"qs{i}{c}"] for c in range(2)] for i in range(2)], (s["ks0"], s["ks1"])
    QS, KS = 3 * GH * 16, 3 * 16
    ZT0, W0, SH0, R0, E0, PV0, AC0, N0, ST0, DMA0 = 4, 2, 1, 4, 2, 2, 2, 1, 2, 16

    pro, body, body6, body7 = prologue(), iteration(), iteration(proj=False), iteration(False, False)
    plan_pro, U_PRO = bank_plan(pro, spare=(2, 3, 4, 5))
    plan = {id(order): bank_plan(order)[0] for order in (body, body6, body7)}
    U_IT, U_IT6 = bank_plan(body)[1], bank_plan(body6)[1]
    U_BATCH = U_PRO + 6 * U_IT + U_IT6
    RB = 20

    with ExitStack() as ctx:
        def sb(name, shape, dt=F32):
            return ctx.enter_context(nc.sbuf_tensor(f"a{layer}_{name}", shape, dt))

        ident = sb("ident", [P, P])
        identb = sb("identb", [P, P], BF16)
        negmask = sb("negmask", [P, P], BF16)
        ones = sb("ones", [P, HD])
        nhalf = sb("nhalf", [P, 1])
        cos = sb("cos", [P, S])
        sin = sb("sin", [P, S])
        xin = [sb(f"xin{i}", [P, D]) for i in range(2)]
        stat = [sb(f"stat{i}", [P, 2, 6]) for i in range(2)]
        mv = [sb(f"mv{i}", [P, 4]) for i in range(2)]
        xT = [sb(f"xT_{n}", [P, KC, S], F32R) for n in ("hi", "lo")]
        wraw = [sb(f"wraw{i}", [P, KC, P]) for i in range(2)]
        w = [[sb(f"w_{n}{i}", [P, KC, P], F32R) for n in ("hi", "lo")] for i in range(2)]
        rot = [sb(f"rot{i}", [P, BANK]) for i in range(2)]
        swp = [sb(f"swp{i}", [P, BANK]) for i in range(2)]
        stg = [sb(f"stg_{n}", [P, S], F32R) for n in ("hi", "lo")]
        qst = [sb(f"qst{i}", [P, GH, S], F32R) for i in range(2)]
        kst = [sb(f"kst{i}", [P, S], F32R) for i in range(2)]
        vT = sb("vT", [P, S])
        vall = sb("vall", [P, ST_, NG * HD])
        vg = [sb(f"vg{i}", [P, ST_, HD]) for i in range(2)]
        prob = [sb(f"prob{i}", [P, GH, BANK]) for i in range(2)]
        mx = sb("mx", [P, 2, GH * ST_])
        mT = sb("mT", [GH * ST_, P])
        pvs = sb("pvs", [P, BANK])
        dens = sb("dens", [P, BANK])
        oT = [sb(f"oT{i}", [P, BANK]) for i in range(2)]
        pst = ctx.enter_context(nc.psum_tensor(f"a{layer}_pst", [P, 2, 2, BANK], F32))
        psh = ctx.enter_context(nc.psum_tensor(f"a{layer}_psh", [P, 2, BANK], F32))
        ppv = ctx.enter_context(nc.psum_tensor(f"a{layer}_ppv", [P, BANK], F32))
        pden = ctx.enter_context(nc.psum_tensor(f"a{layer}_pden", [P, BANK], F32))
        xbuf = [x[:, :] for x in xin] + [p[:, 2 * i:2 * i + 2, :].rearrange("p h n -> p (h n)")
                                         for p in prob for i in range(2)]
        X_LOADS = [len(range(i, ST_, NX_BUF)) for i in range(NX_BUF)]
        mx_hq = [mx[:, i, :].rearrange("p (h q) -> p h q", q=ST_) for i in range(2)]
        block = ctx.enter_context(nc.Block())

        def bank(i):
            return psh[:, i, :] if i < 2 else pst[:, (i - 2) // 2, i % 2, :]

        def over_groups(b, eng, group):
            u0 = b * U_BATCH + U_PRO
            with eng.Fori(0, NG // 2 - 1) as j:
                for par in range(2):
                    group(body, b, j * 2 + par, j, par, u0 + (j * 2 + par) * U_IT)
            group(body6, b, NG - 2, NG // 2 - 1, 0, u0 + 6 * U_IT)
            group(body7, b, NG - 1, NG // 2 - 1, 1, u0 + 6 * U_IT + U_IT6)

        @block.sync
        def _(sp):
            def load_w(n, chunk, par):
                sp.wait_ge(s["w_ready"], n + 1)
                sp.dma_start(wraw[par][:, :, :], wqkv[chunk]).then_inc(w_loaded[par], 16)

            def store_k(b, p):
                sp.wait_ge(s["q_lo"], b * RB + 2 * p + 2)
                for part in range(2):
                    sp.dma_start(kT_d[part, ds(b, 1), p * P:(p + 1) * P, :].rearrange("o p n -> p (o n)"),
                                 stg[part][:, :].bitcast(F32)).then_inc(s["k_out"], 16)

            def stack_queries(par, c):
                cols = slice(c * BANK, (c + 1) * BANK)
                for h in range(GH):
                    for row, part in enumerate((0, 1, 0)):
                        sp.dma_start(qst[par][row * HD:(row + 1) * HD, h, cols].bitcast(F32),
                                     stg[part][h * HD:(h + 1) * HD, cols].bitcast(F32)).then_inc(stacked[par][c], 16)

            def stack_keys(b, g, par):
                for row, part in enumerate((0, 0, 1)):
                    src = kT_d[part, ds(b, 1), ds(g * HD, HD), :].rearrange("o p n -> p (o n)")
                    sp.dma_start(kst[par][row * HD:(row + 1) * HD, :].bitcast(F32), src).then_inc(k_stacked[par], 16)

            def row_max(b, g, par):
                n = b * NG + g
                sp.wait_ge(s["mT_ready"], n + 1)
                sp.dma_start(m_d[par], mT[:, :]).then_inc(s["m_out"], 16)
                sp.wait_ge(s["m_out"], DMA0 + n * 16 + 16)
                sp.dma_start(qst[par][96:97, :, :].rearrange("o h n -> o (h n)").bitcast(F32),
                             m_d[par].rearrange("a (o n) -> o (a n)", o=1)).then_inc(max_row[par], 16)

            def store_o(b, g, qc):
                sp.wait_ge(s["norm_done"], N0 + (b * NG + g) * 2 + qc + 1)
                sp.dma_start(oT_d[ds(g, 1), :, ds(b * ST_ + qc * 4, 4), :].rearrange("o p t n -> p (o t) n"),
                             oT[qc][:, :].rearrange("p (t n) -> p t n", n=P)).then_inc(o_stored[qc], 16)

            def group(order, b, g, gh, par, u):
                n = b * NG + g
                for what, k, *_ in order:
                    if what == "WL":
                        load_w(b * N_WCHUNK + g + 8, g + 8, par)
                    if what == "RS" and k == 0:
                        sp.wait_ge(s["st_ready"], ST0 + (n * NU + CHUNK_END[0]) * 2 + 2)
                        sp.wait_ge(s["q_lo"], b * RB + 4 + (g + 2) * 2 + 1)
                        stack_queries(par, 0)
                    if what == "RK":
                        sp.wait_ge(s["st_ready"], ST0 + n * 2 * NU + 2 * NU)
                        sp.sem_inc(s["sp_turn"], 1)
                        stack_keys(b, g + 2, par)
                    if what == "RS" and k == 1:
                        sp.wait_ge(s["q_lo"], b * RB + 4 + (g + 2) * 2 + 2)
                        stack_queries(par, 1)
                    if what == "MT":
                        row_max(b, g + 1, 1 - par)
                    if what == "NORM":
                        store_o(b, g, k)

            for credited in (s["m_out"], *o_stored):
                sp.sem_inc(credited, DMA0)
            sp.dma_start(cos[:, :], cos_in).then_inc(s["table"], 16)
            sp.dma_start(sin[:, :], sin_in).then_inc(s["table"], 16)
            load_w(0, 0, 0)
            load_w(1, 1, 1)
            with sp.Fori(0, B) as b:
                for t in range(ST_):
                    if t == 2:
                        sp.wait_ge(s["pv_done"], PV0 + b * NG * NU)
                    if t >= NX_BUF:
                        sp.wait_ge(s["zT_ready"], ZT0 + (b * ST_ + t - NX_BUF) * 2 + 2)
                    i = t % NX_BUF
                    sp.dma_start(xbuf[i], x_in[ds((b * ST_ + t) * P, P), :]).then_inc(x_loaded[i], 16)
                for p in range(2, 8):
                    load_w(b * N_WCHUNK + p, p, p % 2)
                    if p in (2, 3):
                        store_k(b, p - 2)
                    if p in (4, 7):
                        g = p // 7
                        sp.wait_ge(s["k_out"], b * 64 + 64)
                        sp.sem_inc(s["sp_turn"], 1)
                        sp.wait_ge(s["st_ready"], ST0 + b * NG * 2 * NU)
                        sp.sem_inc(s["sp_turn"], 1)
                        if g == 1:
                            row_max(b, 0, 0)
                        stack_keys(b, g, g)
                        for c in range(2):
                            sp.wait_ge(s["q_lo"], b * RB + 4 + 2 * g + c + 1)
                            stack_queries(g, c)
                over_groups(b, sp, group)
            for qc in range(NQC):
                sp.wait_ge(o_stored[qc], DMA0 + 16 * B * NG)
            for par in range(2):
                sp.wait_ge(w_loaded[par], 16 * (B * N_WCHUNK // 2 + 1))

        @block.gpsimd
        def _(pool):
            def copy_v(b, g, par):
                pool.sem_inc(s["pool_turn"], 1)
                pool.tensor_copy(vg[par][:, :, :], vall[:, :, ds(g * HD, HD)]).then_inc(s["vg_ready"], 1)

            def group(order, b, g, gh, par, u):
                n = b * NG + g
                for what, e, *half in order:
                    if what == "ST" and half == [1] and e in DIAGONAL:
                        off = unit_offset(e)
                        pool.wait_ge(s["exp_done"], E0 + (n * NU + e) * 2 + 2)
                        pool.sem_inc(s["pool_turn"], 1)
                        blk = prob[e % 2][:, :, off:off + P]
                        pool.affine_select(out=blk, in_=blk, compare_op=ALU.is_ge, fill=0.0, base=0,
                                           pattern=[[0, GH], [1, P]], channel_multiplier=-1)\
                            .then_inc(s["mask_done"], 1)
                if order is body:
                    pool.wait_ge(s["pv_done"], PV0 + n * NU + NU)
                    copy_v(b, g + 2, par)

            pool.memset(ident[:, :], 0.0)
            pool.memset(negmask[:, :], 0.0)
            pool.memset(ones[:, :], 1.0)
            pool.memset(nhalf[:, :], -0.5)
            pool.drain()
            for i in range(2):
                pool.memset(kst[i][96:97, :].bitcast(F32), -1.0)
            pool.drain()
            pool.affine_select(out=ident[:, :], in_=ident[:, :], compare_op=ALU.not_equal, fill=1.0, base=0,
                               pattern=[[-1, P]], channel_multiplier=1)
            pool.affine_select(out=negmask[:, :], in_=negmask[:, :], compare_op=ALU.is_ge, fill=MASKED, base=0,
                               pattern=[[-1, P]], channel_multiplier=1)
            pool.drain()
            pool.tensor_copy(identb[:, :], ident[:, :])
            pool.drain().then_inc(s["const"], 1)
            with pool.Fori(0, B) as b:
                for t in range(ST_):
                    pool.wait_ge(s["stats"], b * ST_ + t + 1)
                    pool.tensor_tensor(mv[t % 2][:, 3:4], mv[t % 2][:, 2:3], nhalf[:, :], ALU.pow)\
                        .then_inc(s["pow"], 1)
                pool.wait_ge(s["v_ready"], b * 4 + 4)
                copy_v(b, 0, 0)
                copy_v(b, 1, 1)
                over_groups(b, pool, group)

        @block.scalar
        def _(act):
            def w_hi(n, half_n, par):
                act.wait_ge(w_loaded[par], half_n * 16 + 16)
                act.wait_ge(s["roped"], 2 * n + 2)
                act.activation(w[par][0][:, :, :], wraw[par][:, :, :], ACT.Copy).then_inc(s["w_hi"], 1)

            def part_hi(n, c):
                act.wait_ge(s["roped"], R0 + 2 * n + c + 1)
                act.activation(stg[0][:, c * BANK:(c + 1) * BANK], rot[c][:, :], ACT.Copy).then_inc(s["q_hi"], 1)

            def group(order, b, g, gh, par, u):
                n = b * NG + g
                for what, k, *part in order:
                    if what == "ST":
                        off = unit_offset(k)
                        half = part[0]
                        if half == 0:
                            act.wait_ge(s["pv_done"], n * NU + k + 1)
                        act.wait_ge(s["st_ready"], ST0 + (n * NU + k) * 2 + half + 1)
                        act.activation(prob[k % 2][:, 2 * half:2 * half + 2, off:], pst[:, half, :, off:],
                                       ACT.Exp, scale=scale).then_inc(s["exp_done"], 1)
                    if what == "PV" and part == [1] and k in CHUNK_END:
                        q = n * 2 + CHUNK_END.index(k)
                        act.wait_ge(s["pv_done"], PV0 + n * NU + k + 1)
                        act.wait_ge(s["norm_done"], q + 1)
                        act.copy(pvs[:, :], ppv[:, :]).then_inc(s["acc_copied"], 1)
                        act.copy(dens[:, :], pden[:, :]).then_inc(s["acc_copied"], 1)
                    if what == "WS":
                        w_hi(b * N_WCHUNK + g + 7, b * 6 + gh + 3 + par, 1 - par)
                    if what == "HI":
                        act.wait_ge(stacked[1 - par][k], (b * 4 + gh + par + 1) * QS)
                        part_hi(b * N_WCHUNK + g + 6, k)

            act.drain().then_inc(s["exp_done"], E0)
            act.drain().then_inc(s["acc_copied"], AC0)
            w_hi(0, 0, 0)
            with act.Fori(0, B) as b:
                for t in range(ST_):
                    for half in range(2):
                        n = 2 * t + half
                        act.wait_ge(s["zT_ready"], ZT0 + b * 2 * ST_ + n + 1)
                        act.activation(xT[0][:, 4 * half:4 * half + 4, t * P:(t + 1) * P],
                                       pst[:, n // 2 % 2, n % 2, :].rearrange("p (k n) -> p k n", n=P),
                                       ACT.Copy).then_inc(s["zT_hi"], 1)
                for p in range(6):
                    w_hi(b * N_WCHUNK + p + 1, b * 6 + (p + 1) // 2, (p + 1) % 2)
                    if p == 1:
                        act.wait_ge(s["k_out"], b * 64 + 32)
                    if p == 2:
                        act.wait_ge(s["k_out"], b * 64 + 64)
                    if p == 5:
                        for c in range(2):
                            act.wait_ge(stacked[0][c], (b * 4 + 1) * QS)
                    if p not in VALUES:
                        for c in range(2):
                            part_hi(b * N_WCHUNK + p, c)
                over_groups(b, act, group)

        @block.vector
        def _(dve):
            def w_lo(n, par):
                dve.wait_ge(s["w_hi"], n + 1)
                dve.tensor_tensor(w[par][1][:, :, :], wraw[par][:, :, :], w[par][0][:, :, :].bitcast(F32),
                                  ALU.subtract).then_inc(s["w_ready"], 1)

            def rotate(u, at, c):
                dve.drain()
                dve.wait_ge(s["sh_ready"], u + 1)
                dve.tensor_tensor(rot[c][:, :], bank(at), cos[:, c * BANK:(c + 1) * BANK], ALU.mult)
                dve.stream_shuffle(swp[c][:, :], bank(at), swap).then_inc(s["sh_free"], 1)
                dve.drain()
                dve.tensor_tensor(swp[c][:, :], swp[c][:, :], sin[:, c * BANK:(c + 1) * BANK], ALU.mult)
                dve.drain()
                dve.tensor_tensor(rot[c][:, :], rot[c][:, :], swp[c][:, :], ALU.add).then_inc(s["roped"], 1)

            def part_lo(r, c):
                cols = slice(c * BANK, (c + 1) * BANK)
                dve.wait_ge(s["q_hi"], r + 1)
                dve.tensor_tensor(stg[1][:, cols], rot[c][:, :], stg[0][:, cols].bitcast(F32), ALU.subtract)\
                    .then_inc(s["q_lo"], 1)

            def maximum(u, at, k):
                qt, kc, n, heads, _ = USES[k]
                m = len(heads)
                dve.wait_ge(s["sh_ready"], u + 1)
                dve.tensor_reduce(mx_hq[kc][:, heads[0]:heads[0] + m, qt],
                                  psh[:, at, 0:m * n].rearrange("p (m n) -> p m n", n=n), AX.X, ALU.max)\
                    .then_inc(s["sh_free"], 1)

            def max_rows(u, at):
                dve.tensor_tensor(mx_hq[0][:, :, 4:], mx_hq[0][:, :, 4:], mx_hq[1][:, :, 4:], ALU.max)\
                    .then_inc(s["mx_ready"], 1)
                dve.wait_ge(s["sh_ready"], u + 1)
                dve.tensor_copy(mT[:, :], psh[0:GH * ST_, at, 0:P]).then_inc(s["sh_free"], 1)
                dve.drain().then_inc(s["mT_ready"], 1)

            def group(order, b, g, gh, par, u):
                n = b * NG + g
                for step in order:
                    what, k = step[:2]
                    if what == "P" and step[-1] == PIECES - 1:
                        i, at, _ = plan[id(order)][step[:-1]]
                        rotate(u + i, at, k)
                    if what == "S":
                        i, at, _ = plan[id(order)][step]
                        maximum(u + i, at, k)
                    if what == "MT":
                        i, at, _ = plan[id(order)][step]
                        dve.drain()
                        dve.wait_ge(s["m_out"], DMA0 + (n + 1) * 16)
                        max_rows(u + i, at)
                    if what == "LO":
                        part_lo(b * RB + 4 + (g + 2) * 2 + k, k)
                    if what == "WS":
                        w_lo(b * N_WCHUNK + g + 7, 1 - par)
                    if what == "NORM":
                        q = n * 2 + k
                        dve.drain()
                        dve.wait_ge(s["acc_copied"], AC0 + 2 * q + 2)
                        dve.reciprocal(dens[:, :], dens[:, :])
                        dve.drain()
                        dve.wait_ge(o_stored[k], DMA0 + n * 16)
                        dve.tensor_tensor(oT[k][:, :], pvs[:, :], dens[:, :], ALU.mult).then_inc(s["norm_done"], 1)

            dve.drain().then_inc(s["zT_evac"], ZT0)
            dve.drain().then_inc(s["w_ready"], W0)
            dve.drain().then_inc(s["sh_free"], SH0)
            dve.drain().then_inc(s["roped"], R0)
            dve.drain().then_inc(s["norm_done"], N0)
            w_lo(0, 0)
            dve.wait_ge(s["table"], 32)
            with dve.Fori(0, B) as b:
                for t in range(ST_ + 2):
                    if t < ST_:
                        dve.wait_ge(x_loaded[t % NX_BUF], (b * X_LOADS[t % NX_BUF] + t // NX_BUF) * 16 + 16)
                        for i in range(2):
                            dve.bn_stats(stat[t % 2][:, i, :], xbuf[t % NX_BUF][:, i * BANK:(i + 1) * BANK])
                        dve.drain()
                        dve.bn_aggr(mv[t % 2][:, 0:2], stat[t % 2][:, :, :])
                        dve.drain()
                        dve.tensor_scalar(mv[t % 2][:, 2:3], mv[t % 2][:, 1:2], LN_EPS, None, ALU.add)\
                            .then_inc(s["stats"], 1)
                    if 1 <= t <= ST_:
                        i, tile = (t - 1) % 2, xbuf[(t - 1) % NX_BUF]
                        dve.wait_ge(s["pow"], b * ST_ + t)
                        dve.tensor_scalar(tile, tile, mv[i][:, 0:1], mv[i][:, 3:4],
                                          ALU.subtract, ALU.mult).then_inc(s["z_ready"], 1)
                    if t >= 2:
                        for half in range(2):
                            n = 2 * (t - 2) + half
                            dve.wait_ge(s["zT_hi"], b * 2 * ST_ + n + 1)
                            at = (slice(None), slice(4 * half, 4 * half + 4), slice((t - 2) * P, (t - 1) * P))
                            dve.tensor_tensor(xT[1][at], pst[:, n // 2 % 2, n % 2, :].rearrange("p (k n) -> p k n", n=P),
                                              xT[0][at].bitcast(F32), ALU.subtract).then_inc(s["zT_evac"], 1)
                for step in pro:
                    what, p = step[:2]
                    if what == "P":
                        c, piece = step[2:]
                        if piece < PIECES - 1:
                            continue
                        i, at, _ = plan_pro[step[:-1]]
                        u = b * U_BATCH + i
                        if c == 0:
                            w_lo(b * N_WCHUNK + p + 1, (p + 1) % 2)
                        if p in VALUES:
                            dve.wait_ge(s["sh_ready"], u + 1)
                            dve.tensor_copy(vT[:, c * BANK:(c + 1) * BANK], bank(at)).then_inc(s["sh_free"], 1)
                            dve.drain().then_inc(s["roped"], 1)
                        else:
                            rotate(u, at, c)
                        if c == 1 and p not in VALUES:
                            for h in range(2):
                                part_lo(b * RB + 2 * LO_ORDER.index(p) + h, h)
                    if what == "VT":
                        i, at, _ = plan_pro[step]
                        c = step[2]
                        dve.wait_ge(s["sh_ready"], b * U_BATCH + i + 1)
                        dve.tensor_copy(vall[:, 4 * c:4 * c + 4, (p - VALUES[0]) * P:(p - VALUES[0] + 1) * P],
                                        bank(at).rearrange("p (k n) -> p k n", n=P)).then_inc(s["sh_free"], 1)
                        dve.drain().then_inc(s["v_ready"], 1)
                    if what == "S":
                        i, at, _ = plan_pro[step]
                        maximum(b * U_BATCH + i, at, p)
                    if what == "MT":
                        i, at, _ = plan_pro[step]
                        dve.drain()
                        dve.wait_ge(s["m_out"], DMA0 + b * NG * 16)
                        max_rows(b * U_BATCH + i, at)
                over_groups(b, dve, group)

        @block.tensor
        def _(pe):
            def project(n, u, where, par, c, piece):
                _, at, prev = where
                if piece == 0:
                    pe.wait_ge(s["w_ready"], W0 + n + 1)
                    pe.wait_ge(s["sh_free"], SH0 + u + prev + 1)
                passes = [(k, a, x) for k in range(KC) for a, x in ((0, 0), (0, 1), (1, 0))]
                step = len(passes) // PIECES
                for i in range(piece * step, (piece + 1) * step):
                    k, a, x = passes[i]
                    mm = pe.matmul(bank(at), w[par][a][:, k, :], xT[x][:, k, c * BANK:(c + 1) * BANK],
                                   start=(i == 0), stop=(i == len(passes) - 1))
                if piece == PIECES - 1:
                    mm.then_inc(s["sh_ready"], 1)

            def row_scores(u, where, par, k):
                _, at, prev = where
                qt, kc, n, heads, last = USES[k]
                pe.wait_ge(s["sh_free"], SH0 + u + prev + 1)
                for i, h in enumerate(heads):
                    mm = pe.matmul(psh[:, at, i * n:(i + 1) * n], qst[par][0:96, h, qt * P:(qt + 1) * P],
                                   kst[par][0:96, kc * BANK:kc * BANK + n], start=True, stop=not last,
                                   skip_group_check=True)
                    if last:
                        mm = pe.matmul(psh[:, at, (i + 1) * n - P:(i + 1) * n], identb[:, :], negmask[:, :],
                                       start=False, stop=True, skip_group_check=True)
                mm.then_inc(s["sh_ready"], 1)

            def transpose_max(n, u, where):
                _, at, prev = where
                pe.wait_ge(s["mx_ready"], n + 1)
                pe.wait_ge(s["sh_free"], SH0 + u + prev + 1)
                pe.transpose(psh[0:GH * ST_, at, 0:P], mx[:, 0, :], ident[:, :]).then_inc(s["sh_ready"], 1)

            def group(order, b, g, gh, par, u):
                n = b * NG + g
                for step in order:
                    what, k = step[:2]
                    if what == "P":
                        project(b * N_WCHUNK + g + 6, u, plan[id(order)][step[:-1]], par, k, step[-1])
                    if what == "S":
                        if k == 0:
                            pe.wait_ge(k_stacked[1 - par], (b * 4 + gh + par + 1) * KS)
                        if k in (0, SECOND_HALF):
                            pe.wait_ge(stacked[1 - par][int(k > 0)], (b * 4 + gh + par + 1) * QS)
                        row_scores(u, plan[id(order)][step], 1 - par, k)
                    if what == "MT":
                        transpose_max(n + 1, u, plan[id(order)][step])
                    if what == "ST":
                        qc, ki = UNITS[k]
                        half = step[2]
                        off = min(unit_offset(k), BANK // 2)
                        if k == 0 and half == 0:
                            pe.wait_ge(max_row[par], (b * 4 + gh + 1) * 16)
                        pe.wait_ge(s["exp_done"], (n * NU + k) * 2 + half + 1)
                        for hh in range(2):
                            mm = pe.matmul(pst[:, half, hh, off:], kst[par][0:97, ki * P:(ki + 1) * P],
                                           qst[par][0:97, 2 * half + hh, qc * BANK + off:(qc + 1) * BANK],
                                           start=True, stop=True)
                        mm.then_inc(s["st_ready"], 1)
                    if what == "PV":
                        qc, ki = UNITS[k]
                        off = unit_offset(k)
                        part = step[2]
                        if part == 0:
                            if k == 0:
                                pe.wait_ge(s["vg_ready"], n + 1)
                            if k in DIAGONAL:
                                pe.wait_ge(s["mask_done"], n * len(DIAGONAL) + DIAGONAL.index(k) + 1)
                            else:
                                pe.wait_ge(s["exp_done"], E0 + (n * NU + k) * 2 + 2)
                            if ki == 0:
                                pe.wait_ge(s["acc_copied"], (n * 2 + qc) * 2 + 2)
                        acc, lhs = ((ppv, vg[par][:, ki, :]), (pden, ones[:, :]))[part]
                        for h in range(GH):
                            mm = pe.matmul(acc[h * HD:(h + 1) * HD, off:], lhs, prob[k % 2][:, h, off:],
                                           start=(ki == 0), stop=(ki == 4 * qc + 3), skip_group_check=True)
                        if part == 1:
                            mm.then_inc(s["pv_done"], 1)

            pe.wait_ge(s["const"], 1)
            pe.sem_inc(s["zT_ready"], ZT0)
            pe.sem_inc(s["pv_done"], PV0)
            pe.sem_inc(s["st_ready"], ST0)
            with pe.Fori(0, B) as b:
                pe.wait_ge(s["exp_done"], E0 + b * NG * NU * 2)
                for t in range(ST_):
                    pe.wait_ge(s["z_ready"], b * ST_ + t + 1)
                    for half in range(2):
                        n = 2 * t + half
                        pe.wait_ge(s["zT_evac"], b * 2 * ST_ + n + 1)
                        for k in range(4):
                            tr = pe.transpose(pst[:, n // 2 % 2, n % 2, k * P:(k + 1) * P],
                                              xbuf[t % NX_BUF][:, (4 * half + k) * P:(4 * half + k + 1) * P], ident[:, :])
                        tr.then_inc(s["zT_ready"], 1)
                pe.wait_ge(s["zT_evac"], ZT0 + (b + 1) * 2 * ST_)
                for step in pro:
                    what, p = step[:2]
                    u = b * U_BATCH
                    if what == "P":
                        project(b * N_WCHUNK + p, u, plan_pro[step[:-1]], p % 2, step[2], step[3])
                    if what == "VT":
                        _, at, prev = plan_pro[step]
                        c = step[2]
                        if c == 0:
                            pe.wait_ge(s["roped"], R0 + (b * N_WCHUNK + p) * 2 + 2)
                        pe.wait_ge(s["sh_free"], SH0 + u + prev + 1)
                        for k in range(4):
                            tr = pe.transpose(psh[:, at, k * P:(k + 1) * P],
                                              vT[:, (4 * c + k) * P:(4 * c + k + 1) * P], ident[:, :])
                        tr.then_inc(s["sh_ready"], 1)
                    if what == "S":
                        if p == 0:
                            pe.wait_ge(k_stacked[0], (b * 4 + 1) * KS)
                        if p in (0, SECOND_HALF):
                            pe.wait_ge(stacked[0][int(p > 0)], (b * 4 + 1) * QS)
                        row_scores(u, plan_pro[step], 0, p)
                    if what == "MT":
                        transpose_max(b * NG, u, plan_pro[step])
                pe.wait_ge(s["sh_free"], SH0 + b * U_BATCH + U_PRO)
                pe.sem_inc(s["pe_turn"], 1)
                over_groups(b, pe, group)


def output_projection(nc, sem, layer, oT_d, wo, x_in, x_out):
    s = {n: sem(f"o{layer}_{n}") for n in (
        "wl0", "wl1", "w_hi", "w_lo", "ol0", "ol1", "o_hi", "o_lo", "x0", "x1", "mm", "sum", "st0", "st1")}
    w_loaded, o_loaded, x_loaded, stored = ((s["wl0"], s["wl1"]), (s["ol0"], s["ol1"]), (s["x0"], s["x1"]),
                                            (s["st0"], s["st1"]))
    M0, L0, S0, DMA0 = 8, 2, 4, 16
    TURNS = NT // 4
    with ExitStack() as ctx:
        def sb(name, shape, dt=F32):
            return ctx.enter_context(nc.sbuf_tensor(f"o{layer}_{name}", shape, dt))

        wraw = [sb(f"wraw{i}", [P, D]) for i in range(2)]
        w = [sb(f"w_{n}", [P, KC, D], F32R) for n in ("hi", "lo")]
        oraw = [sb(f"oraw{i}", [P, NG, 2 * P]) for i in range(2)]
        o = [[sb(f"o_{n}{i}", [P, NG, 2 * P], F32R) for n in ("hi", "lo")] for i in range(2)]
        xres = [sb(f"xres{i}", [P, D]) for i in range(2)]
        pout = ctx.enter_context(nc.psum_tensor(f"o{layer}_pout", [P, 2, 2, BANK], F32))
        block = ctx.enter_context(nc.Block())

        @block.sync
        def _(sp):
            def load_w(k):
                if k >= 2:
                    sp.wait_ge(s["w_lo"], k - 1)
                sp.dma_start(wraw[k % 2][:, :], wo[k * P:(k + 1) * P, :]).then_inc(w_loaded[k % 2], 16)

            def load_o(i, par):
                sp.wait_ge(s["o_lo"], i + 1)
                sp.dma_start(oraw[par][:, :, :].rearrange("p g (t n) -> p g t n", n=P),
                             oT_d[:, :, ds(i * 2, 2), :].rearrange("g p t n -> p g t n")).then_inc(o_loaded[par], 16)

            for i in range(2):
                sp.sem_inc(stored[i], DMA0)
            load_w(0)
            load_o(0, 0)
            for k in range(1, KC):
                load_w(k)
            load_o(1, 1)

            def turn(j, more):
                for q in range(4):
                    sp.wait_ge(stored[q % 2], DMA0 + (j * 2 + q // 2) * 16)
                    sp.dma_start(xres[q % 2][:, :], x_in[ds((j * 4 + q) * P, P), :]).then_inc(x_loaded[q % 2], 16)
                    if q % 2 == 1:
                        sp.wait_ge(s["sum"], S0 + (j * 4 + q) * 2)
                        sp.dma_start(x_out[ds((j * 4 + q - 1) * P, P), :], xres[0][:, :]).then_inc(stored[0], 16)
                        if more:
                            load_o(j * 2 + 2 + q // 2, q // 2)
                        sp.wait_ge(s["sum"], S0 + (j * 4 + q) * 2 + 2)
                        sp.dma_start(x_out[ds((j * 4 + q) * P, P), :], xres[1][:, :]).then_inc(stored[1], 16)

            with sp.Fori(0, TURNS - 1) as j:
                turn(j, True)
            turn(TURNS - 1, False)
            for i in range(2):
                sp.wait_ge(stored[i], DMA0 + 16 * NT // 2)

        @block.scalar
        def _(act):
            def o_hi(i, i_half, par):
                act.wait_ge(o_loaded[par], i_half * 16 + 16)
                act.wait_ge(s["mm"], M0 - 4 + i * 4)
                act.activation(o[par][0][:, :, :], oraw[par][:, :, :], ACT.Copy).then_inc(s["o_hi"], 1)

            for k in range(KC):
                act.wait_ge(w_loaded[k % 2], (k // 2 + 1) * 16)
                act.activation(w[0][:, k, :], wraw[k % 2][:, :], ACT.Copy).then_inc(s["w_hi"], 1)
                if k == 0:
                    o_hi(0, 0, 0)
            with act.Fori(0, TURNS - 1) as j:
                o_hi(j * 2 + 1, j, 1)
                o_hi(j * 2 + 2, j + 1, 0)
            o_hi(NT // 2 - 1, TURNS - 1, 1)

        @block.vector
        def _(dve):
            def o_lo(i, par):
                dve.wait_ge(s["o_hi"], i + 1)
                dve.tensor_tensor(o[par][1][:, :, :], oraw[par][:, :, :], o[par][0][:, :, :].bitcast(F32),
                                  ALU.subtract).then_inc(s["o_lo"], 1)

            dve.drain().then_inc(s["o_lo"], L0)
            dve.drain().then_inc(s["sum"], S0)
            for k in range(KC):
                dve.wait_ge(s["w_hi"], k + 1)
                dve.tensor_tensor(w[1][:, k, :], wraw[k % 2][:, :], w[0][:, k, :].bitcast(F32), ALU.subtract)\
                    .then_inc(s["w_lo"], 1)
                if k == 0:
                    o_lo(0, 0)

            def turn(j, more):
                for q in range(4):
                    if q == 0:
                        o_lo(j * 2 + 1, 1)
                    if q == 2 and more:
                        o_lo(j * 2 + 2, 0)
                    dve.wait_ge(x_loaded[q % 2], (j * 2 + q // 2) * 16 + 16)
                    for half in range(2):
                        cols = slice(half * BANK, (half + 1) * BANK)
                        dve.wait_ge(s["mm"], M0 + (j * 4 + q) * 2 + half + 1)
                        dve.tensor_tensor(xres[q % 2][:, cols], xres[q % 2][:, cols], pout[:, q % 2, half, :],
                                          ALU.add).then_inc(s["sum"], 1)

            with dve.Fori(0, TURNS - 1) as j:
                turn(j, True)
            turn(TURNS - 1, False)

        @block.tensor
        def _(pe):
            pe.sem_inc(s["mm"], M0)
            with pe.Fori(0, TURNS) as j:
                for q in range(4):
                    par = q // 2
                    if q == 0:
                        pe.wait_ge(s["w_lo"], KC)
                    if q % 2 == 0:
                        pe.wait_ge(s["o_lo"], L0 + j * 2 + par + 1)
                    for half in range(2):
                        pe.wait_ge(s["sum"], (j * 4 + q) * 2 + half + 1)
                        passes = [(k, a, x) for k in range(KC) for a, x in ((0, 0), (0, 1), (1, 0))]
                        for i, (k, a, x) in enumerate(passes):
                            mm = pe.matmul(pout[:, q % 2, half, :], o[par][a][:, k, (q % 2) * P:(q % 2 + 1) * P],
                                           w[x][:, k, half * BANK:(half + 1) * BANK],
                                           start=(i == 0), stop=(i == len(passes) - 1))
                        mm.then_inc(s["mm"], 1)


NS = 4
C = D // NS
NL = NS * NS + 2 * NS
SINKHORN_ITERS = 50
TAU = 0.1


def hyper_connection(nc, sem, x_in, w24, base24, gate, w_branch, x_out):
    s = {n: sem(f"h_{n}") for n in (
        "const", "small", "x0", "x1", "stat_in", "rstd", "rms_in", "rms", "z", "zT_ready", "zT", "logit",
        "read", "gate", "e_in", "e_out", "z2", "pre", "preT_ready", "preT", "y", "mixed", "stored")}
    x_loaded = (s["x0"], s["x1"])
    ZR0, ZT0, LG0, RD0, MX0, PR0, PT0, Y0, DMA0 = 4, 4, 2, 2, 2, 2, 1, 1, 16
    with ExitStack() as ctx:
        def sb(name, shape, dt=F32):
            return ctx.enter_context(nc.sbuf_tensor(f"h_{name}", shape, dt))

        ident = sb("ident", [P, P])
        x = sb("x", [P, NT, D])
        z = [sb(f"z{i}", [P, D]) for i in range(2)]
        stat = sb("stat", [P, 2, 6])
        aggr = sb("aggr", [P, 2])
        mv = sb("mv", [P, NT, 2])
        nhalf = sb("nhalf", [P, NT])
        nmr = sb("nmr", [P, NT])
        rstd, var_e, rms, rms_e = (sb(n, [P, NT]) for n in ("rstd", "var_e", "rms", "rms_e"))
        zT = [sb(f"zT{i}", [P, KC, P]) for i in range(2)]
        w24_sb = sb("w24", [P, KC, NL])
        base = sb("base", [P, NL])
        wb = sb("wb", [P, C // P, C])
        lg = sb("lg", [P, NT, NL])
        m = sb("m", [P, NT, NS * NS])
        e = sb("e", [P, NT, NS * NS])
        pp = sb("pp", [P, NT, 2, NS])
        r64 = sb("r64", [P, NT, NS])
        sums = sb("sums", [P, NT, 2])
        g = sb("g", [P, 4])
        pre = [sb(f"pre{i}", [P, C]) for i in range(2)]
        preT = sb("preT", [P, C // P, P])
        pz = ctx.enter_context(nc.psum_tensor("h_pz", [P, 2, 2, BANK], F32))
        plg = ctx.enter_context(nc.psum_tensor("h_plg", [P, 2, BANK], F32))
        ppre = ctx.enter_context(nc.psum_tensor("h_ppre", [P, BANK], F32))
        py = plg
        block = ctx.enter_context(nc.Block())

        def lines(buf, axis):
            return buf[:, :, :].rearrange("p t (i j) -> p t i j" if axis == "row" else "p t (i j) -> p t j i", j=NS)

        def spread(v, n=NS):
            return v.unsqueeze(3).broadcast_to([P, NT, v.shape[2], n])

        def tile(buf, t):
            return buf[:, ds(t, 1), :].rearrange("p o n -> p (o n)")

        @block.sync
        def _(sp):
            for dst, src in ((w24_sb[:, :, :], w24), (base[:, :], base24), (g[:, 0:1], gate),
                             (wb[:, :, :], w_branch.rearrange("(c p) n -> p c n", p=P))):
                sp.dma_start(dst, src).then_inc(s["small"], 16)
            for i in range(2):
                sp.sem_inc(x_loaded[i], DMA0)
            with sp.Fori(0, NT // 2) as j:
                for i in range(2):
                    sp.wait_ge(x_loaded[i], DMA0 + j * 16)
                    sp.dma_start(x[:, ds(j * 2 + i, 1), :].rearrange("p o n -> p (o n)"),
                                 x_in[ds((j * 2 + i) * P, P), :]).then_inc(x_loaded[i], 16)
            with sp.Fori(0, NT) as t:
                sp.wait_ge(s["mixed"], MX0 + t + 1)
                sp.dma_start(x_out[ds(t * P, P), :],
                             x[:, ds(t, 1), :].rearrange("p o n -> p (o n)")).then_inc(s["stored"], 16)
            sp.wait_ge(s["stored"], 16 * NT)

        @block.gpsimd
        def _(pool):
            pool.memset(ident[:, :], 0.0)
            pool.memset(nhalf[:, :], -0.5)
            pool.drain()
            pool.affine_select(out=ident[:, :], in_=ident[:, :], compare_op=ALU.not_equal, fill=1.0, base=0,
                               pattern=[[-1, P]], channel_multiplier=1).then_inc(s["const"], 1)
            pool.wait_ge(s["stat_in"], 1)
            pool.tensor_tensor(rstd[:, :], var_e[:, :], nhalf[:, :], ALU.pow).then_inc(s["rstd"], 1)
            pool.wait_ge(s["rms_in"], 1)
            pool.tensor_tensor(rms[:, :], rms_e[:, :], nhalf[:, :], ALU.pow).then_inc(s["rms"], 1)

        @block.scalar
        def _(act):
            act.wait_ge(s["small"], 64)
            act.activation(g[:, 1:2], g[:, 0:1], ACT.Exp, scale=-1.0).then_inc(s["gate"], 1)
            act.drain().then_inc(s["zT"], ZT0)
            act.drain().then_inc(s["preT"], PT0)
            with act.Fori(0, NT // 2) as j:
                for par in range(2):
                    t = j * 2 + par
                    for half in range(2):
                        act.wait_ge(s["logit"], t + 1)
                        act.wait_ge(s["zT_ready"], ZR0 + t * 2 + half + 1)
                        act.activation(zT[par][:, 4 * half:4 * half + 4, :],
                                       pz[:, par, half, :].rearrange("p (k n) -> p k n", n=P), ACT.Copy)\
                            .then_inc(s["zT"], 1)
            act.wait_ge(s["e_in"], 1)
            act.activation(pp[:, :, :, :], pp[:, :, :, :], ACT.Exp).then_inc(s["e_out"], 1)
            act.activation(e[:, :, :], m[:, :, :], ACT.Exp).then_inc(s["e_out"], 1)
            act.wait_ge(s["e_in"], 2)
            act.activation(r64[:, :, :], r64[:, :, :], ACT.Ln).then_inc(s["e_out"], 1)
            act.wait_ge(s["e_in"], 3)
            act.activation(m[:, :, :], m[:, :, :], ACT.Exp).then_inc(s["e_out"], 1)

            def normalise(t, par):
                act.wait_ge(s["mixed"], t + 1)
                act.activation(z[par][:, :], tile(x, t), ACT.Identity, bias=nmr[:, ds(t, 1)],
                               scale=rstd[:, ds(t, 1)]).then_inc(s["z2"], 1)

            def copy_pre(t):
                act.wait_ge(s["y"], t + 1)
                act.wait_ge(s["preT_ready"], PR0 + t + 1)
                act.activation(preT[:, :, :], ppre[:, 0:C].rearrange("p (k n) -> p k n", n=P), ACT.Copy)\
                    .then_inc(s["preT"], 1)

            normalise(0, 0)
            normalise(1, 1)
            with act.Fori(0, NT // 2 - 1) as j:
                for par in range(2):
                    copy_pre(j * 2 + par)
                    normalise(j * 2 + par + 2, par)
            for par in range(2):
                copy_pre(NT - 2 + par)

        @block.vector
        def _(dve):
            dve.drain().then_inc(s["read"], RD0)
            dve.drain().then_inc(s["mixed"], MX0)
            with dve.Fori(0, NT // 2) as j:
                for i in range(2):
                    t = j * 2 + i
                    dve.wait_ge(x_loaded[i], DMA0 + j * 16 + 16)
                    for half in range(2):
                        dve.bn_stats(stat[:, half, :], x[:, ds(t, 1), half * BANK:(half + 1) * BANK]
                                     .rearrange("p o n -> p (o n)"))
                    dve.drain()
                    dve.bn_aggr(aggr[:, :], stat[:, :, :])
                    dve.drain()
                    dve.tensor_copy(tile(mv, t), aggr[:, :])
            dve.drain()
            dve.tensor_scalar(var_e[:, :], mv[:, :, 1], LN_EPS, None, ALU.add).then_inc(s["stat_in"], 1)
            dve.wait_ge(s["rstd"], 1)
            dve.tensor_tensor(rms_e[:, :], rstd[:, :], rstd[:, :], ALU.mult)
            dve.drain()
            dve.tensor_tensor(rms_e[:, :], rms_e[:, :], mv[:, :, 1], ALU.mult)
            dve.drain()
            dve.tensor_scalar(rms_e[:, :], rms_e[:, :], RMS_EPS, None, ALU.add).then_inc(s["rms_in"], 1)
            dve.tensor_tensor(nmr[:, :], rstd[:, :], mv[:, :, 0], ALU.mult)
            dve.drain()
            dve.tensor_scalar(nmr[:, :], nmr[:, :], -1.0, None, ALU.mult)

            def normalise_tile(t, par):
                dve.wait_ge(s["zT_ready"], 2 * t + 2)
                dve.tensor_scalar(z[par][:, :], tile(x, t), mv[:, ds(t, 1), 0], rstd[:, ds(t, 1)],
                                  ALU.subtract, ALU.mult).then_inc(s["z"], 1)

            def logits(t, par):
                dve.wait_ge(s["logit"], LG0 + t + 1)
                dve.scalar_tensor_tensor(tile(lg, t), plg[:, par, 0:NL], rms[:, ds(t, 1)], base[:, :],
                                         ALU.mult, ALU.add).then_inc(s["read"], 1)

            normalise_tile(0, 0)
            normalise_tile(1, 1)
            dve.wait_ge(s["rms"], 1)
            dve.wait_ge(s["small"], 64)
            with dve.Fori(0, NT // 2 - 1) as j:
                for par in range(2):
                    normalise_tile(j * 2 + par + 2, par)
                    logits(j * 2 + par, par)
            for par in range(2):
                logits(NT - 2 + par, par)
            dve.drain()
            ppl = lg[:, :, NS * NS:].rearrange("p t (a n) -> p t a n", a=2)
            half64 = r64[:, :, 0:2]
            dve.tensor_reduce(half64, ppl, AX.X, ALU.max)
            dve.drain()
            dve.tensor_tensor(pp[:, :, :, :], ppl, spread(half64), ALU.subtract)
            dve.tensor_scalar(m[:, :, :], lg[:, :, 0:NS * NS], 1.0 / TAU, None, ALU.mult)
            dve.drain()
            dve.tensor_reduce(r64[:, :, :], lines(m, "row"), AX.X, ALU.max)
            dve.drain()
            dve.tensor_tensor(lines(m, "row"), lines(m, "row"), spread(r64[:, :, :]), ALU.subtract)\
                .then_inc(s["e_in"], 1)
            dve.wait_ge(s["e_out"], 2)
            dve.tensor_reduce(r64[:, :, :], lines(e, "row"), AX.X, ALU.add)\
                .then_inc(s["e_in"], 1)
            dve.wait_ge(s["gate"], 1)
            dve.tensor_scalar(g[:, 2:3], g[:, 1:2], 1.0, None, ALU.add)
            dve.drain()
            dve.reciprocal(g[:, 2:3], g[:, 2:3])
            dve.drain()
            dve.tensor_scalar(g[:, 3:4], g[:, 2:3], -1.0, 1.0, ALU.mult, ALU.add)
            dve.wait_ge(s["e_out"], 3)
            dve.tensor_tensor(lines(m, "row"), lines(m, "row"), spread(r64[:, :, :]), ALU.subtract)
            dve.drain()
            dve.tensor_reduce(r64[:, :, :], lines(m, "col"), AX.X, ALU.max)
            dve.drain()
            dve.tensor_tensor(lines(m, "col"), lines(m, "col"), spread(r64[:, :, :]), ALU.subtract)\
                .then_inc(s["e_in"], 1)
            dve.tensor_reduce(sums[:, :, :], pp[:, :, :, :], AX.X, ALU.add)
            dve.drain()
            dve.reciprocal(sums[:, :, :], sums[:, :, :])
            dve.drain()
            dve.tensor_tensor(pp[:, :, :, :], pp[:, :, :, :], spread(sums[:, :, :]), ALU.mult)
            dve.wait_ge(s["e_out"], 4)

            def normalise(axis):
                dve.drain()
                dve.tensor_reduce(r64[:, :, :], lines(m, axis), AX.X, ALU.add)
                dve.drain()
                dve.reciprocal(r64[:, :, :], r64[:, :, :])
                dve.drain()
                dve.tensor_tensor(lines(m, axis), lines(m, axis), spread(r64[:, :, :]), ALU.mult)

            normalise("col")
            with dve.Fori(0, SINKHORN_ITERS - 1):
                normalise("row")
                normalise("col")
            dve.drain()
            dve.tensor_scalar(m[:, :, :], m[:, :, :], g[:, 2:3], None, ALU.mult)
            dve.drain()
            diag = m[:, :, 0:NS * NS:NS + 1]
            dve.tensor_scalar(diag, diag, g[:, 3:4], None, ALU.add)
            dve.drain()

            def stream(t, n):
                return x[:, ds(t, 1), n * C:(n + 1) * C].rearrange("p o n -> p (o n)")

            def premix(t, par):
                dve.wait_ge(s["z2"], t + 1)
                dve.wait_ge(s["preT_ready"], t + 1)
                for n in range(NS):
                    zn = z[par][:, n * C:(n + 1) * C]
                    if n == 0:
                        dve.tensor_scalar(pre[par][:, :], zn, pp[:, ds(t, 1), 0, n], None, ALU.mult)
                    else:
                        dve.drain()
                        ins = dve.scalar_tensor_tensor(pre[par][:, :], zn, pp[:, ds(t, 1), 0, n],
                                                       pre[par][:, :], ALU.mult, ALU.add)
                ins.then_inc(s["pre"], 1)

            def mix(t, par):
                for j in range(NS):
                    for i in range(NS):
                        dve.scalar_tensor_tensor(stream(t, i), z[par][:, j * C:(j + 1) * C],
                                                 m[:, ds(t, 1), i * NS + j], stream(t, i), ALU.mult, ALU.add)
                    dve.drain()
                dve.wait_ge(s["y"], Y0 + t + 1)
                for i in range(NS):
                    dve.scalar_tensor_tensor(stream(t, i), py[:, par, 0:C], pp[:, ds(t, 1), 1, i],
                                             stream(t, i), ALU.mult, ALU.add)
                dve.drain().then_inc(s["mixed"], 1)

            premix(0, 0)
            with dve.Fori(0, NT // 2 - 1) as j:
                for par in range(2):
                    premix(j * 2 + par + 1, 1 - par)
                    mix(j * 2 + par, par)
            premix(NT - 1, 1)
            mix(NT - 2, 0)
            mix(NT - 1, 1)

        @block.tensor
        def _(pe):
            def transposes(t, par):
                pe.wait_ge(s["z"], t + 1)
                for half in range(2):
                    pe.wait_ge(s["zT"], 2 * t + half + 1)
                    for k in range(4):
                        tr = pe.transpose(pz[:, par, half, k * P:(k + 1) * P],
                                          z[par][:, (4 * half + k) * P:(4 * half + k + 1) * P], ident[:, :])
                    tr.then_inc(s["zT_ready"], 1)

            def logits(t, par):
                pe.wait_ge(s["read"], t + 1)
                pe.wait_ge(s["zT"], ZT0 + 2 * t + 2)
                for k in range(KC):
                    mm = pe.matmul(plg[:, par, 0:NL], zT[par][:, k, :], w24_sb[:, k, :],
                                   start=(k == 0), stop=(k == KC - 1))
                mm.then_inc(s["logit"], 1)

            def branch(t, par):
                pe.wait_ge(s["pre"], t + 1)
                pe.wait_ge(s["preT"], t + 1)
                for k in range(C // P):
                    tr = pe.transpose(ppre[:, k * P:(k + 1) * P], pre[par][:, k * P:(k + 1) * P], ident[:, :])
                tr.then_inc(s["preT_ready"], 1)
                pe.wait_ge(s["mixed"], t + 1)
                pe.wait_ge(s["preT"], PT0 + t + 1)
                for k in range(C // P):
                    mm = pe.matmul(py[:, par, 0:C], preT[:, k, :], wb[:, k, :],
                                   start=(k == 0), stop=(k == C // P - 1))
                mm.then_inc(s["y"], 1)

            pe.wait_ge(s["const"], 1)
            pe.wait_ge(s["small"], 64)
            pe.sem_inc(s["zT_ready"], ZR0)
            pe.sem_inc(s["logit"], LG0)
            pe.sem_inc(s["preT_ready"], PR0)
            pe.sem_inc(s["y"], Y0)
            transposes(0, 0)
            with pe.Fori(0, NT // 2 - 1) as j:
                for par in range(2):
                    transposes(j * 2 + par + 1, 1 - par)
                    logits(j * 2 + par, par)
            transposes(NT - 1, 1)
            logits(NT - 2, 0)
            logits(NT - 1, 1)
            with pe.Fori(0, NT // 2) as j:
                for par in range(2):
                    branch(j * 2 + par, par)


NE, NR = 8, 16
ER = NE * NR
NX = 256
SCALING = 32.0 / 16.0
MAX_THRESHOLD = 0.125


def expert_ffn(nc, sem, x_in, w_base, w_small, w_b, bias, b_thr, x_out):
    s = {n: sem(f"e_{n}") for n in (
        "const", "small", "w0", "w1", "w_hi", "w_lo", "x0", "x1", "x2", "x3", "stats", "pow", "z", "zT_ready",
        "zT_hi", "zT_lo", "ex", "g_in", "g_exp", "hw", "hwT_ready", "hw_hi", "hw_lo", "out", "xb", "done",
        "st0", "st1", "st2", "st3")}
    x_loaded, stored = [s[f"x{i}"] for i in range(4)], [s[f"st{i}"] for i in range(4)]
    w_loaded = (s["w0"], s["w1"])
    ZT0, HL0, DN0, ZR0, DMA0 = 2, 2, 4, 4, 16
    TURNS = NT // 4
    with ExitStack() as ctx:
        def sb(name, shape, dt=F32):
            return ctx.enter_context(nc.sbuf_tensor(f"e_{name}", shape, dt))

        ident = sb("ident", [P, P])
        nhalf = sb("nhalf", [P, 1])
        bias_sb = sb("bias", [P, D])
        thr_b = sb("thr_b", [P, 1])
        wraw = [sb(f"wraw{i}", [P, D]) for i in range(2)]
        wbase = [sb(f"wbase_{n}", [P, KC, D], F32R) for n in ("hi", "lo")]
        wsmall = [sb(f"wsmall_{n}", [P, KC, NX], F32R) for n in ("hi", "lo")]
        wexp = [sb(f"wexp_{n}", [P, D], F32R) for n in ("hi", "lo")]
        x = [sb(f"x{i}", [P, D]) for i in range(4)]
        z = sb("z", [P, D])
        stat = sb("stat", [P, 2, 6])
        mv = [sb(f"mv{i}", [P, 4]) for i in range(2)]
        zT = [[sb(f"zT_{n}{i}", [P, KC, P], F32R) for n in ("hi", "lo")] for i in range(2)]
        lg = sb("lg", [P, NE + 1])
        nmx = sb("nmx", [P, 1])
        ge = sb("ge", [P, NE + 1])
        sc = sb("sc", [P, 8])
        hw = sb("hw", [P, ER])
        hwT = [sb(f"hwT_{n}", [P, P], F32R) for n in ("hi", "lo")]
        pz = ctx.enter_context(nc.psum_tensor("e_pz", [P, 2, BANK], F32))
        pex = ctx.enter_context(nc.psum_tensor("e_pex", [P, 2, BANK], F32))
        pout = ctx.enter_context(nc.psum_tensor("e_pout", [P, 2, 2, BANK], F32))
        block = ctx.enter_context(nc.Block())

        W = [(w_small[k * P:(k + 4) * P, :].rearrange("(k p) n -> p k n", p=P), 4,
              [w[:, k:k + 4, :] for w in wsmall]) for k in (0, 4)]
        W += [(w_base[k * P:(k + 1) * P, :].rearrange("p (o n) -> p o n", o=1), 1,
               [w[:, k:k + 1, :] for w in wbase]) for k in range(KC)]
        W += [(w_b.rearrange("p (o n) -> p o n", o=1), 1,
               [w[:, :].rearrange("p (o n) -> p o n", o=1) for w in wexp])]

        def turns(eng, turn):
            with eng.Fori(0, TURNS - 1) as j:
                turn(j, False)
            turn(TURNS - 1, True)

        @block.sync
        def _(sp):
            def load_x(t, q, j):
                sp.wait_ge(stored[q], DMA0 + j * 16)
                sp.dma_start(x[q][:, :], x_in[ds(t * P, P), :]).then_inc(x_loaded[q], 16)

            def load_w(i):
                if i >= 2:
                    sp.wait_ge(s["w_lo"], i - 1)
                src, n, _ = W[i]
                sp.dma_start(wraw[i % 2][:, :].rearrange("p (k n) -> p k n", k=n), src).then_inc(w_loaded[i % 2], 16)

            for q in range(4):
                sp.sem_inc(stored[q], DMA0)
            for q in range(2):
                load_x(q, q, 0)
            sp.dma_start(bias_sb[:, :], bias).then_inc(s["small"], 16)
            sp.dma_start(thr_b[:, :], b_thr).then_inc(s["small"], 16)
            for i in range(len(W)):
                load_w(i)
            for q in range(2, 4):
                load_x(q, q, 0)

            def turn(j, last):
                for q in range(4):
                    sp.wait_ge(s["done"], DN0 + (j * 4 + q) * 2 + 2)
                    sp.dma_start(x_out[ds((j * 4 + q) * P, P), :], x[q][:, :]).then_inc(stored[q], 16)
                    if not last:
                        load_x((j + 1) * 4 + q, q, j + 1)

            turns(sp, turn)
            for q in range(4):
                sp.wait_ge(stored[q], DMA0 + 16 * TURNS)

        @block.gpsimd
        def _(pool):
            pool.memset(ident[:, :], 0.0)
            pool.memset(nhalf[:, :], -0.5)
            pool.drain()
            pool.affine_select(out=ident[:, :], in_=ident[:, :], compare_op=ALU.not_equal, fill=1.0, base=0,
                               pattern=[[-1, P]], channel_multiplier=1).then_inc(s["const"], 1)
            pool.wait_ge(s["small"], 32)

            def rstd(t, par):
                pool.wait_ge(s["stats"], t + 1)
                pool.tensor_tensor(mv[par][:, 3:4], mv[par][:, 2:3], nhalf[:, :], ALU.pow).then_inc(s["pow"], 1)

            def add_bias(t, q):
                pool.wait_ge(s["z"], t + 1)
                pool.tensor_tensor(x[q][:, :], x[q][:, :], bias_sb[:, :], ALU.add).then_inc(s["xb"], 1)

            rstd(0, 0)
            add_bias(0, 0)
            rstd(1, 1)

            def turn(j, last):
                for q in range(4):
                    if last and q == 3:
                        continue
                    add_bias(j * 4 + q + 1, (q + 1) % 4)
                    if not (last and q == 2):
                        rstd(j * 4 + q + 2, q % 2)

            turns(pool, turn)

        @block.scalar
        def _(act):
            for i, (_, n, dst) in enumerate(W):
                act.wait_ge(w_loaded[i % 2], (i // 2 + 1) * 16)
                act.activation(dst[0], wraw[i % 2][:, :].rearrange("p (k n) -> p k n", k=n), ACT.Copy)\
                    .then_inc(s["w_hi"], 1)

            def part_hi(t, par):
                for half in range(2):
                    act.wait_ge(s["zT_ready"], ZR0 + 2 * t + half + 1)
                    act.activation(zT[par][0][:, 4 * half:4 * half + 4, :],
                                   pz[:, half, :].rearrange("p (k n) -> p k n", n=P), ACT.Copy).then_inc(s["zT_hi"], 1)

            def experts(t, par):
                act.wait_ge(s["g_in"], t + 1)
                act.activation(ge[:, :], lg[:, :], ACT.Exp).then_inc(s["g_exp"], 1)
                act.wait_ge(s["hwT_ready"], t + 1)
                act.activation(hwT[0][:, :], pex[:, par, NX:NX + P], ACT.Copy).then_inc(s["hw_hi"], 1)

            part_hi(0, 0)

            def turn(j, last):
                for q in range(4):
                    if not (last and q == 3):
                        part_hi(j * 4 + q + 1, (q + 1) % 2)
                    experts(j * 4 + q, q % 2)

            turns(act, turn)

        @block.vector
        def _(dve):
            dve.drain().then_inc(s["zT_lo"], ZT0)
            dve.drain().then_inc(s["hw_lo"], HL0)
            dve.drain().then_inc(s["done"], DN0)

            def statistics(t, par, q, jq):
                dve.wait_ge(x_loaded[q], jq * 16 + 16)
                for half in range(2):
                    dve.bn_stats(stat[:, half, :], x[q][:, half * BANK:(half + 1) * BANK])
                dve.drain()
                dve.bn_aggr(mv[par][:, 0:2], stat[:, :, :])
                dve.drain()
                dve.tensor_scalar(mv[par][:, 2:3], mv[par][:, 1:2], LN_EPS, None, ALU.add).then_inc(s["stats"], 1)

            def normalise(t, par, q):
                dve.wait_ge(s["pow"], t + 1)
                dve.wait_ge(s["zT_ready"], 2 * t + 2 + 2)
                dve.tensor_scalar(z[:, :], x[q][:, :], mv[par][:, 0:1], mv[par][:, 3:4],
                                  ALU.subtract, ALU.mult).then_inc(s["z"], 1)

            def part_lo(t, par):
                for half in range(2):
                    dve.wait_ge(s["zT_hi"], 2 * t + half + 1)
                    cols = slice(4 * half, 4 * half + 4)
                    dve.tensor_tensor(zT[par][1][:, cols, :], pz[:, half, :].rearrange("p (k n) -> p k n", n=P),
                                      zT[par][0][:, cols, :].bitcast(F32), ALU.subtract).then_inc(s["zT_lo"], 1)

            def experts(t, par):
                logits = pex[:, par, ER:ER + NE + 1]
                dve.wait_ge(s["ex"], t + 1)
                dve.tensor_reduce(nmx[:, :], logits[:, 0:NE], AX.X, ALU.max)
                dve.tensor_scalar(lg[:, NE:], logits[:, NE:], thr_b[:, :], -1.0, ALU.add, ALU.mult)
                dve.drain()
                dve.tensor_scalar(lg[:, 0:NE], logits[:, 0:NE], nmx[:, :], None, ALU.subtract).then_inc(s["g_in"], 1)
                dve.wait_ge(s["g_exp"], t + 1)
                dve.tensor_reduce(sc[:, 0:1], ge[:, 0:NE], AX.X, ALU.add)
                dve.tensor_scalar(sc[:, 1:2], ge[:, NE:], 1.0, None, ALU.add)
                dve.drain()
                dve.reciprocal(sc[:, 2:4], sc[:, 0:2])
                dve.drain()
                dve.tensor_scalar(sc[:, 3:4], sc[:, 3:4], MAX_THRESHOLD, None, ALU.mult)
                dve.drain()
                dve.tensor_scalar(ge[:, 0:NE], ge[:, 0:NE], sc[:, 2:3], sc[:, 3:4], ALU.mult, ALU.subtract)
                dve.drain()
                dve.tensor_scalar(ge[:, 0:NE], ge[:, 0:NE], 0.0, None, ALU.max)
                dve.drain()
                dve.tensor_reduce(sc[:, 4:5], ge[:, 0:NE], AX.X, ALU.add)
                dve.drain()
                dve.tensor_scalar(sc[:, 5:6], sc[:, 4:5], 0.0, None, ALU.is_equal)
                dve.drain()
                dve.tensor_tensor(sc[:, 4:5], sc[:, 4:5], sc[:, 5:6], ALU.add)
                dve.drain()
                dve.reciprocal(sc[:, 6:7], sc[:, 4:5])
                dve.drain()
                dve.tensor_scalar(ge[:, 0:NE], ge[:, 0:NE], sc[:, 6:7], SCALING, ALU.mult, ALU.mult)
                dve.drain()
                dve.tensor_tensor(hw[:, :].rearrange("p (e r) -> p e r", r=NR),
                                  pex[:, par, 0:ER].rearrange("p (e r) -> p e r", r=NR),
                                  ge[:, 0:NE].unsqueeze(2).broadcast_to([P, NE, NR]), ALU.mult).then_inc(s["hw"], 1)

            def expert_lo(t, par):
                dve.wait_ge(s["hw_hi"], t + 1)
                dve.tensor_tensor(hwT[1][:, :], pex[:, par, NX:NX + P], hwT[0][:, :].bitcast(F32), ALU.subtract)\
                    .then_inc(s["hw_lo"], 1)

            def finish(t, par, q):
                dve.wait_ge(s["xb"], t + 1)
                for half in range(2):
                    cols = slice(half * BANK, (half + 1) * BANK)
                    dve.wait_ge(s["out"], 2 * t + half + 1)
                    dve.tensor_tensor(x[q][:, cols], x[q][:, cols], pout[:, par, half, :], ALU.add)\
                        .then_inc(s["done"], 1)

            statistics(0, 0, 0, 0)
            normalise(0, 0, 0)
            statistics(1, 1, 1, 0)
            for i, (_, n, dst) in enumerate(W):
                dve.wait_ge(s["w_hi"], i + 1)
                dve.tensor_tensor(dst[1], wraw[i % 2][:, :].rearrange("p (k n) -> p k n", k=n), dst[0].bitcast(F32),
                                  ALU.subtract).then_inc(s["w_lo"], 1)
            part_lo(0, 0)
            dve.wait_ge(s["small"], 32)

            def turn(j, last):
                for q in range(4):
                    t, par = j * 4 + q, q % 2
                    if not (last and q == 3):
                        normalise(t + 1, 1 - par, (q + 1) % 4)
                    if not (last and q >= 2):
                        dve.drain()
                        statistics(t + 2, par, (q + 2) % 4, j + (q + 2) // 4)
                    experts(t, par)
                    if not (last and q == 3):
                        part_lo(t + 1, 1 - par)
                    expert_lo(t, par)
                    finish(t, par, q)

            turns(dve, turn)

        @block.tensor
        def _(pe):
            THREE = ((0, 0), (0, 1), (1, 0))

            def transposes(t):
                pe.wait_ge(s["z"], t + 1)
                for half in range(2):
                    pe.wait_ge(s["zT_lo"], 2 * t + half + 1)
                    for k in range(4):
                        tr = pe.transpose(pz[:, half, k * P:(k + 1) * P],
                                          z[:, (4 * half + k) * P:(4 * half + k + 1) * P], ident[:, :])
                    tr.then_inc(s["zT_ready"], 1)

            def products(t, par):
                pe.wait_ge(s["zT_lo"], ZT0 + 2 * t + 2)
                pe.wait_ge(s["hw_lo"], t + 1)
                n = 0
                for k in range(KC):
                    for a, b in THREE:
                        mm = pe.matmul(pex[:, par, 0:NX], zT[par][a][:, k, :], wsmall[b][:, k, :],
                                       start=(n == 0), stop=(n == 3 * KC - 1))
                        n += 1
                mm.then_inc(s["ex"], 1)
                for half in range(2):
                    pe.wait_ge(s["done"], 2 * t + half + 1)
                    n = 0
                    for k in range(KC):
                        for a, b in THREE:
                            pe.matmul(pout[:, par, half, :], zT[par][a][:, k, :],
                                      wbase[b][:, k, half * BANK:(half + 1) * BANK], start=(n == 0), stop=False)
                            n += 1
                pe.wait_ge(s["hw"], t + 1)
                pe.transpose(pex[:, par, NX:NX + P], hw[:, :], ident[:, :]).then_inc(s["hwT_ready"], 1)
                pe.wait_ge(s["hw_lo"], HL0 + t + 1)
                for half in range(2):
                    for n, (a, b) in enumerate(THREE):
                        mm = pe.matmul(pout[:, par, half, :], hwT[a][:, :], wexp[b][:, half * BANK:(half + 1) * BANK],
                                       start=False, stop=(n == 2))
                    mm.then_inc(s["out"], 1)

            pe.wait_ge(s["const"], 1)
            pe.sem_inc(s["zT_ready"], ZR0)
            transposes(0)
            pe.wait_ge(s["w_lo"], len(W))

            def turn(j, last):
                for q in range(4):
                    if not (last and q == 3):
                        transposes(j * 4 + q + 1)
                    products(j * 4 + q, q % 2)

            turns(pe, turn)


@contextmanager
def stage(nc):
    taken = []

    def sem(name):
        taken.append(nc.alloc_semaphore(name))
        return taken[-1]

    yield sem
    nc.clear_and_free_semaphores(taken)
    nc.all_engine_barrier()


def build(nc, x, wqkv, rope, wo, ffn0, ffn1, out):
    def scratch(name, shape):
        return nc.dram_tensor(name, shape, F32, kind="Internal").ap()

    x1, x2, x3 = (scratch(f"x{i}", (T, D)) for i in (1, 2, 3))
    oT_d = [scratch(f"oT_{i}", (NG, P, NT, P)) for i in range(2)]
    swaps = [[i ^ 1 for i in range(HD)], [(i + HD // 2) % HD for i in range(HD)]]
    with stage(nc) as sem:
        attention(nc, sem, 0, x, wqkv[0], *rope[0], swaps[0], oT_d[0])
    with stage(nc) as sem:
        output_projection(nc, sem, 0, oT_d[0], wo[0], x, x1)
    with stage(nc) as sem:
        hyper_connection(nc, sem, x1, *ffn0, x2)
    with stage(nc) as sem:
        attention(nc, sem, 1, x2, wqkv[1], *rope[1], swaps[1], oT_d[1])
    with stage(nc) as sem:
        output_projection(nc, sem, 1, oT_d[1], wo[1], x2, x3)
    with stage(nc) as sem:
        expert_ffn(nc, sem, x3, *ffn1, out)


def rope_tables(pair_of, sign_of):
    freq = (1.0 / np.float32(THETA) ** (np.arange(0, HD, 2, dtype=np.float32) / np.float32(HD))).astype(np.float32)
    ang = np.outer(freq[pair_of], np.arange(S, dtype=np.float32)).astype(np.float32)
    cos, sin = np.cos(ang).astype(np.float32), (np.sin(ang) * sign_of[:, None]).astype(np.float32)
    return np.tile(cos, (GH, 1)), np.tile(sin, (GH, 1))


def qkv_layout(wk, wv, wq):
    w = np.concatenate([wk, wq[:, :P], wv, wq[:, P:]], axis=1).reshape(KC, P, N_WCHUNK, P).transpose(2, 1, 0, 3)
    return np.concatenate([w, w[:2]], axis=0)


def laid_out(a):
    i = np.arange(HD)
    rope = [rope_tables(i // 2, np.where(i % 2 == 0, -1, 1).astype(np.float32)),
            rope_tables(i % (HD // 2), np.where(i < HD // 2, -1, 1).astype(np.float32))]
    w24 = np.concatenate([a["L0_ffn_W_res"], a["L0_ffn_W_pre"], a["L0_ffn_W_post"]], axis=0)
    base24 = np.concatenate([a["L0_ffn_H_res_base"].reshape(-1), a["L0_ffn_H_pre_base"], a["L0_ffn_H_post_base"]])
    small = np.concatenate([a["L1_ffn_A_w"].reshape(ER, D), a["L1_ffn_W_gate"], a["L1_ffn_W_thr"][None, :],
                            np.zeros((NX - ER - NE - 1, D), np.float32)], axis=0)
    out = {
        "x": a["L0_attn_x"].reshape(T, D),
        "wqkv0": qkv_layout(a["L0_attn_wk"], a["L0_attn_wv"], a["L0_attn_wq"]),
        "wqkv1": qkv_layout(a["L1_attn_Wk"], a["L1_attn_Wv"], a["L1_attn_Wq"]),
        "cos0": rope[0][0], "sin0": rope[0][1], "cos1": rope[1][0], "sin1": rope[1][1],
        "wo0": a["L0_attn_wo"], "wo1": a["L1_attn_Wo"],
        "w24": w24.T.reshape(KC, P, NL).transpose(1, 0, 2),
        "base24": np.broadcast_to(base24, (P, NL)),
        "gate": np.broadcast_to(a["L0_ffn_gate"], (P, 1)),
        "w_branch": a["L0_ffn_W_branch"],
        "w_base": a["L1_ffn_W_base"].T,
        "w_small": small.T,
        "w_b": a["L1_ffn_B_w"].transpose(0, 2, 1).reshape(ER, D),
        "bias": np.broadcast_to(a["L1_ffn_b_base"], (P, D)),
        "b_thr": np.broadcast_to(a["L1_ffn_b_thr"], (P, 1)),
    }
    return {n: np.ascontiguousarray(v) for n, v in out.items()}


def program(nc, t, out):
    build(nc, t["x"], (t["wqkv0"], t["wqkv1"]), ((t["cos0"], t["sin0"]), (t["cos1"], t["sin1"])),
          (t["wo0"], t["wo1"]), (t["w24"], t["base24"], t["gate"], t["w_branch"]),
          (t["w_base"], t["w_small"], t["w_b"], t["bias"], t["b_thr"]), out)


def kernel(**inputs):
    import concourse.bacc as bacc
    from concourse.bass_utils import run_bass_kernel_spmd

    nc = bacc.Bacc("TRN2", target_bir_lowering=False, num_devices=1)
    arrays = laid_out({n: np.asarray(v) for n, v in inputs.items()})
    aps = {n: nc.dram_tensor(f"in_{n}", v.shape, F32, kind="ExternalInput").ap() for n, v in arrays.items()}
    out = nc.dram_tensor("out", (T, D), F32, kind="ExternalOutput").ap()
    program(nc, aps, out)
    r = run_bass_kernel_spmd(nc, [{f"in_{n}": v for n, v in arrays.items()}], core_ids=[0])
    return r.results[0]["out"].reshape(B, S, D)
```

```python
from contextlib import ExitStack, contextmanager

import numpy as np

import concourse.bass as bass
from concourse import mybir

F32 = mybir.dt.float32
F32R = mybir.dt.float32r
BF16 = mybir.dt.bfloat16
ALU = mybir.AluOpType
ACT = mybir.ActivationFunctionType
AX = mybir.AxisListType

P = 128
B, S, D = 2, 1024, 1024
T = B * S
NT = T // P
ST_ = S // P
KC = D // P
HD = 32
NG = 8
GH = 4
BANK = 512
NQC = S // BANK
NX_BUF = 6
NX_AHEAD = 4
LN_EPS = 1e-5
RMS_EPS = 1.1920929e-07
THETA = 10000.0
MASKED = -1e30
N_WCHUNK = 12
ds = bass.ds


UNITS = [(qc, ki) for qc in range(NQC) for ki in range(4 * qc + 4)]
NU = len(UNITS)
DIAGONAL = [e for e, (qc, ki) in enumerate(UNITS) if ki >= 4 * qc]
CHUNK_END = [e for e, (qc, ki) in enumerate(UNITS) if ki == 4 * qc + 3]


def unit_offset(e):
    qc, ki = UNITS[e]
    return max(0, ki * P - qc * BANK)


def score_uses():
    out = []
    for qt in range(ST_):
        for kc in range(qt // 4 + 1):
            n = min(BANK, (qt + 1) * P - kc * BANK)
            m = BANK // n if BANK % n == 0 else 1
            for h in range(0, GH, m):
                out.append((qt, kc, n, tuple(range(h, h + m)), kc == qt // 4))
    return out


USES = score_uses()
SECOND_HALF = [qt for qt, *_ in USES].index(ST_ // 2)


PIECES = 8


def columns(step):
    what, e, _ = step
    n = BANK - unit_offset(e)
    return 2 * max(n, BANK // 2) if what == "ST" else 4 * n


def iteration(full_s=True, proj=True, ahead=False):
    steps = [[("ST", e + 1, 0), ("ST", e + 1, 1), ("PV", e, 0), ("PV", e, 1)] for e in range(NU)]
    steps[-1] = steps[-1][2:]
    after = {step: [] for unit in steps for step in unit}
    first = []
    if proj:
        quarter = lambda c, i: [("P", c, k) for k in range(i * PIECES // 4, (i + 1) * PIECES // 4)]
        first = quarter(0, 0)
        for i, step in enumerate(steps[0][:3]):
            after[step] += quarter(0, i + 1)
        after[steps[0][0]] += [("WS", 0)]
        after[steps[1][1]] += [("HI", 0)]
        after[steps[2][0]] += [("LO", 0)]
        after[steps[2][0]] += [("WL", 0)]
        after[steps[5][0]] += [("RS", 0)]
        after[steps[10][1]] += quarter(1, 0)
        after[steps[10][2]] += quarter(1, 1) + [("RK", 0)]
        after[steps[10][3]] += quarter(1, 2) + quarter(1, 3)
    if full_s:
        window = [step for unit in steps[1:10] for step in unit]
        total, done, k = sum(map(columns, window)), 0, 0
        for step in window:
            done += columns(step)
            while k < len(USES) and k * total < done * len(USES) - total // 2:
                after[step] += [("S", k)]
                k += 1
        assert k == len(USES)
        after[steps[10][1]] += [("MT", 0)]
    after[steps[10][1]] += [("NORM", 0)]
    if ahead:
        for i in range(ST_):
            after[steps[i][0]] += [("XS", i)]
            after[steps[i][2]] += [("XN", i)]
            after[steps[i + 2][1]] += [("XT", i)]
            after[steps[i + 2][2]] += [("XC", i)] + [("XL", i + NX_AHEAD)] * (i + NX_AHEAD < ST_)
        first = [("XL", i) for i in range(NX_AHEAD)]
        for i in range(PIECES):
            after[steps[10][i * 3 // PIECES]] += [("P", "next", i)]
    order = [("ST", 0, 0), ("ST", 0, 1)] + ([("HI", 1), ("LO", 1), ("RS", 1)] if full_s else []) + first
    for unit in steps:
        for step in unit:
            order += [step] + after[step]
    return order + [("NORM", 1)]


def prologue():
    order = []
    for p in range(6):
        for c in range(2):
            for i in range(PIECES):
                order += [("P", p, c, i)]
        if p in VALUES:
            order += [("VT", p, 0), ("VT", p, 1)]
    out, k, n = [], 0, 0
    for step in order:
        out.append(step)
        if step[0] == "P" and (4, 0) <= step[1:3] <= (5, 0):
            n += 1
            while k * S_STEPS < n * len(USES) and k < len(USES):
                out.append(("S", k))
                k += 1
            if n == S_STEPS:
                out.append(("MT", 0))
    assert k == len(USES)
    return out[PIECES:]


S_STEPS = 3 * PIECES - 5
VALUES = (3, 4)
LO_ORDER = (0, 1, 2, 5)


def bank_plan(order, spare=()):
    last, plan, n, held = {}, {}, 0, None
    for step in order:
        what = step[0]
        if what == "P" and step[-1] == 0:
            held = spare[len([k for k in plan if k[0] == "P"]) % len(spare)] if spare else \
                min((0, 1), key=lambda x: last.get(x, -1))
            plan[step[:-1]] = [None, held, last.get(held, -1)]
        if what == "P" and step[-1] == PIECES - 1:
            plan[step[:-1]][0] = n
            last[held], held = n, None
            n += 1
        if what in ("S", "MT", "VT"):
            bank = min((x for x in (0, 1) if x != held), key=lambda x: last.get(x, -1))
            plan[step] = [n, bank, last.get(bank, -1)]
            last[bank] = n
            n += 1
    return plan, n


def attention(nc, sem, layer, x_in, wqkv, cos_in, sin_in, swap, oT_d):
    kT_d = nc.dram_tensor(f"kT_{layer}", (2, B, NG * HD, S), F32, kind="Internal").ap()
    q_d = nc.dram_tensor(f"q_{layer}", (2, 2, P, S), F32, kind="Internal").ap()
    m_d = nc.dram_tensor(f"rowmax_{layer}", (2, GH * ST_, P), F32, kind="Internal").ap()
    scale = 1.0 / float(np.sqrt(np.float32(HD)))

    s = {n: sem(f"a{layer}_{n}") for n in (
        "const", "table", *(f"xf{i}" for i in range(NX_BUF)), *(f"xl{i}" for i in range(NX_AHEAD)), "stats", "pow", "z_ready", "zT_ready", "zT_hi", "zT_evac",
        "wl0", "wl1", "w_hi", "w_ready", "sh_ready", "sh_free", "roped", "q_hi", "q_lo", "v_ready",
        "k_out", "q_out", "qs00", "qs01", "qs10", "qs11", "ks0", "ks1", "mx_ready", "mT_ready", "m_out", "mr0", "mr1", "st_ready",
        "exp_done", "mask_done", "pv_done", "acc_copied", "norm_done", "vg_ready", "os0", "os1",
        "pool_turn", "sp_turn", "pe_turn")}
    x_first, x_loaded = [s[f"xf{i}"] for i in range(NX_BUF)], [s[f"xl{i}"] for i in range(NX_AHEAD)]
    w_loaded = (s["wl0"], s["wl1"])
    max_row, o_stored = (s["mr0"], s["mr1"]), (s["os0"], s["os1"])
    stacked, k_stacked = [[s[f"qs{i}{c}"] for c in range(2)] for i in range(2)], (s["ks0"], s["ks1"])
    QS, KS = 3 * 16, 3 * 16
    ZT0, W0, SH0, R0, E0, PV0, AC0, N0, ST0, DMA0 = 4, 2, 1, 4, 2, 2, 2, 1, 2, 16

    pro, body, body6, body7 = prologue(), iteration(), iteration(proj=False), iteration(False, False)
    ahead7 = iteration(False, False, True)
    plan_pro, U_PRO = bank_plan(pro, spare=(2, 3, 4, 5))
    plan = {id(order): bank_plan(order)[0] for order in (body, body6, body7, ahead7)}
    U_IT, U_IT6 = bank_plan(body)[1], bank_plan(body6)[1]
    U_BATCH = U_PRO + 6 * U_IT + U_IT6 + 1
    RB = 20

    with ExitStack() as ctx:
        def sb(name, shape, dt=F32):
            return ctx.enter_context(nc.sbuf_tensor(f"a{layer}_{name}", shape, dt))

        ident = sb("ident", [P, P])
        identb = sb("identb", [P, P], BF16)
        negmask = sb("negmask", [P, P], BF16)
        ones = sb("ones", [P, HD])
        nhalf = sb("nhalf", [P, 1])
        cos = sb("cos", [P, S])
        sin = sb("sin", [P, S])
        xin = [sb(f"xin{i}", [P, D]) for i in range(2)]
        stat = [sb(f"stat{i}", [P, 2, 6]) for i in range(2)]
        mv = [sb(f"mv{i}", [P, 4]) for i in range(2)]
        xT = [sb(f"xT_{n}", [P, KC, S], F32R) for n in ("hi", "lo")]
        wraw = [sb(f"wraw{i}", [P, KC, P]) for i in range(2)]
        w = [[sb(f"w_{n}{i}", [P, KC, P], F32R) for n in ("hi", "lo")] for i in range(2)]
        rot = [sb(f"rot{i}", [P, BANK]) for i in range(2)]
        swp = [sb(f"swp{i}", [P, BANK]) for i in range(2)]
        stg = [sb(f"stg_{n}", [P, S], F32R) for n in ("hi", "lo")]
        qst = [sb(f"qst{i}", [P, GH, S], F32R) for i in range(2)]
        kst = [sb(f"kst{i}", [P, S], F32R) for i in range(2)]
        vT = sb("vT", [P, S])
        vall = sb("vall", [P, ST_, NG * HD])
        vg = [sb(f"vg{i}", [P, ST_, HD]) for i in range(2)]
        prob = [sb(f"prob{i}", [P, GH, BANK]) for i in range(2)]
        mx = sb("mx", [P, 2, GH * ST_])
        mT = sb("mT", [GH * ST_, P])
        pvs = sb("pvs", [P, BANK])
        dens = sb("dens", [P, BANK])
        oT = [sb(f"oT{i}", [P, BANK]) for i in range(2)]
        pst = ctx.enter_context(nc.psum_tensor(f"a{layer}_pst", [P, 2, 2, BANK], F32))
        psh = ctx.enter_context(nc.psum_tensor(f"a{layer}_psh", [P, 2, BANK], F32))
        ppv = ctx.enter_context(nc.psum_tensor(f"a{layer}_ppv", [P, BANK], F32))
        pden = ctx.enter_context(nc.psum_tensor(f"a{layer}_pden", [P, BANK], F32))
        xbuf = [x[:, :] for x in xin] + [p[:, 2 * i:2 * i + 2, :].rearrange("p h n -> p (h n)")
                                         for p in prob for i in range(2)]
        x_next = [x[:, :] for x in xin] + [vT[:, :], wraw[0][:, :, :].rearrange("p k n -> p (k n)")]
        mx_hq = [mx[:, i, :].rearrange("p (h q) -> p h q", q=ST_) for i in range(2)]
        block = ctx.enter_context(nc.Block())

        def bank(i):
            return psh[:, i, :] if i < 2 else pst[:, (i - 2) // 2, i % 2, :]

        def pst_banks(k, half):
            return pst[:, k % 2, half, :]

        def psh_banks(k, half):
            return psh[:, half, :]

        def batches(eng, batch):
            with eng.Fori(0, B - 1) as b:
                batch(b, False)
            batch(B - 1, True)

        def over_groups(b, eng, group, last):
            u0 = 1 + b * U_BATCH + U_PRO
            with eng.Fori(0, NG // 2 - 1) as j:
                for par in range(2):
                    group(body, b, j * 2 + par, j, par, u0 + (j * 2 + par) * U_IT)
            group(body6, b, NG - 2, NG // 2 - 1, 0, u0 + 6 * U_IT)
            group(body7 if last else ahead7, b, NG - 1, NG // 2 - 1, 1, u0 + 6 * U_IT + U_IT6)

        @block.sync
        def _(sp):
            def load_w(n, chunk, par):
                sp.wait_ge(s["w_ready"], n + 1)
                sp.dma_start(wraw[par][:, :, :], wqkv[chunk]).then_inc(w_loaded[par], 16)

            def store_k(b, p):
                sp.wait_ge(s["q_lo"], b * RB + 2 * p + 2)
                for part in range(2):
                    sp.dma_start(kT_d[part, ds(b, 1), p * P:(p + 1) * P, :].rearrange("o p n -> p (o n)"),
                                 stg[part][:, :].bitcast(F32)).then_inc(s["k_out"], 16)

            def stack_queries(u, par, c):
                cols = slice(c * BANK, (c + 1) * BANK)
                for part in range(2):
                    sp.dma_start(q_d[par, part, :, cols], stg[part][:, cols].bitcast(F32)).then_inc(s["q_out"], 16)
                sp.wait_ge(s["q_out"], (u + 1) * 32)
                for row, part in enumerate((0, 1, 0)):
                    sp.dma_start(qst[par][row * HD:(row + 1) * HD, :, cols].bitcast(F32),
                                 q_d[par, part, :, cols].rearrange("(h p) n -> p h n", p=HD))\
                        .then_inc(stacked[par][c], 16)

            def stack_keys(b, g, par):
                for row, part in enumerate((0, 0, 1)):
                    src = kT_d[part, ds(b, 1), ds(g * HD, HD), :].rearrange("o p n -> p (o n)")
                    sp.dma_start(kst[par][row * HD:(row + 1) * HD, :].bitcast(F32), src).then_inc(k_stacked[par], 16)

            def row_max(b, g, par):
                n = b * NG + g
                sp.wait_ge(s["mT_ready"], n + 1)
                sp.dma_start(m_d[par], mT[:, :]).then_inc(s["m_out"], 16)
                sp.wait_ge(s["m_out"], DMA0 + n * 16 + 16)
                sp.dma_start(qst[par][96:97, :, :].rearrange("o h n -> o (h n)").bitcast(F32),
                             m_d[par].rearrange("a (o n) -> o (a n)", o=1)).then_inc(max_row[par], 16)

            def store_o(b, g, qc):
                sp.wait_ge(s["norm_done"], N0 + (b * NG + g) * 2 + qc + 1)
                sp.dma_start(oT_d[ds(g, 1), :, ds(b * ST_ + qc * 4, 4), :].rearrange("o p t n -> p (o t) n"),
                             oT[qc][:, :].rearrange("p (t n) -> p t n", n=P)).then_inc(o_stored[qc], 16)

            def group(order, b, g, gh, par, u):
                n = b * NG + g
                for what, k, *_ in order:
                    if what == "WL":
                        load_w(b * N_WCHUNK + g + 8, g + 8, par)
                    if what == "RS" and k == 0:
                        sp.wait_ge(s["st_ready"], ST0 + (n * NU + CHUNK_END[0]) * 2 + 2)
                        sp.wait_ge(s["q_lo"], b * RB + 4 + (g + 2) * 2 + 1)
                        stack_queries(b * 2 * NG + (g + 2) * 2, par, 0)
                    if what == "RK":
                        sp.wait_ge(s["st_ready"], ST0 + n * 2 * NU + 2 * NU)
                        sp.sem_inc(s["sp_turn"], 1)
                        stack_keys(b, g + 2, par)
                    if what == "RS" and k == 1:
                        sp.wait_ge(s["q_lo"], b * RB + 4 + (g + 1) * 2 + 2)
                        stack_queries(b * 2 * NG + (g + 1) * 2 + 1, 1 - par, 1)
                    if what == "MT":
                        row_max(b, g + 1, 1 - par)
                    if what == "NORM":
                        store_o(b, g, k)
                    if what == "XL":
                        if k == 0:
                            sp.wait_ge(s["w_ready"], W0 + (b + 1) * N_WCHUNK + 1)
                            sp.sem_inc(s["sp_turn"], 1)
                        if k >= NX_AHEAD:
                            sp.wait_ge(s["zT_ready"], ZT0 + ((b + 1) * ST_ + k - NX_AHEAD) * 2 + 2)
                            sp.sem_inc(s["sp_turn"], 1)
                        sp.dma_start(x_next[k % NX_AHEAD], x_in[ds((b + 1) * S + k * P, P), :])\
                            .then_inc(x_loaded[k % NX_AHEAD], 16)

            for credited in (s["m_out"], *o_stored):
                sp.sem_inc(credited, DMA0)
            for k in range(ST_):
                if k == NX_BUF:
                    load_w(0, 0, 0)
                    sp.dma_start(cos[:, :], cos_in).then_inc(s["table"], 16)
                    sp.dma_start(sin[:, :], sin_in).then_inc(s["table"], 16)
                    load_w(1, 1, 1)
                if k >= NX_BUF:
                    sp.wait_ge(s["zT_ready"], ZT0 + (k - NX_BUF) * 2 + 2)
                sp.dma_start(xbuf[k % NX_BUF], x_in[k * P:(k + 1) * P, :]).then_inc(x_first[k % NX_BUF], 16)

            def batch(b, last):
                sp.wait_ge(s["zT_ready"], ZT0 + (b + 1) * 2 * ST_)
                sp.sem_inc(s["sp_turn"], 1)
                for p in range(2, 8):
                    load_w(b * N_WCHUNK + p, p, p % 2)
                    if p in (2, 3):
                        store_k(b, p - 2)
                    if p in (4, 7):
                        g = p // 7
                        sp.wait_ge(s["k_out"], b * 64 + 64)
                        sp.sem_inc(s["sp_turn"], 1)
                        sp.wait_ge(s["st_ready"], ST0 + b * NG * 2 * NU)
                        sp.sem_inc(s["sp_turn"], 1)
                        if g == 1:
                            row_max(b, 0, 0)
                        stack_keys(b, g, g)
                        for c in range(2 - g):
                            sp.wait_ge(s["q_lo"], b * RB + 4 + 2 * g + c + 1)
                            stack_queries(b * 2 * NG + g * 2 + c, g, c)
                over_groups(b, sp, group, last)

            batches(sp, batch)
            for qc in range(NQC):
                sp.wait_ge(o_stored[qc], DMA0 + 16 * B * NG)
            for par in range(2):
                sp.wait_ge(w_loaded[par], 16 * (B * N_WCHUNK // 2 + 1))

        @block.gpsimd
        def _(pool):
            def reciprocal_deviation(tile, k):
                pool.wait_ge(s["stats"], tile + 1)
                pool.tensor_tensor(mv[k % 2][:, 3:4], mv[k % 2][:, 2:3], nhalf[:, :], ALU.pow).then_inc(s["pow"], 1)

            def copy_v(b, g, par):
                pool.sem_inc(s["pool_turn"], 1)
                pool.tensor_copy(vg[par][:, :, :], vall[:, :, ds(g * HD, HD)]).then_inc(s["vg_ready"], 1)

            def group(order, b, g, gh, par, u):
                n = b * NG + g
                for what, e, *half in order:
                    if what == "ST" and half == [1] and e in DIAGONAL:
                        off = unit_offset(e)
                        pool.wait_ge(s["exp_done"], E0 + (n * NU + e) * 2 + 2)
                        pool.sem_inc(s["pool_turn"], 1)
                        blk = prob[e % 2][:, :, off:off + P]
                        pool.affine_select(out=blk, in_=blk, compare_op=ALU.is_ge, fill=0.0, base=0,
                                           pattern=[[0, GH], [1, P]], channel_multiplier=-1)\
                            .then_inc(s["mask_done"], 1)
                    if what == "XS":
                        reciprocal_deviation((b + 1) * ST_ + e, e)
                if order is body:
                    pool.wait_ge(s["pv_done"], PV0 + n * NU + NU)
                    copy_v(b, g + 2, par)

            pool.memset(ident[:, :], 0.0)
            pool.memset(negmask[:, :], 0.0)
            pool.memset(ones[:, :], 1.0)
            pool.memset(nhalf[:, :], -0.5)
            pool.drain()
            for i in range(2):
                pool.memset(kst[i][96:97, :].bitcast(F32), -1.0)
            pool.drain()
            pool.affine_select(out=ident[:, :], in_=ident[:, :], compare_op=ALU.not_equal, fill=1.0, base=0,
                               pattern=[[-1, P]], channel_multiplier=1)
            pool.affine_select(out=negmask[:, :], in_=negmask[:, :], compare_op=ALU.is_ge, fill=MASKED, base=0,
                               pattern=[[-1, P]], channel_multiplier=1)
            pool.drain()
            pool.tensor_copy(identb[:, :], ident[:, :])
            pool.drain().then_inc(s["const"], 1)
            for k in range(ST_):
                reciprocal_deviation(k, k)

            def batch(b, last):
                pool.wait_ge(s["v_ready"], b * 4 + 4)
                copy_v(b, 0, 0)
                copy_v(b, 1, 1)
                over_groups(b, pool, group, last)

            batches(pool, batch)

        @block.scalar
        def _(act):
            def w_hi(n, half_n, par):
                act.wait_ge(w_loaded[par], half_n * 16 + 16)
                act.wait_ge(s["roped"], 2 * n + 2)
                act.activation(w[par][0][:, :, :], wraw[par][:, :, :], ACT.Copy).then_inc(s["w_hi"], 1)

            def xT_hi(tile, k, banks):
                for half in range(2):
                    act.wait_ge(s["zT_ready"], ZT0 + tile * 2 + half + 1)
                    act.activation(xT[0][:, 4 * half:4 * half + 4, k * P:(k + 1) * P],
                                   banks(k, half).rearrange("p (k n) -> p k n", n=P), ACT.Copy).then_inc(s["zT_hi"], 1)

            def part_hi(n, c):
                act.wait_ge(s["roped"], R0 + 2 * n + c + 1)
                act.activation(stg[0][:, c * BANK:(c + 1) * BANK], rot[c][:, :], ACT.Copy).then_inc(s["q_hi"], 1)

            def group(order, b, g, gh, par, u):
                n = b * NG + g
                for what, k, *part in order:
                    if what == "ST":
                        off = unit_offset(k)
                        half = part[0]
                        if half == 0:
                            act.wait_ge(s["pv_done"], n * NU + k + 1)
                        act.wait_ge(s["st_ready"], ST0 + (n * NU + k) * 2 + half + 1)
                        act.activation(prob[k % 2][:, 2 * half:2 * half + 2, off:], pst[:, half, :, off:],
                                       ACT.Exp, scale=scale).then_inc(s["exp_done"], 1)
                    if what == "PV" and part == [1] and k in CHUNK_END:
                        q = n * 2 + CHUNK_END.index(k)
                        act.wait_ge(s["pv_done"], PV0 + n * NU + k + 1)
                        act.wait_ge(s["norm_done"], q + 1)
                        act.copy(pvs[:, :], ppv[:, :]).then_inc(s["acc_copied"], 1)
                        act.copy(dens[:, :], pden[:, :]).then_inc(s["acc_copied"], 1)
                    if what == "WS":
                        w_hi(b * N_WCHUNK + g + 7, b * 6 + gh + 3 + par, 1 - par)
                    if what == "XC":
                        xT_hi((b + 1) * ST_ + k, k, psh_banks)
                    if what == "HI" and k == 0:
                        act.wait_ge(stacked[1 - par][0], (b * 4 + gh + par + 1) * QS)
                        part_hi(b * N_WCHUNK + g + 6, 0)
                    if what == "HI" and k == 1:
                        act.wait_ge(stacked[par][1], (b * 4 + gh + 1) * QS)
                        part_hi(b * N_WCHUNK + g + 5, 1)

            act.drain().then_inc(s["exp_done"], E0)
            act.drain().then_inc(s["acc_copied"], AC0)
            for k in range(ST_):
                xT_hi(k, k, pst_banks)
                if k == 1:
                    w_hi(0, 0, 0)

            def batch(b, last):
                for p in range(6):
                    w_hi(b * N_WCHUNK + p + 1, b * 6 + (p + 1) // 2, (p + 1) % 2)
                    if p == 1:
                        act.wait_ge(s["k_out"], b * 64 + 32)
                    if p == 2:
                        act.wait_ge(s["k_out"], b * 64 + 64)
                    if p == 5:
                        act.wait_ge(stacked[0][0], (b * 4 + 1) * QS)
                    if p not in VALUES:
                        for c in range(2 if p < 5 else 1):
                            part_hi(b * N_WCHUNK + p, c)
                over_groups(b, act, group, last)

            batches(act, batch)

        @block.vector
        def _(dve):
            def w_lo(n, par):
                dve.wait_ge(s["w_hi"], n + 1)
                dve.tensor_tensor(w[par][1][:, :, :], wraw[par][:, :, :], w[par][0][:, :, :].bitcast(F32),
                                  ALU.subtract).then_inc(s["w_ready"], 1)

            def statistics(buf, k):
                for i in range(2):
                    dve.bn_stats(stat[k % 2][:, i, :], buf[:, i * BANK:(i + 1) * BANK])
                dve.drain()
                dve.bn_aggr(mv[k % 2][:, 0:2], stat[k % 2][:, :, :])
                dve.drain()
                dve.tensor_scalar(mv[k % 2][:, 2:3], mv[k % 2][:, 1:2], LN_EPS, None, ALU.add)\
                    .then_inc(s["stats"], 1)

            def normalise(tile, buf, k):
                dve.wait_ge(s["pow"], tile + 1)
                dve.tensor_scalar(buf, buf, mv[k % 2][:, 0:1], mv[k % 2][:, 3:4], ALU.subtract, ALU.mult)\
                    .then_inc(s["z_ready"], 1)

            def xT_lo(tile, k, banks):
                for half in range(2):
                    dve.wait_ge(s["zT_hi"], tile * 2 + half + 1)
                    at = (slice(None), slice(4 * half, 4 * half + 4), slice(k * P, (k + 1) * P))
                    dve.tensor_tensor(xT[1][at], banks(k, half).rearrange("p (k n) -> p k n", n=P),
                                      xT[0][at].bitcast(F32), ALU.subtract).then_inc(s["zT_evac"], 1)

            def rotate(u, at, c):
                dve.drain()
                dve.wait_ge(s["sh_ready"], u + 1)
                dve.tensor_tensor(rot[c][:, :], bank(at), cos[:, c * BANK:(c + 1) * BANK], ALU.mult)
                dve.stream_shuffle(swp[c][:, :], bank(at), swap).then_inc(s["sh_free"], 1)
                dve.drain()
                dve.tensor_tensor(swp[c][:, :], swp[c][:, :], sin[:, c * BANK:(c + 1) * BANK], ALU.mult)
                dve.drain()
                dve.tensor_tensor(rot[c][:, :], rot[c][:, :], swp[c][:, :], ALU.add).then_inc(s["roped"], 1)

            def part_lo(r, c):
                cols = slice(c * BANK, (c + 1) * BANK)
                dve.wait_ge(s["q_hi"], r + 1)
                dve.tensor_tensor(stg[1][:, cols], rot[c][:, :], stg[0][:, cols].bitcast(F32), ALU.subtract)\
                    .then_inc(s["q_lo"], 1)

            def maximum(u, at, k):
                qt, kc, n, heads, _ = USES[k]
                m = len(heads)
                dve.wait_ge(s["sh_ready"], u + 1)
                dve.tensor_reduce(mx_hq[kc][:, heads[0]:heads[0] + m, qt],
                                  psh[:, at, 0:m * n].rearrange("p (m n) -> p m n", n=n), AX.X, ALU.max)\
                    .then_inc(s["sh_free"], 1)

            def max_rows(u, at):
                dve.tensor_tensor(mx_hq[0][:, :, 4:], mx_hq[0][:, :, 4:], mx_hq[1][:, :, 4:], ALU.max)\
                    .then_inc(s["mx_ready"], 1)
                dve.wait_ge(s["sh_ready"], u + 1)
                dve.tensor_copy(mT[:, :], psh[0:GH * ST_, at, 0:P]).then_inc(s["sh_free"], 1)
                dve.drain().then_inc(s["mT_ready"], 1)

            def group(order, b, g, gh, par, u):
                n = b * NG + g
                for step in order:
                    what, k = step[:2]
                    if what == "P" and step[-1] == PIECES - 1:
                        i, at, _ = plan[id(order)][step[:-1]]
                        rotate(u + i, at, 0 if k == "next" else k)
                    if what == "S":
                        i, at, _ = plan[id(order)][step]
                        maximum(u + i, at, k)
                    if what == "MT":
                        i, at, _ = plan[id(order)][step]
                        dve.drain()
                        dve.wait_ge(s["m_out"], DMA0 + (n + 1) * 16)
                        max_rows(u + i, at)
                    if what == "XS":
                        i = k % NX_AHEAD
                        dve.wait_ge(x_loaded[i], (b * (ST_ // NX_AHEAD) + k // NX_AHEAD) * 16 + 16)
                        statistics(x_next[i], k)
                    if what == "XN":
                        normalise((b + 1) * ST_ + k, x_next[k % NX_AHEAD], k)
                    if what == "XC":
                        xT_lo((b + 1) * ST_ + k, k, psh_banks)
                    if what == "LO":
                        part_lo(b * RB + 4 + (g + 2 - k) * 2 + k, k)
                    if what == "WS":
                        w_lo(b * N_WCHUNK + g + 7, 1 - par)
                    if what == "NORM":
                        q = n * 2 + k
                        dve.drain()
                        dve.wait_ge(s["acc_copied"], AC0 + 2 * q + 2)
                        dve.reciprocal(dens[:, :], dens[:, :])
                        dve.drain()
                        dve.wait_ge(o_stored[k], DMA0 + n * 16)
                        dve.tensor_tensor(oT[k][:, :], pvs[:, :], dens[:, :], ALU.mult).then_inc(s["norm_done"], 1)

            dve.drain().then_inc(s["zT_evac"], ZT0)
            dve.drain().then_inc(s["w_ready"], W0)
            dve.drain().then_inc(s["sh_free"], SH0)
            dve.drain().then_inc(s["roped"], R0)
            dve.drain().then_inc(s["norm_done"], N0)
            for k in range(ST_ + 2):
                if k < ST_:
                    dve.wait_ge(x_first[k % NX_BUF], k // NX_BUF * 16 + 16)
                    statistics(xbuf[k % NX_BUF], k)
                if 1 <= k <= ST_:
                    normalise(k - 1, xbuf[(k - 1) % NX_BUF], k - 1)
                if k >= 2:
                    xT_lo(k - 2, k - 2, pst_banks)
                if k == 3:
                    w_lo(0, 0)
            dve.wait_ge(s["table"], 32)
            rotate(0, 0, 0)

            def batch(b, last):
                w_lo(b * N_WCHUNK + 1, 1)
                for step in pro:
                    what, p = step[:2]
                    if what == "P":
                        c, piece = step[2:]
                        if piece < PIECES - 1:
                            continue
                        i, at, _ = plan_pro[step[:-1]]
                        u = 1 + b * U_BATCH + i
                        if c == 0:
                            w_lo(b * N_WCHUNK + p + 1, (p + 1) % 2)
                        if p in VALUES:
                            dve.wait_ge(s["sh_ready"], u + 1)
                            dve.tensor_copy(vT[:, c * BANK:(c + 1) * BANK], bank(at)).then_inc(s["sh_free"], 1)
                            dve.drain().then_inc(s["roped"], 1)
                        else:
                            rotate(u, at, c)
                        if c == 1 and p not in VALUES:
                            for h in range(2 if p < 5 else 1):
                                part_lo(b * RB + 2 * LO_ORDER.index(p) + h, h)
                    if what == "VT":
                        i, at, _ = plan_pro[step]
                        c = step[2]
                        dve.wait_ge(s["sh_ready"], 1 + b * U_BATCH + i + 1)
                        dve.tensor_copy(vall[:, 4 * c:4 * c + 4, (p - VALUES[0]) * P:(p - VALUES[0] + 1) * P],
                                        bank(at).rearrange("p (k n) -> p k n", n=P)).then_inc(s["sh_free"], 1)
                        dve.drain().then_inc(s["v_ready"], 1)
                    if what == "S":
                        i, at, _ = plan_pro[step]
                        maximum(1 + b * U_BATCH + i, at, p)
                    if what == "MT":
                        i, at, _ = plan_pro[step]
                        dve.drain()
                        dve.wait_ge(s["m_out"], DMA0 + b * NG * 16)
                        max_rows(1 + b * U_BATCH + i, at)
                over_groups(b, dve, group, last)

            batches(dve, batch)

        @block.tensor
        def _(pe):
            def project(n, u, where, par, c, piece):
                _, at, prev = where
                if piece == 0:
                    pe.wait_ge(s["w_ready"], W0 + n + 1)
                    pe.wait_ge(s["sh_free"], SH0 + u + prev + 1)
                passes = [(k, a, x) for k in range(KC) for a, x in ((0, 0), (0, 1), (1, 0))]
                step = len(passes) // PIECES
                for i in range(piece * step, (piece + 1) * step):
                    k, a, x = passes[i]
                    mm = pe.matmul(bank(at), w[par][a][:, k, :], xT[x][:, k, c * BANK:(c + 1) * BANK],
                                   start=(i == 0), stop=(i == len(passes) - 1))
                if piece == PIECES - 1:
                    mm.then_inc(s["sh_ready"], 1)

            def x_transposes(tile, k, buf, banks, n_banks):
                pe.wait_ge(s["z_ready"], tile + 1)
                for half in range(2):
                    pe.wait_ge(s["zT_evac"], ZT0 + tile * 2 + half + 1 - n_banks)
                    for i in range(4):
                        tr = pe.transpose(banks(k, half)[:, i * P:(i + 1) * P],
                                          buf[:, (4 * half + i) * P:(4 * half + i + 1) * P], ident[:, :])
                    tr.then_inc(s["zT_ready"], 1)

            def row_scores(u, where, par, k):
                _, at, prev = where
                qt, kc, n, heads, last = USES[k]
                pe.wait_ge(s["sh_free"], SH0 + u + prev + 1)
                for i, h in enumerate(heads):
                    mm = pe.matmul(psh[:, at, i * n:(i + 1) * n], qst[par][0:96, h, qt * P:(qt + 1) * P],
                                   kst[par][0:96, kc * BANK:kc * BANK + n], start=True, stop=not last,
                                   skip_group_check=True)
                    if last:
                        mm = pe.matmul(psh[:, at, (i + 1) * n - P:(i + 1) * n], identb[:, :], negmask[:, :],
                                       start=False, stop=True, skip_group_check=True)
                mm.then_inc(s["sh_ready"], 1)

            def transpose_max(n, u, where):
                _, at, prev = where
                pe.wait_ge(s["mx_ready"], n + 1)
                pe.wait_ge(s["sh_free"], SH0 + u + prev + 1)
                pe.transpose(psh[0:GH * ST_, at, 0:P], mx[:, 0, :], ident[:, :]).then_inc(s["sh_ready"], 1)

            def group(order, b, g, gh, par, u):
                n = b * NG + g
                for step in order:
                    what, k = step[:2]
                    if what == "XT":
                        if k == 0:
                            pe.wait_ge(s["sh_free"], SH0 + u)
                            pe.sem_inc(s["pe_turn"], 1)
                        x_transposes((b + 1) * ST_ + k, k, x_next[k % NX_AHEAD], psh_banks, 2)
                    if what == "P" and k == "next":
                        if step[-1] == 0:
                            pe.wait_ge(s["zT_evac"], ZT0 + (b + 2) * 2 * ST_)
                            pe.sem_inc(s["pe_turn"], 1)
                        project((b + 1) * N_WCHUNK, u, plan[id(order)][step[:-1]], 0, 0, step[-1])
                    elif what == "P":
                        project(b * N_WCHUNK + g + 6, u, plan[id(order)][step[:-1]], par, k, step[-1])
                    if what == "S":
                        if k == 0:
                            pe.wait_ge(k_stacked[1 - par], (b * 4 + gh + par + 1) * KS)
                        if k in (0, SECOND_HALF):
                            pe.wait_ge(stacked[1 - par][int(k > 0)], (b * 4 + gh + par + 1) * QS)
                        row_scores(u, plan[id(order)][step], 1 - par, k)
                    if what == "MT":
                        transpose_max(n + 1, u, plan[id(order)][step])
                    if what == "ST":
                        qc, ki = UNITS[k]
                        half = step[2]
                        off = min(unit_offset(k), BANK // 2)
                        if k == 0 and half == 0:
                            pe.wait_ge(max_row[par], (b * 4 + gh + 1) * 16)
                        pe.wait_ge(s["exp_done"], (n * NU + k) * 2 + half + 1)
                        for hh in range(2):
                            mm = pe.matmul(pst[:, half, hh, off:], kst[par][0:97, ki * P:(ki + 1) * P],
                                           qst[par][0:97, 2 * half + hh, qc * BANK + off:(qc + 1) * BANK],
                                           start=True, stop=True)
                        mm.then_inc(s["st_ready"], 1)
                    if what == "PV":
                        qc, ki = UNITS[k]
                        off = unit_offset(k)
                        part = step[2]
                        if part == 0:
                            if k == 0:
                                pe.wait_ge(s["vg_ready"], n + 1)
                            if k in DIAGONAL:
                                pe.wait_ge(s["mask_done"], n * len(DIAGONAL) + DIAGONAL.index(k) + 1)
                            else:
                                pe.wait_ge(s["exp_done"], E0 + (n * NU + k) * 2 + 2)
                            if ki == 0:
                                pe.wait_ge(s["acc_copied"], (n * 2 + qc) * 2 + 2)
                        acc, lhs = ((ppv, vg[par][:, ki, :]), (pden, ones[:, :]))[part]
                        for h in range(GH):
                            mm = pe.matmul(acc[h * HD:(h + 1) * HD, off:], lhs, prob[k % 2][:, h, off:],
                                           start=(ki == 0), stop=(ki == 4 * qc + 3), skip_group_check=True)
                        if part == 1:
                            mm.then_inc(s["pv_done"], 1)

            pe.wait_ge(s["const"], 1)
            pe.sem_inc(s["zT_ready"], ZT0)
            pe.sem_inc(s["pv_done"], PV0)
            pe.sem_inc(s["st_ready"], ST0)
            for k in range(ST_):
                x_transposes(k, k, xbuf[k % NX_BUF], pst_banks, 4)
                if k >= ST_ // 2:
                    if k == ST_ // 2:
                        pe.wait_ge(s["zT_evac"], ZT0 + ST_)
                    for i in range(2 * PIECES // ST_):
                        project(0, 0, (0, 0, -1), 0, 0, (k - ST_ // 2) * 2 * PIECES // ST_ + i)

            def batch(b, last):
                pe.wait_ge(s["exp_done"], E0 + b * NG * NU * 2)
                pe.sem_inc(s["pe_turn"], 1)
                pe.wait_ge(s["zT_evac"], ZT0 + (b + 1) * 2 * ST_)
                pe.sem_inc(s["pe_turn"], 1)
                for step in pro:
                    what, p = step[:2]
                    u = 1 + b * U_BATCH
                    if what == "P":
                        project(b * N_WCHUNK + p, u, plan_pro[step[:-1]], p % 2, step[2], step[3])
                    if what == "VT":
                        _, at, prev = plan_pro[step]
                        c = step[2]
                        if c == 0:
                            pe.wait_ge(s["roped"], R0 + (b * N_WCHUNK + p) * 2 + 2)
                        pe.wait_ge(s["sh_free"], SH0 + u + prev + 1)
                        for k in range(4):
                            tr = pe.transpose(psh[:, at, k * P:(k + 1) * P],
                                              vT[:, (4 * c + k) * P:(4 * c + k + 1) * P], ident[:, :])
                        tr.then_inc(s["sh_ready"], 1)
                    if what == "S":
                        if p == 0:
                            pe.wait_ge(k_stacked[0], (b * 4 + 1) * KS)
                        if p in (0, SECOND_HALF):
                            pe.wait_ge(stacked[0][int(p > 0)], (b * 4 + 1) * QS)
                        row_scores(u, plan_pro[step], 0, p)
                    if what == "MT":
                        transpose_max(b * NG, u, plan_pro[step])
                pe.wait_ge(s["sh_free"], SH0 + 1 + b * U_BATCH + U_PRO)
                pe.sem_inc(s["pe_turn"], 1)
                over_groups(b, pe, group, last)

            batches(pe, batch)


def output_projection(nc, sem, layer, oT_d, wo, x_in, x_out):
    s = {n: sem(f"o{layer}_{n}") for n in (
        *(f"wl{k}" for k in range(KC)), "w_hi", "w_lo", "ol0", "ol1", "o_hi", "o_lo", "x0", "x1", "mm", "sum", "st0", "st1")}
    w_loaded, o_loaded, x_loaded, stored = ([s[f"wl{k}"] for k in range(KC)], (s["ol0"], s["ol1"]), (s["x0"], s["x1"]),
                                            (s["st0"], s["st1"]))
    M0, L0, S0, DMA0 = 8, 2, 4, 16
    TURNS = NT // 4
    with ExitStack() as ctx:
        def sb(name, shape, dt=F32):
            return ctx.enter_context(nc.sbuf_tensor(f"o{layer}_{name}", shape, dt))

        wraw = [sb(f"wraw{k}", [P, D]) for k in range(KC)]
        w = [sb(f"w_{n}", [P, KC, D], F32R) for n in ("hi", "lo")]
        oraw = [sb(f"oraw{i}", [P, NG, 2 * P]) for i in range(2)]
        o = [[sb(f"o_{n}{i}", [P, NG, 2 * P], F32R) for n in ("hi", "lo")] for i in range(2)]
        xres = [sb(f"xres{i}", [P, D]) for i in range(2)]
        pout = ctx.enter_context(nc.psum_tensor(f"o{layer}_pout", [P, 2, 2, BANK], F32))
        block = ctx.enter_context(nc.Block())

        @block.sync
        def _(sp):
            def load_w(k):
                sp.dma_start(wraw[k][:, :], wo[k * P:(k + 1) * P, :]).then_inc(w_loaded[k], 16)

            def load_o(i, par):
                sp.wait_ge(s["o_lo"], i + 1)
                sp.dma_start(oraw[par][:, :, :].rearrange("p g (t n) -> p g t n", n=P),
                             oT_d[:, :, ds(i * 2, 2), :].rearrange("g p t n -> p g t n")).then_inc(o_loaded[par], 16)

            for i in range(2):
                sp.sem_inc(stored[i], DMA0)
            load_w(0)
            load_o(0, 0)
            for k in range(1, KC):
                load_w(k)
            load_o(1, 1)

            def turn(j, more):
                for q in range(4):
                    sp.wait_ge(stored[q % 2], DMA0 + (j * 2 + q // 2) * 16)
                    sp.dma_start(xres[q % 2][:, :], x_in[ds((j * 4 + q) * P, P), :]).then_inc(x_loaded[q % 2], 16)
                    if q % 2 == 1:
                        sp.wait_ge(s["sum"], S0 + (j * 4 + q) * 2)
                        sp.dma_start(x_out[ds((j * 4 + q - 1) * P, P), :], xres[0][:, :]).then_inc(stored[0], 16)
                        if more:
                            load_o(j * 2 + 2 + q // 2, q // 2)
                        sp.wait_ge(s["sum"], S0 + (j * 4 + q) * 2 + 2)
                        sp.dma_start(x_out[ds((j * 4 + q) * P, P), :], xres[1][:, :]).then_inc(stored[1], 16)

            with sp.Fori(0, TURNS - 1) as j:
                turn(j, True)
            turn(TURNS - 1, False)
            for i in range(2):
                sp.wait_ge(stored[i], DMA0 + 16 * NT // 2)

        @block.scalar
        def _(act):
            def o_hi(i, i_half, par):
                act.wait_ge(o_loaded[par], i_half * 16 + 16)
                act.wait_ge(s["mm"], M0 - 4 + i * 4)
                act.activation(o[par][0][:, :, :], oraw[par][:, :, :], ACT.Copy).then_inc(s["o_hi"], 1)

            for k in range(KC):
                act.wait_ge(w_loaded[k], 16)
                act.activation(w[0][:, k, :], wraw[k][:, :], ACT.Copy).then_inc(s["w_hi"], 1)
                if k == 0:
                    o_hi(0, 0, 0)
            with act.Fori(0, TURNS - 1) as j:
                o_hi(j * 2 + 1, j, 1)
                o_hi(j * 2 + 2, j + 1, 0)
            o_hi(NT // 2 - 1, TURNS - 1, 1)

        @block.vector
        def _(dve):
            def o_lo(i, par):
                dve.wait_ge(s["o_hi"], i + 1)
                dve.tensor_tensor(o[par][1][:, :, :], oraw[par][:, :, :], o[par][0][:, :, :].bitcast(F32),
                                  ALU.subtract).then_inc(s["o_lo"], 1)

            dve.drain().then_inc(s["o_lo"], L0)
            dve.drain().then_inc(s["sum"], S0)
            for k in range(KC):
                dve.wait_ge(s["w_hi"], k + 1)
                dve.tensor_tensor(w[1][:, k, :], wraw[k][:, :], w[0][:, k, :].bitcast(F32), ALU.subtract)\
                    .then_inc(s["w_lo"], 1)
                if k == 0:
                    o_lo(0, 0)

            def turn(j, more):
                for q in range(4):
                    if q == 0:
                        o_lo(j * 2 + 1, 1)
                    if q == 2 and more:
                        o_lo(j * 2 + 2, 0)
                    dve.wait_ge(x_loaded[q % 2], (j * 2 + q // 2) * 16 + 16)
                    for half in range(2):
                        cols = slice(half * BANK, (half + 1) * BANK)
                        dve.wait_ge(s["mm"], M0 + (j * 4 + q) * 2 + half + 1)
                        dve.tensor_tensor(xres[q % 2][:, cols], xres[q % 2][:, cols], pout[:, q % 2, half, :],
                                          ALU.add).then_inc(s["sum"], 1)

            with dve.Fori(0, TURNS - 1) as j:
                turn(j, True)
            turn(TURNS - 1, False)

        @block.tensor
        def _(pe):
            pe.sem_inc(s["mm"], M0)

            def turn(j, first=False):
                for q in range(4):
                    par = q // 2
                    if q % 2 == 0:
                        pe.wait_ge(s["o_lo"], L0 + j * 2 + par + 1)
                    groups = [[(k, half, a, x) for k in range(KC) for a, x in ((0, 0), (0, 1), (1, 0))]
                              for half in range(2)]
                    if first and q == 0:
                        groups = [[(k, half, a, x) for k in range(KC) for half in range(2)
                                   for a, x in ((0, 0), (0, 1), (1, 0))]]
                    for products in groups:
                        pe.wait_ge(s["sum"], (j * 4 + q) * 2 + products[-1][1] + 1)
                        for i, (k, half, a, x) in enumerate(products):
                            if len(groups) == 1 and i % 6 == 0:
                                pe.wait_ge(s["w_lo"], k + 1)
                            mm = pe.matmul(pout[:, q % 2, half, :], o[par][a][:, k, (q % 2) * P:(q % 2 + 1) * P],
                                           w[x][:, k, half * BANK:(half + 1) * BANK],
                                           start=(k == 0 and (a, x) == (0, 0)), stop=(k == KC - 1 and a == 1),
                                           skip_group_check=True)
                            if k == KC - 1 and a == 1:
                                mm.then_inc(s["mm"], 1)

            turn(0, True)
            with pe.Fori(1, TURNS) as j:
                turn(j)


NS = 4
C = D // NS
NL = NS * NS + 2 * NS
SINKHORN_ITERS = 50
TAU = 0.1


def mixing_layer(nc, sem, oT_d, wo, x_in, w24, base24, gate, w_branch, x_out):
    s = {n: sem(f"h_{n}") for n in (
        "const", "small", *(f"wl{k}" for k in range(KC)), "w_hi", "w_lo", "ol0", "ol1", "o_hi", "o_lo", "x0", "x1", "mm", "sum",
        "stats", "rstd", "rms_in", "rms", "z", "zT_ready", "zT", "logit", "read", "gate", "e_in", "e_out",
        "pp", "z2", "dp", "pre_ready", "preT", "y_ready", "y", "h_res", "dm", "mix", "mixed", "stored")}
    w_loaded, o_loaded, x_loaded = [s[f"wl{k}"] for k in range(KC)], (s["ol0"], s["ol1"]), (s["x0"], s["x1"])
    M0, L0, S0, ZR0, ZT0, LG0, RD0, MX0, DMA0 = 4, 2, 2, 4, 2, 2, 2, 2, 16
    PR0, PT0, YR0, Y0, MI0 = 1, 1, 1, 1, 2
    HALF = NS // 2
    with ExitStack() as ctx:
        def sb(name, shape, dt=F32):
            return ctx.enter_context(nc.sbuf_tensor(f"h_{name}", shape, dt))

        ident = sb("ident", [P, P])
        x = sb("x", [P, NT, D])
        wraw = [x[:, NT - KC + k, :] for k in range(KC)]
        w = sb("w", [P, 2, KC, D], F32R)
        oraw = sb("oraw", [P, 2, NG, P])
        o = sb("o", [P, 2, 2, NG, P], F32R)
        z = [sb(f"z{i}", [P, D]) for i in range(2)]
        stat = [sb(f"stat{i}", [P, 2, 6]) for i in range(2)]
        mvt = [sb(f"mvt{i}", [P, 4]) for i in range(2)]
        mv = sb("mv", [P, NT, 4])
        nhalf = sb("nhalf", [P, NT])
        nmr, rstd, rms, rms_e = (sb(n, [P, NT]) for n in ("nmr", "rstd", "rms", "rms_e"))
        zT = [sb(f"zT{i}", [P, KC, P]) for i in range(2)]
        w24_sb = sb("w24", [P, KC, NL])
        base = sb("base", [P, NL])
        wb = sb("wb", [P, C // P, C])
        lg = sb("lg", [P, NT, NL])
        m = sb("m", [P, NT, NS * NS])
        e = sb("e", [P, NT, NS * NS])
        pp = sb("pp", [P, NT, 2, NS])
        r64 = sb("r64", [P, NT, NS])
        sums = sb("sums", [P, NT, 2])
        g = sb("g", [P, 4])
        preT = sb("preT", [P, C // P, P])
        dg = [sb(f"dg{i}", [P, HALF * (NS + 1), P]) for i in range(2)]
        z_all = w[:, :, :, :].rearrange("p a k n -> p (a k) n").bitcast(F32)
        y_all = o[:, :, :, :, :].rearrange("p a b k n -> p (a b k n)")[:, 0:NT * C].bitcast(F32)\
            .rearrange("p (t n) -> p t n", n=C)
        pout = ctx.enter_context(nc.psum_tensor("h_pout", [P, 2, BANK], F32))
        pz = ctx.enter_context(nc.psum_tensor("h_pz", [P, 2, BANK], F32))
        plg = ctx.enter_context(nc.psum_tensor("h_plg", [P, 2, BANK], F32))
        ppre = ctx.enter_context(nc.psum_tensor("h_ppre", [P, BANK], F32))
        py = ctx.enter_context(nc.psum_tensor("h_py", [P, BANK], F32))
        block = ctx.enter_context(nc.Block())

        def lines(buf, axis):
            return buf[:, :, :].rearrange("p t (i j) -> p t i j" if axis == "row" else "p t (i j) -> p t j i", j=NS)

        def spread(v, n=NS):
            return v.unsqueeze(3).broadcast_to([P, NT, v.shape[2], n])

        def tile(buf, t):
            return buf[:, ds(t, 1), :].rearrange("p o n -> p (o n)")

        def turns(eng, turn):
            turn(0, 0, 0, True, False)
            turn(1, 0, 1, True, False)
            with eng.Fori(1, NT // 2 - 1) as j:
                for par in range(2):
                    turn(j * 2 + par, j, par, False, False)
            for par in range(2):
                turn(NT - 2 + par, NT // 2 - 1, par, False, par == 1)

        @block.sync
        def _(sp):
            def load_w(k):
                sp.dma_start(wraw[k], wo[k * P:(k + 1) * P, :]).then_inc(w_loaded[k], 16)

            def load_o(t, j, par):
                sp.wait_ge(s["o_lo"], t + 1)
                sp.dma_start(oraw[:, par, :, :],
                             oT_d[:, :, ds(t, 1), :].rearrange("g p o n -> p g (o n)")).then_inc(o_loaded[par], 16)

            def load_x(t, j, par):
                sp.wait_ge(x_loaded[par], DMA0 + j * 16)
                sp.dma_start(tile(x, t), x_in[ds(t * P, P), :]).then_inc(x_loaded[par], 16)

            for i in range(2):
                sp.sem_inc(x_loaded[i], DMA0)
            load_w(0)
            load_o(0, 0, 0)
            for k in range(1, KC):
                load_w(k)
            load_x(0, 0, 0)
            load_o(1, 0, 1)
            load_x(1, 0, 1)
            for dst, src in ((w24_sb[:, :, :], w24), (base[:, :], base24), (g[:, 0:1], gate),
                             (wb[:, :, :], w_branch.rearrange("(c p) n -> p c n", p=P))):
                sp.dma_start(dst, src).then_inc(s["small"], 16)
            sp.wait_ge(s["w_lo"], KC)
            with sp.Fori(1, NT // 2) as j:
                for par in range(2):
                    load_o(j * 2 + par, j, par)
                    load_x(j * 2 + par, j, par)
            with sp.Fori(0, NT) as t:
                sp.wait_ge(s["mixed"], MX0 + t + 1)
                sp.dma_start(x_out[ds(t * P, P), :], tile(x, t)).then_inc(s["stored"], 16)
            sp.wait_ge(s["stored"], 16 * NT)

        @block.gpsimd
        def _(pool):
            pool.memset(ident[:, :], 0.0)
            pool.memset(nhalf[:, :], -0.5)
            pool.drain()
            pool.affine_select(out=ident[:, :], in_=ident[:, :], compare_op=ALU.not_equal, fill=1.0, base=0,
                               pattern=[[-1, P]], channel_multiplier=1).then_inc(s["const"], 1)
            with pool.Fori(0, NT // 2) as j:
                for par in range(2):
                    pool.wait_ge(s["stats"], j * 2 + par + 1)
                    pool.tensor_tensor(mvt[par][:, 3:4], mvt[par][:, 2:3], nhalf[:, 0:1], ALU.pow)\
                        .then_inc(s["rstd"], 1)
            pool.wait_ge(s["rms_in"], 1)
            pool.tensor_tensor(rms[:, :], rms_e[:, :], nhalf[:, :], ALU.pow).then_inc(s["rms"], 1)

        @block.scalar
        def _(act):
            def o_hi(t, j, par):
                act.wait_ge(o_loaded[par], j * 16 + 16)
                act.wait_ge(s["mm"], 2 * t + 2)
                act.activation(o[:, par, 0, :, :], oraw[:, par, :, :], ACT.Copy).then_inc(s["o_hi"], 1)

            def copy_zT(t, par):
                for half in range(2):
                    act.wait_ge(s["logit"], t + 1)
                    act.wait_ge(s["zT_ready"], ZR0 + t * 2 + half + 1)
                    act.activation(zT[par][:, 4 * half:4 * half + 4, :],
                                   pz[:, half, :].rearrange("p (k n) -> p k n", n=P), ACT.Copy).then_inc(s["zT"], 1)

            def copy_logits(t, par):
                act.wait_ge(s["logit"], LG0 + t + 1)
                act.activation(tile(lg, t), plg[:, par, 0:NL], ACT.Copy).then_inc(s["read"], 1)

            act.drain().then_inc(s["zT"], ZT0)
            act.drain().then_inc(s["read"], RD0)
            act.drain().then_inc(s["preT"], PT0)
            act.drain().then_inc(s["y"], Y0)
            for k in range(KC):
                act.wait_ge(w_loaded[k], 16)
                act.activation(w[:, 0, k, :], wraw[k], ACT.Copy).then_inc(s["w_hi"], 1)
                if k == 0:
                    o_hi(0, 0, 0)

            def turn(t, j, par, first, last):
                if not last:
                    o_hi(t + 1, j + par, 1 - par)
                if not first or par == 1:
                    copy_zT(t - 1, 1 - par)
                if not first:
                    copy_logits(t - 2, par)

            turns(act, turn)
            copy_zT(NT - 1, 1)
            copy_logits(NT - 2, 0)
            copy_logits(NT - 1, 1)
            act.wait_ge(s["small"], 64)
            act.activation(g[:, 1:2], g[:, 0:1], ACT.Exp, scale=-1.0).then_inc(s["gate"], 1)
            act.wait_ge(s["e_in"], 1)
            act.activation(pp[:, :, :, :], pp[:, :, :, :], ACT.Exp).then_inc(s["e_out"], 1)
            act.activation(e[:, :, :], m[:, :, :], ACT.Exp).then_inc(s["e_out"], 1)
            act.wait_ge(s["e_in"], 2)
            act.activation(r64[:, :, :], r64[:, :, :], ACT.Ln).then_inc(s["e_out"], 1)
            act.wait_ge(s["e_in"], 3)
            act.activation(m[:, :, :], m[:, :, :], ACT.Exp).then_inc(s["e_out"], 1)
            act.wait_ge(s["pp"], 1)
            act.wait_ge(s["mm"], M0 + 2 * NT)

            with act.Fori(0, NT) as t:
                act.wait_ge(s["pre_ready"], t + 1)
                act.activation(z[0][:, :], tile(x, t), ACT.Identity, bias=nmr[:, ds(t, 1)],
                               scale=rstd[:, ds(t, 1)]).then_inc(s["z2"], 1)
                for n in range(NS):
                    act.activation(dg[0][:, n, :], ident[:, :], ACT.Copy, scale=pp[:, ds(t, 1), 0, n])\
                        .then_inc(s["dp"], 1)
                act.activation(tile(z_all, t), tile(x, t), ACT.Identity, bias=nmr[:, ds(t, 1)],
                               scale=rstd[:, ds(t, 1)])
                act.wait_ge(s["pre_ready"], PR0 + t + 1)
                act.wait_ge(s["y_ready"], t + 1)
                act.activation(preT[:, :, :], ppre[:, 0:C].rearrange("p (k n) -> p k n", n=P), ACT.Copy)\
                    .then_inc(s["preT"], 1)
                act.wait_ge(s["y_ready"], YR0 + t + 1)
                act.activation(tile(y_all, t), py[:, 0:C], ACT.Copy).then_inc(s["y"], 1)

            act.wait_ge(s["h_res"], 1)
            with act.Fori(0, NT // 2) as j:
                for par in range(2):
                    t = j * 2 + par
                    act.wait_ge(s["mix"], t + 1)
                    for i in range(HALF):
                        for n in range(NS):
                            act.activation(dg[par][:, i * (NS + 1) + n, :], ident[:, :], ACT.Copy,
                                           scale=m[:, ds(t, 1), i * NS + n]).then_inc(s["dm"], 1)
                        act.activation(dg[par][:, i * (NS + 1) + NS, :], ident[:, :], ACT.Copy,
                                       scale=pp[:, ds(t, 1), 1, i]).then_inc(s["dm"], 1)

        @block.vector
        def _(dve):
            def o_lo(t, par):
                dve.wait_ge(s["o_hi"], t + 1)
                dve.tensor_tensor(o[:, par, 1, :, :], oraw[:, par, :, :], o[:, par, 0, :, :].bitcast(F32),
                                  ALU.subtract).then_inc(s["o_lo"], 1)

            dve.drain().then_inc(s["o_lo"], L0)
            dve.drain().then_inc(s["sum"], S0)
            dve.drain().then_inc(s["mixed"], MX0)
            for k in range(KC):
                dve.wait_ge(s["w_hi"], k + 1)
                dve.tensor_tensor(w[:, 1, k, :], wraw[k], w[:, 0, k, :].bitcast(F32), ALU.subtract)\
                    .then_inc(s["w_lo"], 1)
                if k == 0:
                    o_lo(0, 0)

            def turn(t, j, par, first, last):
                if not last:
                    o_lo(t + 1, 1 - par)
                dve.wait_ge(x_loaded[par], DMA0 + j * 16 + 16)
                for half in range(2):
                    cols = x[:, ds(t, 1), half * BANK:(half + 1) * BANK].rearrange("p o n -> p (o n)")
                    dve.wait_ge(s["mm"], M0 + 2 * t + half + 1)
                    dve.tensor_tensor(cols, cols, pout[:, half, :], ALU.add).then_inc(s["sum"], 1)
                dve.drain()
                for half in range(2):
                    dve.bn_stats(stat[par][:, half, :], x[:, ds(t, 1), half * BANK:(half + 1) * BANK]
                                 .rearrange("p o n -> p (o n)"))
                dve.drain()
                dve.bn_aggr(mvt[par][:, 0:2], stat[par][:, :, :])
                dve.drain()
                dve.tensor_scalar(mvt[par][:, 2:3], mvt[par][:, 1:2], LN_EPS, None, ALU.add).then_inc(s["stats"], 1)
                dve.wait_ge(s["rstd"], t + 1)
                dve.tensor_copy(tile(mv, t), mvt[par][:, :])
                dve.wait_ge(s["zT_ready"], 2 * t + 2)
                dve.tensor_scalar(z[par][:, :], tile(x, t), mvt[par][:, 0:1], mvt[par][:, 3:4],
                                  ALU.subtract, ALU.mult).then_inc(s["z"], 1)

            turns(dve, turn)
            dve.drain()
            dve.tensor_copy(rstd[:, :], mv[:, :, 3])
            dve.tensor_tensor(rms_e[:, :], mv[:, :, 3], mv[:, :, 3], ALU.mult)
            dve.tensor_tensor(nmr[:, :], mv[:, :, 3], mv[:, :, 0], ALU.mult)
            dve.drain()
            dve.tensor_tensor(rms_e[:, :], rms_e[:, :], mv[:, :, 1], ALU.mult)
            dve.tensor_scalar(nmr[:, :], nmr[:, :], -1.0, None, ALU.mult)
            dve.drain()
            dve.tensor_scalar(rms_e[:, :], rms_e[:, :], RMS_EPS, None, ALU.add).then_inc(s["rms_in"], 1)
            dve.wait_ge(s["rms"], 1)
            dve.wait_ge(s["small"], 64)
            dve.wait_ge(s["read"], RD0 + NT)
            dve.tensor_tensor(lg[:, :, :], lg[:, :, :], rms[:, :].unsqueeze(2).broadcast_to([P, NT, NL]), ALU.mult)
            dve.drain()
            dve.tensor_tensor(lg[:, :, :], lg[:, :, :], base[:, :].unsqueeze(1).broadcast_to([P, NT, NL]), ALU.add)
            dve.drain()
            ppl = lg[:, :, NS * NS:].rearrange("p t (a n) -> p t a n", a=2)
            half64 = r64[:, :, 0:2]
            dve.tensor_reduce(half64, ppl, AX.X, ALU.max)
            dve.drain()
            dve.tensor_tensor(pp[:, :, :, :], ppl, spread(half64), ALU.subtract)
            dve.tensor_scalar(m[:, :, :], lg[:, :, 0:NS * NS], 1.0 / TAU, None, ALU.mult)
            dve.drain()
            dve.tensor_reduce(r64[:, :, :], lines(m, "row"), AX.X, ALU.max)
            dve.drain()
            dve.tensor_tensor(lines(m, "row"), lines(m, "row"), spread(r64[:, :, :]), ALU.subtract)\
                .then_inc(s["e_in"], 1)
            dve.wait_ge(s["e_out"], 2)
            dve.tensor_reduce(r64[:, :, :], lines(e, "row"), AX.X, ALU.add)\
                .then_inc(s["e_in"], 1)
            dve.wait_ge(s["gate"], 1)
            dve.tensor_scalar(g[:, 2:3], g[:, 1:2], 1.0, None, ALU.add)
            dve.drain()
            dve.reciprocal(g[:, 2:3], g[:, 2:3])
            dve.drain()
            dve.tensor_scalar(g[:, 3:4], g[:, 2:3], -1.0, 1.0, ALU.mult, ALU.add)
            dve.wait_ge(s["e_out"], 3)
            dve.tensor_tensor(lines(m, "row"), lines(m, "row"), spread(r64[:, :, :]), ALU.subtract)
            dve.drain()
            dve.tensor_reduce(r64[:, :, :], lines(m, "col"), AX.X, ALU.max)
            dve.drain()
            dve.tensor_tensor(lines(m, "col"), lines(m, "col"), spread(r64[:, :, :]), ALU.subtract)\
                .then_inc(s["e_in"], 1)
            dve.tensor_reduce(sums[:, :, :], pp[:, :, :, :], AX.X, ALU.add)
            dve.drain()
            dve.reciprocal(sums[:, :, :], sums[:, :, :])
            dve.drain()
            dve.tensor_tensor(pp[:, :, :, :], pp[:, :, :, :], spread(sums[:, :, :]), ALU.mult).then_inc(s["pp"], 1)
            dve.wait_ge(s["e_out"], 4)

            def normalise(axis):
                dve.drain()
                dve.tensor_reduce(r64[:, :, :], lines(m, axis), AX.X, ALU.add)
                dve.drain()
                dve.reciprocal(r64[:, :, :], r64[:, :, :])
                dve.drain()
                dve.tensor_tensor(lines(m, axis), lines(m, axis), spread(r64[:, :, :]), ALU.mult)

            normalise("col")
            with dve.Fori(0, SINKHORN_ITERS - 1):
                normalise("row")
                normalise("col")
            dve.drain()
            dve.tensor_scalar(m[:, :, :], m[:, :, :], g[:, 2:3], None, ALU.mult)
            dve.drain()
            diag = m[:, :, 0:NS * NS:NS + 1]
            dve.tensor_scalar(diag, diag, g[:, 3:4], None, ALU.add)
            dve.drain().then_inc(s["h_res"], 1)


            def stream(t, n):
                return x[:, ds(t, 1), n * C:(n + 1) * C].rearrange("p o n -> p (o n)")

            dve.wait_ge(s["y"], Y0 + NT)
            with dve.Fori(0, NT // 2) as j:
                for par in range(2):
                    t = j * 2 + par
                    for n in range(NS):
                        zn = z_all[:, ds(t, 1), n * C:(n + 1) * C].rearrange("p o n -> p (o n)")
                        for i in range(HALF, NS):
                            dve.scalar_tensor_tensor(stream(t, i), zn, m[:, ds(t, 1), i * NS + n], stream(t, i),
                                                     ALU.mult, ALU.add)
                        dve.drain()
                    for i in range(HALF, NS):
                        dve.scalar_tensor_tensor(stream(t, i), tile(y_all, t), pp[:, ds(t, 1), 1, i], stream(t, i),
                                                 ALU.mult, ALU.add)
                    dve.wait_ge(s["mix"], MI0 + t + 1)
                    cols = x[:, ds(t, 1), 0:HALF * C].rearrange("p o n -> p (o n)")
                    dve.tensor_tensor(cols, cols, pout[:, par, 0:HALF * C], ALU.add)
                    dve.drain().then_inc(s["mixed"], 1)

        @block.tensor
        def _(pe):
            def project(t, par):
                pe.wait_ge(s["o_lo"], L0 + t + 1)
                for half in range(2):
                    pe.wait_ge(s["sum"], 2 * t + half + 1)
                    passes = [(k, a, b) for k in range(KC) for a, b in ((0, 0), (0, 1), (1, 0))]
                    for i, (k, a, b) in enumerate(passes):
                        mm = pe.matmul(pout[:, half, :], o[:, par, a, k, :], w[:, b, k, half * BANK:(half + 1) * BANK],
                                       start=(i == 0), stop=(i == len(passes) - 1))
                    mm.then_inc(s["mm"], 1)

            def transposes(t, par):
                pe.wait_ge(s["z"], t + 1)
                for half in range(2):
                    pe.wait_ge(s["zT"], 2 * t + half + 1)
                    for k in range(4):
                        tr = pe.transpose(pz[:, half, k * P:(k + 1) * P],
                                          z[par][:, (4 * half + k) * P:(4 * half + k + 1) * P], ident[:, :])
                    tr.then_inc(s["zT_ready"], 1)

            def logits(t, par):
                pe.wait_ge(s["read"], t + 1)
                pe.wait_ge(s["zT"], ZT0 + 2 * t + 2)
                for k in range(KC):
                    mm = pe.matmul(plg[:, par, 0:NL], zT[par][:, k, :], w24_sb[:, k, :],
                                   start=(k == 0), stop=(k == KC - 1))
                mm.then_inc(s["logit"], 1)

            pe.wait_ge(s["const"], 1)
            pe.sem_inc(s["mm"], M0)
            pe.sem_inc(s["zT_ready"], ZR0)
            pe.sem_inc(s["logit"], LG0)
            pe.sem_inc(s["pre_ready"], PR0)
            pe.sem_inc(s["y_ready"], YR0)
            pe.sem_inc(s["mix"], MI0)

            pe.wait_ge(s["o_lo"], L0 + 1)
            for k in range(KC):
                pe.wait_ge(s["w_lo"], k + 1)
                for half in range(2):
                    for i, (a, b) in enumerate(((0, 0), (0, 1), (1, 0))):
                        mm = pe.matmul(pout[:, half, :], o[:, 0, a, k, :], w[:, b, k, half * BANK:(half + 1) * BANK],
                                       start=(k == 0 and i == 0), stop=(k == KC - 1 and i == 2),
                                       skip_group_check=True)
                    if k == KC - 1:
                        mm.then_inc(s["mm"], 1)
            pe.wait_ge(s["small"], 64)

            def turn(t, j, par, first, last):
                if not (first and par == 0):
                    project(t, par)
                if not first or par == 1:
                    transposes(t - 1, 1 - par)
                if not first:
                    logits(t - 2, par)

            turns(pe, turn)
            transposes(NT - 1, 1)
            logits(NT - 2, 0)
            logits(NT - 1, 1)

            with pe.Fori(0, NT) as t:
                pe.wait_ge(s["z2"], t + 1)
                pe.wait_ge(s["preT"], t + 1)
                pe.wait_ge(s["dp"], NS * t + NS)
                for c in range(C // P):
                    for n in range(NS):
                        mm = pe.matmul(ppre[:, c * P:(c + 1) * P], z[0][:, n * C + c * P:n * C + (c + 1) * P],
                                       dg[0][:, n, :], start=(n == 0), stop=(n == NS - 1))
                mm.then_inc(s["pre_ready"], 1)
                pe.wait_ge(s["y"], t + 1)
                pe.wait_ge(s["preT"], PT0 + t + 1)
                for k in range(C // P):
                    mm = pe.matmul(py[:, 0:C], preT[:, k, :], wb[:, k, :], start=(k == 0), stop=(k == C // P - 1))
                mm.then_inc(s["y_ready"], 1)

            pe.wait_ge(s["y"], Y0 + NT)
            with pe.Fori(0, NT // 2) as j:
                for par in range(2):
                    t = j * 2 + par
                    pe.wait_ge(s["mixed"], t + 1)
                    for i in range(HALF):
                        for n in range(NS + 1):
                            if n == 0:
                                pe.wait_ge(s["dm"], (t * HALF + i) * (NS + 1) + NS + 1)
                            rhs = z_all[:, ds(t, 1), n * C:(n + 1) * C].rearrange("p o n -> p (o n)") if n < NS \
                                else tile(y_all, t)
                            mm = pe.matmul(pout[:, par, i * C:(i + 1) * C], dg[par][:, i * (NS + 1) + n, :], rhs,
                                           start=(n == 0), stop=(n == NS), skip_group_check=True)
                    mm.then_inc(s["mix"], 1)


NE, NR = 8, 16
ER = NE * NR
NX = 256
SCALING = 32.0 / 16.0
MAX_THRESHOLD = 0.125
N_RAW = 2 + KC + 1


def expert_ffn(nc, sem, x_in, w_base, w_small, w_b, bias, b_thr, x_out):
    s = {n: sem(f"e_{n}") for n in (
        "const", "small", *(f"w{i}" for i in range(N_RAW)), "w_hi", "w_lo", "x0", "x1", "x2", "x3", "stats", "pow", "z", "zT_ready",
        "zT_hi", "zT_lo", "ex", "g_in", "g_exp", "hw", "hwT_ready", "hw_hi", "hw_lo", "out", "xb", "done",
        "st0", "st1", "st2", "st3")}
    x_loaded, stored = [s[f"x{i}"] for i in range(4)], [s[f"st{i}"] for i in range(4)]
    w_loaded = [s[f"w{i}"] for i in range(N_RAW)]
    ZT0, HL0, DN0, ZR0, DMA0 = 2, 2, 4, 4, 16
    TURNS = NT // 4
    with ExitStack() as ctx:
        def sb(name, shape, dt=F32):
            return ctx.enter_context(nc.sbuf_tensor(f"e_{name}", shape, dt))

        ident = sb("ident", [P, P])
        nhalf = sb("nhalf", [P, 1])
        bias_sb = sb("bias", [P, D])
        thr_b = sb("thr_b", [P, 1])
        wraw = [sb(f"wraw{i}", [P, D]) for i in range(N_RAW)]
        wbase = [sb(f"wbase_{n}", [P, KC, D], F32R) for n in ("hi", "lo")]
        wsmall = [sb(f"wsmall_{n}", [P, KC, NX], F32R) for n in ("hi", "lo")]
        wexp = [sb(f"wexp_{n}", [P, D], F32R) for n in ("hi", "lo")]
        x = [sb(f"x{i}", [P, D]) for i in range(4)]
        z = sb("z", [P, D])
        stat = sb("stat", [P, 2, 6])
        mv = [sb(f"mv{i}", [P, 4]) for i in range(2)]
        zT = [[sb(f"zT_{n}{i}", [P, KC, P], F32R) for n in ("hi", "lo")] for i in range(2)]
        lg = sb("lg", [P, NE + 1])
        nmx = sb("nmx", [P, 1])
        ge = sb("ge", [P, NE + 1])
        sc = sb("sc", [P, 8])
        hw = sb("hw", [P, ER])
        hwT = [sb(f"hwT_{n}", [P, P], F32R) for n in ("hi", "lo")]
        pz = ctx.enter_context(nc.psum_tensor("e_pz", [P, 2, BANK], F32))
        pex = ctx.enter_context(nc.psum_tensor("e_pex", [P, 2, BANK], F32))
        pout = ctx.enter_context(nc.psum_tensor("e_pout", [P, 2, 2, BANK], F32))
        block = ctx.enter_context(nc.Block())

        W = [(w_small[k * P:(k + 4) * P, :].rearrange("(k p) n -> p k n", p=P), 4,
              [w[:, k:k + 4, :] for w in wsmall]) for k in (0, 4)]
        W += [(w_base[k * P:(k + 1) * P, :].rearrange("p (o n) -> p o n", o=1), 1,
               [w[:, k:k + 1, :] for w in wbase]) for k in range(KC)]
        W += [(w_b.rearrange("p (o n) -> p o n", o=1), 1,
               [w[:, :].rearrange("p (o n) -> p o n", o=1) for w in wexp])]

        def turns(eng, turn):
            with eng.Fori(0, TURNS - 1) as j:
                turn(j, False)
            turn(TURNS - 1, True)

        @block.sync
        def _(sp):
            def load_x(t, q, j):
                sp.wait_ge(stored[q], DMA0 + j * 16)
                sp.dma_start(x[q][:, :], x_in[ds(t * P, P), :]).then_inc(x_loaded[q], 16)

            def load_w(i):
                src, n, _ = W[i]
                sp.dma_start(wraw[i][:, :].rearrange("p (k n) -> p k n", k=n), src).then_inc(w_loaded[i], 16)

            for q in range(4):
                sp.sem_inc(stored[q], DMA0)
            for q in range(2):
                load_x(q, q, 0)
            sp.dma_start(bias_sb[:, :], bias).then_inc(s["small"], 16)
            sp.dma_start(thr_b[:, :], b_thr).then_inc(s["small"], 16)
            for i in range(len(W)):
                load_w(i)
            for q in range(2, 4):
                load_x(q, q, 0)

            def turn(j, last):
                for q in range(4):
                    sp.wait_ge(s["done"], DN0 + (j * 4 + q) * 2 + 2)
                    sp.dma_start(x_out[ds((j * 4 + q) * P, P), :], x[q][:, :]).then_inc(stored[q], 16)
                    if not last:
                        load_x((j + 1) * 4 + q, q, j + 1)

            turns(sp, turn)
            for q in range(4):
                sp.wait_ge(stored[q], DMA0 + 16 * TURNS)

        @block.gpsimd
        def _(pool):
            pool.memset(ident[:, :], 0.0)
            pool.memset(nhalf[:, :], -0.5)
            pool.drain()
            pool.affine_select(out=ident[:, :], in_=ident[:, :], compare_op=ALU.not_equal, fill=1.0, base=0,
                               pattern=[[-1, P]], channel_multiplier=1).then_inc(s["const"], 1)
            pool.wait_ge(s["small"], 32)

            def rstd(t, par):
                pool.wait_ge(s["stats"], t + 1)
                pool.tensor_tensor(mv[par][:, 3:4], mv[par][:, 2:3], nhalf[:, :], ALU.pow).then_inc(s["pow"], 1)

            def add_bias(t, q):
                pool.wait_ge(s["z"], t + 1)
                pool.tensor_tensor(x[q][:, :], x[q][:, :], bias_sb[:, :], ALU.add).then_inc(s["xb"], 1)

            rstd(0, 0)
            add_bias(0, 0)
            rstd(1, 1)

            def turn(j, last):
                for q in range(4):
                    if last and q == 3:
                        continue
                    add_bias(j * 4 + q + 1, (q + 1) % 4)
                    if not (last and q == 2):
                        rstd(j * 4 + q + 2, q % 2)

            turns(pool, turn)

        @block.scalar
        def _(act):
            def part_hi(t, par):
                for half in range(2):
                    act.wait_ge(s["zT_ready"], ZR0 + 2 * t + half + 1)
                    act.activation(zT[par][0][:, 4 * half:4 * half + 4, :],
                                   pz[:, half, :].rearrange("p (k n) -> p k n", n=P), ACT.Copy).then_inc(s["zT_hi"], 1)

            part_hi(0, 0)
            for i, (_, n, dst) in enumerate(W):
                act.wait_ge(w_loaded[i], 16)
                act.activation(dst[0], wraw[i][:, :].rearrange("p (k n) -> p k n", k=n), ACT.Copy)\
                    .then_inc(s["w_hi"], 1)

            def experts(t, par):
                act.wait_ge(s["g_in"], t + 1)
                act.activation(ge[:, :], lg[:, :], ACT.Exp).then_inc(s["g_exp"], 1)
                act.wait_ge(s["hwT_ready"], t + 1)
                act.activation(hwT[0][:, :], pex[:, par, NX:NX + P], ACT.Copy).then_inc(s["hw_hi"], 1)

            def turn(j, last):
                for q in range(4):
                    if not (last and q == 3):
                        part_hi(j * 4 + q + 1, (q + 1) % 2)
                    experts(j * 4 + q, q % 2)

            turns(act, turn)

        @block.vector
        def _(dve):
            dve.drain().then_inc(s["zT_lo"], ZT0)
            dve.drain().then_inc(s["hw_lo"], HL0)
            dve.drain().then_inc(s["done"], DN0)

            def statistics(t, par, q, jq):
                dve.wait_ge(x_loaded[q], jq * 16 + 16)
                for half in range(2):
                    dve.bn_stats(stat[:, half, :], x[q][:, half * BANK:(half + 1) * BANK])
                dve.drain()
                dve.bn_aggr(mv[par][:, 0:2], stat[:, :, :])
                dve.drain()
                dve.tensor_scalar(mv[par][:, 2:3], mv[par][:, 1:2], LN_EPS, None, ALU.add).then_inc(s["stats"], 1)

            def normalise(t, par, q):
                dve.wait_ge(s["pow"], t + 1)
                dve.wait_ge(s["zT_ready"], 2 * t + 2 + 2)
                dve.tensor_scalar(z[:, :], x[q][:, :], mv[par][:, 0:1], mv[par][:, 3:4],
                                  ALU.subtract, ALU.mult).then_inc(s["z"], 1)

            def part_lo(t, par):
                for half in range(2):
                    dve.wait_ge(s["zT_hi"], 2 * t + half + 1)
                    cols = slice(4 * half, 4 * half + 4)
                    dve.tensor_tensor(zT[par][1][:, cols, :], pz[:, half, :].rearrange("p (k n) -> p k n", n=P),
                                      zT[par][0][:, cols, :].bitcast(F32), ALU.subtract).then_inc(s["zT_lo"], 1)

            def experts(t, par):
                logits = pex[:, par, ER:ER + NE + 1]
                dve.wait_ge(s["ex"], t + 1)
                dve.tensor_reduce(nmx[:, :], logits[:, 0:NE], AX.X, ALU.max)
                dve.tensor_scalar(lg[:, NE:], logits[:, NE:], thr_b[:, :], -1.0, ALU.add, ALU.mult)
                dve.drain()
                dve.tensor_scalar(lg[:, 0:NE], logits[:, 0:NE], nmx[:, :], None, ALU.subtract).then_inc(s["g_in"], 1)
                dve.wait_ge(s["g_exp"], t + 1)
                dve.tensor_reduce(sc[:, 0:1], ge[:, 0:NE], AX.X, ALU.add)
                dve.tensor_scalar(sc[:, 1:2], ge[:, NE:], 1.0, None, ALU.add)
                dve.drain()
                dve.reciprocal(sc[:, 2:4], sc[:, 0:2])
                dve.drain()
                dve.tensor_scalar(sc[:, 3:4], sc[:, 3:4], MAX_THRESHOLD, None, ALU.mult)
                dve.drain()
                dve.tensor_scalar(ge[:, 0:NE], ge[:, 0:NE], sc[:, 2:3], sc[:, 3:4], ALU.mult, ALU.subtract)
                dve.drain()
                dve.tensor_scalar(ge[:, 0:NE], ge[:, 0:NE], 0.0, None, ALU.max)
                dve.drain()
                dve.tensor_reduce(sc[:, 4:5], ge[:, 0:NE], AX.X, ALU.add)
                dve.drain()
                dve.tensor_scalar(sc[:, 5:6], sc[:, 4:5], 0.0, None, ALU.is_equal)
                dve.drain()
                dve.tensor_tensor(sc[:, 4:5], sc[:, 4:5], sc[:, 5:6], ALU.add)
                dve.drain()
                dve.reciprocal(sc[:, 6:7], sc[:, 4:5])
                dve.drain()
                dve.tensor_scalar(ge[:, 0:NE], ge[:, 0:NE], sc[:, 6:7], SCALING, ALU.mult, ALU.mult)
                dve.drain()
                dve.tensor_tensor(hw[:, :].rearrange("p (e r) -> p e r", r=NR),
                                  pex[:, par, 0:ER].rearrange("p (e r) -> p e r", r=NR),
                                  ge[:, 0:NE].unsqueeze(2).broadcast_to([P, NE, NR]), ALU.mult).then_inc(s["hw"], 1)

            def expert_lo(t, par):
                dve.wait_ge(s["hw_hi"], t + 1)
                dve.tensor_tensor(hwT[1][:, :], pex[:, par, NX:NX + P], hwT[0][:, :].bitcast(F32), ALU.subtract)\
                    .then_inc(s["hw_lo"], 1)

            def finish(t, par, q):
                dve.wait_ge(s["xb"], t + 1)
                for half in range(2):
                    cols = slice(half * BANK, (half + 1) * BANK)
                    dve.wait_ge(s["out"], 2 * t + half + 1)
                    dve.tensor_tensor(x[q][:, cols], x[q][:, cols], pout[:, par, half, :], ALU.add)\
                        .then_inc(s["done"], 1)

            statistics(0, 0, 0, 0)
            normalise(0, 0, 0)
            statistics(1, 1, 1, 0)
            part_lo(0, 0)
            normalise(1, 1, 1)
            for i, (_, n, dst) in enumerate(W):
                dve.wait_ge(s["w_hi"], i + 1)
                dve.tensor_tensor(dst[1], wraw[i][:, :].rearrange("p (k n) -> p k n", k=n), dst[0].bitcast(F32),
                                  ALU.subtract).then_inc(s["w_lo"], 1)
            dve.wait_ge(s["small"], 32)

            def turn(j, last):
                for q in range(4):
                    t, par = j * 4 + q, q % 2
                    if not (last and q >= 2):
                        dve.drain()
                        statistics(t + 2, par, (q + 2) % 4, j + (q + 2) // 4)
                    experts(t, par)
                    if not (last and q == 3):
                        part_lo(t + 1, 1 - par)
                    if not (last and q >= 2):
                        normalise(t + 2, par, (q + 2) % 4)
                    expert_lo(t, par)
                    finish(t, par, q)

            turns(dve, turn)

        @block.tensor
        def _(pe):
            THREE = ((0, 0), (0, 1), (1, 0))

            def transposes(t):
                pe.wait_ge(s["z"], t + 1)
                for half in range(2):
                    pe.wait_ge(s["zT_lo"], 2 * t + half + 1)
                    for k in range(4):
                        tr = pe.transpose(pz[:, half, k * P:(k + 1) * P],
                                          z[:, (4 * half + k) * P:(4 * half + k + 1) * P], ident[:, :])
                    tr.then_inc(s["zT_ready"], 1)

            def products(t, par, last=False, first=False):
                pe.wait_ge(s["zT_lo"], ZT0 + 2 * t + 2)
                pe.wait_ge(s["hw_lo"], t + 1)
                if first:
                    pe.wait_ge(s["w_lo"], 2)
                n = 0
                for k in range(KC):
                    for a, b in THREE:
                        mm = pe.matmul(pex[:, par, 0:NX], zT[par][a][:, k, :], wsmall[b][:, k, :],
                                       start=(n == 0), stop=(n == 3 * KC - 1))
                        n += 1
                mm.then_inc(s["ex"], 1)
                if not last:
                    transposes(t + 1)
                for half in range(2):
                    pe.wait_ge(s["done"], 2 * t + half + 1)
                    n = 0
                    for k in range(KC):
                        if first and half == 0:
                            pe.wait_ge(s["w_lo"], 2 + k + 1)
                        for a, b in THREE:
                            pe.matmul(pout[:, par, half, :], zT[par][a][:, k, :],
                                      wbase[b][:, k, half * BANK:(half + 1) * BANK], start=(n == 0), stop=False)
                            n += 1
                        if half == 1 and k == KC - 3:
                            pe.wait_ge(s["hw"], t + 1)
                            pe.transpose(pex[:, par, NX:NX + P], hw[:, :], ident[:, :]).then_inc(s["hwT_ready"], 1)
                if first:
                    pe.wait_ge(s["w_lo"], N_RAW)
                pe.wait_ge(s["hw_lo"], HL0 + t + 1)
                for half in range(2):
                    for n, (a, b) in enumerate(THREE):
                        mm = pe.matmul(pout[:, par, half, :], hwT[a][:, :], wexp[b][:, half * BANK:(half + 1) * BANK],
                                       start=False, stop=(n == 2))
                    mm.then_inc(s["out"], 1)

            pe.wait_ge(s["const"], 1)
            pe.sem_inc(s["zT_ready"], ZR0)
            transposes(0)

            def turn(j, last, first=False):
                for q in range(4):
                    products(j * 4 + q, q % 2, last and q == 3, first and q == 0)

            turn(0, False, True)
            with pe.Fori(1, TURNS - 1) as j:
                turn(j, False)
            turn(TURNS - 1, True)


@contextmanager
def stage(nc):
    taken = []

    def sem(name):
        taken.append(nc.alloc_semaphore(name))
        return taken[-1]

    yield sem
    nc.clear_and_free_semaphores(taken)
    nc.all_engine_barrier()


def build(nc, x, wqkv, rope, wo, ffn0, ffn1, out):
    def scratch(name, shape):
        return nc.dram_tensor(name, shape, F32, kind="Internal").ap()

    x2, x3 = (scratch(f"x{i}", (T, D)) for i in (2, 3))
    oT_d = [scratch(f"oT_{i}", (NG, P, NT, P)) for i in range(2)]
    swaps = [[i ^ 1 for i in range(HD)], [(i + HD // 2) % HD for i in range(HD)]]
    with stage(nc) as sem:
        attention(nc, sem, 0, x, wqkv[0], *rope[0], swaps[0], oT_d[0])
    with stage(nc) as sem:
        mixing_layer(nc, sem, oT_d[0], wo[0], x, *ffn0, x2)
    with stage(nc) as sem:
        attention(nc, sem, 1, x2, wqkv[1], *rope[1], swaps[1], oT_d[1])
    with stage(nc) as sem:
        output_projection(nc, sem, 1, oT_d[1], wo[1], x2, x3)
    with stage(nc) as sem:
        expert_ffn(nc, sem, x3, *ffn1, out)


def rope_tables(pair_of, sign_of):
    freq = (1.0 / np.float32(THETA) ** (np.arange(0, HD, 2, dtype=np.float32) / np.float32(HD))).astype(np.float32)
    ang = np.outer(freq[pair_of], np.arange(S, dtype=np.float32)).astype(np.float32)
    cos, sin = np.cos(ang).astype(np.float32), (np.sin(ang) * sign_of[:, None]).astype(np.float32)
    return np.tile(cos, (GH, 1)), np.tile(sin, (GH, 1))


def qkv_layout(wk, wv, wq):
    w = np.concatenate([wk, wq[:, :P], wv, wq[:, P:]], axis=1).reshape(KC, P, N_WCHUNK, P).transpose(2, 1, 0, 3)
    return np.concatenate([w, w[:2]], axis=0)


def laid_out(a):
    i = np.arange(HD)
    rope = [rope_tables(i // 2, np.where(i % 2 == 0, -1, 1).astype(np.float32)),
            rope_tables(i % (HD // 2), np.where(i < HD // 2, -1, 1).astype(np.float32))]
    w24 = np.concatenate([a["L0_ffn_W_res"], a["L0_ffn_W_pre"], a["L0_ffn_W_post"]], axis=0)
    base24 = np.concatenate([a["L0_ffn_H_res_base"].reshape(-1), a["L0_ffn_H_pre_base"], a["L0_ffn_H_post_base"]])
    small = np.concatenate([a["L1_ffn_A_w"].reshape(ER, D), a["L1_ffn_W_gate"], a["L1_ffn_W_thr"][None, :],
                            np.zeros((NX - ER - NE - 1, D), np.float32)], axis=0)
    out = {
        "x": a["L0_attn_x"].reshape(T, D),
        "wqkv0": qkv_layout(a["L0_attn_wk"], a["L0_attn_wv"], a["L0_attn_wq"]),
        "wqkv1": qkv_layout(a["L1_attn_Wk"], a["L1_attn_Wv"], a["L1_attn_Wq"]),
        "cos0": rope[0][0], "sin0": rope[0][1], "cos1": rope[1][0], "sin1": rope[1][1],
        "wo0": a["L0_attn_wo"], "wo1": a["L1_attn_Wo"],
        "w24": w24.T.reshape(KC, P, NL).transpose(1, 0, 2),
        "base24": np.broadcast_to(base24, (P, NL)),
        "gate": np.broadcast_to(a["L0_ffn_gate"], (P, 1)),
        "w_branch": a["L0_ffn_W_branch"],
        "w_base": a["L1_ffn_W_base"].T,
        "w_small": small.T,
        "w_b": a["L1_ffn_B_w"].transpose(0, 2, 1).reshape(ER, D),
        "bias": np.broadcast_to(a["L1_ffn_b_base"], (P, D)),
        "b_thr": np.broadcast_to(a["L1_ffn_b_thr"], (P, 1)),
    }
    return {n: np.ascontiguousarray(v) for n, v in out.items()}


def program(nc, t, out):
    build(nc, t["x"], (t["wqkv0"], t["wqkv1"]), ((t["cos0"], t["sin0"]), (t["cos1"], t["sin1"])),
          (t["wo0"], t["wo1"]), (t["w24"], t["base24"], t["gate"], t["w_branch"]),
          (t["w_base"], t["w_small"], t["w_b"], t["bias"], t["b_thr"]), out)


def kernel(**inputs):
    import concourse.bacc as bacc
    from concourse.bass_utils import run_bass_kernel_spmd

    nc = bacc.Bacc("TRN2", target_bir_lowering=False, num_devices=1)
    arrays = laid_out({n: np.asarray(v) for n, v in inputs.items()})
    aps = {n: nc.dram_tensor(f"in_{n}", v.shape, F32, kind="ExternalInput").ap() for n, v in arrays.items()}
    out = nc.dram_tensor("out", (T, D), F32, kind="ExternalOutput").ap()
    program(nc, aps, out)
    r = run_bass_kernel_spmd(nc, [{f"in_{n}": v for n, v in arrays.items()}], core_ids=[0])
    return r.results[0]["out"].reshape(B, S, D)
```
